# Optimizing a Trainium2 kernel written in Bass

```python
import numpy as np
import jax
import jax.numpy as jnp

def _softmax(x, axis=-1):
    return jax.nn.softmax(x, axis=axis)

def _gelu(x):
    return jax.nn.gelu(x, approximate=True)

def _silu(x):
    return jax.nn.silu(x)

def _sigmoid(x):
    return jax.nn.sigmoid(x)

def _layernorm(x, axis=-1, eps=1e-05):
    m = jnp.mean(x, axis=axis, keepdims=True)
    v = jnp.var(x, axis=axis, keepdims=True)
    return (x - m) / jnp.sqrt(v + eps)

def _scatter_add(tgt, idx, src, axis=0):
    return tgt.at[idx].add(src)

def _segment_sum(src, seg, n):
    return jax.ops.segment_sum(src, seg, n)
kernel_name = 'mk_decoder_preln_d2_seqx_r8_7653d4'

def setup_inputs(seed: int=0):
    np.random.seed(seed)
    _w = jnp.asarray

    def _rec_inputs():
        import jax
        import jax.numpy as jnp
        _rk = jax.random.key(seed)
        x = 7.22e-05 + 1 * jax.random.normal(jax.random.fold_in(_rk, 1), (8, 256, 256), jnp.float32)
        _lenS = 256 - jax.random.randint(jax.random.fold_in(_rk, 7), (8,), 0, max(1, 256 // 4) + 1, jnp.int32)
        _lenS2 = 1601 - jax.random.randint(jax.random.fold_in(_rk, 8), (8,), 0, max(1, 1601 // 4) + 1, jnp.int32)
        _ctx_1024P = jax.random.normal(jax.random.fold_in(_rk, 11), (8, 16, 128), jnp.float32)
        _ctx_1024c = jax.random.dirichlet(jax.random.fold_in(_rk, 511), 0.3 * jnp.ones((16,), jnp.float32), (8, 1601))
        _ctx_1024t = jnp.einsum('bsk,bkd->bsd', _ctx_1024c, _ctx_1024P)
        _ctx_1024t = _ctx_1024t * jax.lax.rsqrt(jnp.mean(jnp.square(_ctx_1024t)) + 1e-12) * 0.953939
        ctx_1024 = -0.000673644 + 1.00013 * (_ctx_1024t + 0.3 * jax.random.normal(jax.random.fold_in(_rk, 611), (8, 1601, 128), jnp.float32))
        return (x, ctx_1024)
    x, ctx_1024 = _rec_inputs()

    def _L0_attn_setup():
        import jax, jax.numpy as jnp
        import numpy as np
        EMBED_DIM = 256
        NUM_HEADS = 16
        NUM_KV_HEADS = 4
        HEAD_DIM = EMBED_DIM // NUM_HEADS
        KV_DIM = NUM_KV_HEADS * HEAD_DIM
        B, N = (2, 256)
        RMS_EPS = float(jnp.finfo(jnp.float32).eps)
        L2_EPS = 1e-12

        def _rms_norm(t):
            ms = jnp.mean(t * t, axis=-1, keepdims=True)
            return t * jax.lax.rsqrt(ms + RMS_EPS)
        key = jax.random.key(seed)
        ks = jax.random.split(key, 5)
        s = EMBED_DIM ** (-0.5)
        return {'x': jax.random.normal(ks[0], (B, N, EMBED_DIM), dtype=jnp.float32), 'Wq': jax.random.normal(ks[1], (EMBED_DIM, EMBED_DIM), dtype=jnp.float32) * s, 'Wk': jax.random.normal(ks[2], (KV_DIM, EMBED_DIM), dtype=jnp.float32) * s, 'Wv': jax.random.normal(ks[3], (KV_DIM, EMBED_DIM), dtype=jnp.float32) * s, 'Wo': jax.random.normal(ks[4], (EMBED_DIM, EMBED_DIM), dtype=jnp.float32) * s}
    _L0_attn_all = _L0_attn_setup()
    _L0_attn_in = {k: v for k, v in _L0_attn_all.items() if k in ('Wq', 'Wk', 'Wv', 'Wo')}
    del _L0_attn_all

    def _L0_xattn_setup():
        import jax, jax.numpy as jnp
        import numpy as np
        B, S1, S2, DCA = (2, 256, 128, 16)
        QDIM, KDIM, H = (256, 128, 16)
        HD = QDIM // H
        SCALE = HD ** (-0.5)
        EPS = 1e-06
        DCA_WEIGHT = 1.0

        def _ln(t, w, b):
            m = jnp.mean(t, axis=-1, keepdims=True)
            v = jnp.var(t, axis=-1, keepdims=True)
            return (t - m) * jax.lax.rsqrt(v + EPS) * w + b

        def _attn(q, k, v):
            s = jnp.einsum('bhqd,bhkd->bhqk', q, k) * SCALE
            p = jax.nn.softmax(s, axis=-1)
            return jnp.einsum('bhqk,bhkd->bhqd', p, v)
        key = jax.random.key(seed)
        ks = jax.random.split(key, 8)
        w = lambda k, shape: jax.random.normal(k, shape, jnp.float32) * 0.02
        return {'x': jax.random.normal(ks[0], (B, S1, QDIM), jnp.float32), 'y': jax.random.normal(ks[1], (B, S2 + DCA, KDIM), jnp.float32), 'Wq': w(ks[2], (QDIM, QDIM)), 'bq': jnp.zeros((QDIM,), jnp.float32), 'Wk': w(ks[3], (KDIM, QDIM)), 'bk': jnp.zeros((QDIM,), jnp.float32), 'Wv': w(ks[4], (KDIM, QDIM)), 'bv': jnp.zeros((QDIM,), jnp.float32), 'Wkv_dca': w(ks[5], (KDIM, 2 * QDIM)), 'bkv_dca': jnp.zeros((2 * QDIM,), jnp.float32), 'qn_w': jnp.ones((HD,), jnp.float32), 'qn_b': jnp.zeros((HD,), jnp.float32), 'kn_w': jnp.ones((HD,), jnp.float32), 'kn_b': jnp.zeros((HD,), jnp.float32), 'kn_dca_w': jnp.ones((HD,), jnp.float32), 'kn_dca_b': jnp.zeros((HD,), jnp.float32), 'Wo': w(ks[6], (QDIM, QDIM)), 'bo': jnp.zeros((QDIM,), jnp.float32)}
    _L0_xattn_all = _L0_xattn_setup()
    _L0_xattn_in = {k: v for k, v in _L0_xattn_all.items() if k in ('Wq', 'bq', 'Wk', 'bk', 'Wv', 'bv', 'Wkv_dca', 'bkv_dca', 'qn_w', 'qn_b', 'kn_w', 'kn_b', 'kn_dca_w', 'kn_dca_b', 'Wo', 'bo')}
    del _L0_xattn_all

    def _L0_ffn_setup():
        import jax, jax.numpy as jnp
        import numpy as np
        B, T = (1, 64)
        DIM = 256
        MOE_INTER = 176
        N_EXPERTS = 64
        TOPK = 6
        N_SHARED = 2
        SHARED_INTER = N_SHARED * MOE_INTER
        CAPACITY = 128
        ROUTE_SCALE = 1.0
        key = jax.random.key(seed)
        ks = jax.random.split(key, 8)

        def w(k, shape, fan_in):
            return jax.random.normal(k, shape, jnp.float32) * fan_in ** (-0.5)
        return {'x': jax.random.normal(ks[0], (B, T, DIM), jnp.float32), 'gate_w': w(ks[1], (N_EXPERTS, DIM), DIM), 'w1': w(ks[2], (N_EXPERTS, MOE_INTER, DIM), DIM), 'w2': w(ks[3], (N_EXPERTS, DIM, MOE_INTER), MOE_INTER), 'w3': w(ks[4], (N_EXPERTS, MOE_INTER, DIM), DIM), 'sw1': w(ks[5], (SHARED_INTER, DIM), DIM), 'sw2': w(ks[6], (DIM, SHARED_INTER), SHARED_INTER), 'sw3': w(ks[7], (SHARED_INTER, DIM), DIM)}
    _L0_ffn_all = _L0_ffn_setup()
    _L0_ffn_in = {k: v for k, v in _L0_ffn_all.items() if k in ('gate_w', 'w1', 'w2', 'w3', 'sw1', 'sw2', 'sw3')}
    del _L0_ffn_all

    def _L1_attn_setup():
        import jax, jax.numpy as jnp
        import numpy as np
        EPS_NORM = 1e-06
        EPS_Q = 1e-05

        def rmsnorm(x, g):
            var = jnp.mean(jnp.square(x), axis=-1, keepdims=True)
            return x * jax.lax.rsqrt(var + EPS_NORM) * g

        def act_quant(x):
            scale = 127.0 / jnp.clip(jnp.max(jnp.abs(x), axis=-1, keepdims=True), EPS_Q, None)
            return jnp.clip(jnp.round(x * scale), -128.0, 127.0) / scale

        def weight_quant(w):
            scale = 1.0 / jnp.clip(jnp.mean(jnp.abs(w)), EPS_Q, None)
            return jnp.clip(jnp.round(w * scale), -1.0, 1.0) / scale

        def ste(x, fn):
            return x + jax.lax.stop_gradient(fn(x) - x)

        def bitlinear(x, w, g):
            xn = rmsnorm(x, g)
            xq = ste(xn, act_quant)
            wq = ste(w, weight_quant)
            return jnp.einsum('bsd,od->bso', xq, wq)
        key = jax.random.key(seed)
        k1, k2, k3 = jax.random.split(key, 3)
        B, S, D, I = (4, 512, 256, 704)
        x = jax.random.normal(k1, (B, S, D), dtype=jnp.float32)
        w_gate = jax.random.normal(k2, (2 * I, D), dtype=jnp.float32) * D ** (-0.5)
        g_gate = jnp.ones((D,), dtype=jnp.float32)
        w_down = jax.random.normal(k3, (D, I), dtype=jnp.float32) * I ** (-0.5)
        g_down = jnp.ones((I,), dtype=jnp.float32)
        return {'x': x, 'w_gate': w_gate, 'g_gate': g_gate, 'w_down': w_down, 'g_down': g_down}
    _L1_attn_all = _L1_attn_setup()
    _L1_attn_in = {k: v for k, v in _L1_attn_all.items() if k in ('w_gate', 'g_gate', 'w_down', 'g_down')}
    del _L1_attn_all

    def _L1_xattn_setup():
        import jax, jax.numpy as jnp
        import numpy as np
        EPS = 1e-05

        def rmsnorm(x, g, eps=EPS):
            var = jnp.mean(jnp.square(x), axis=-1, keepdims=True)
            return x * jax.lax.rsqrt(var + eps) * g
        key = jax.random.key(seed)
        ks = jax.random.split(key, 8)
        B, Sq, Skv = (2, 512, 64)
        dim, cdim, H, D = (256, 128, 16, 128)
        inner = H * D
        s = lambda f: 1.0 / np.sqrt(f)
        return {'hidden_states': jax.random.normal(ks[0], (B, Sq, dim), jnp.float32), 'encoder_hidden_states': jax.random.normal(ks[1], (B, Skv, cdim), jnp.float32), 'Wq': jax.random.normal(ks[2], (dim, inner), jnp.float32) * s(dim), 'Wk': jax.random.normal(ks[3], (cdim, inner), jnp.float32) * s(cdim), 'Wv': jax.random.normal(ks[4], (cdim, inner), jnp.float32) * s(cdim), 'Wo': jax.random.normal(ks[5], (inner, dim), jnp.float32) * s(inner), 'gq': jnp.ones((D,), jnp.float32), 'gk': jnp.ones((D,), jnp.float32)}
    _L1_xattn_all = _L1_xattn_setup()
    _L1_xattn_in = {k: v for k, v in _L1_xattn_all.items() if k in ('Wq', 'Wk', 'Wv', 'Wo', 'gq', 'gk')}
    del _L1_xattn_all

    def _L1_ffn_setup():
        import jax, jax.numpy as jnp
        import numpy as np
        TOP_K = 2
        key = jax.random.key(seed)
        ks = jax.random.split(key, 7)
        B, S, H = (2, 256, 256)
        E, A, NS = (8, 64, 2048)
        x = jax.random.normal(ks[0], (B, S, H), jnp.float32)
        gate_w = jax.random.normal(ks[1], (E, H), jnp.float32) * 0.01
        W = jax.random.normal(ks[2], (H, H), jnp.float32) * 0.02
        atoms = jax.random.normal(ks[3], (A, NS), jnp.float32) * 0.02
        expert_atom_weights = jax.random.normal(ks[4], (E, A), jnp.float32) * 0.1
        importance = jax.random.normal(ks[5], (E, NS), jnp.float32) * 0.1
        mask_idx = jax.random.randint(ks[6], (NS,), 0, H * H, jnp.int32)
        return dict(x=x, gate_w=gate_w, W=W, atoms=atoms, expert_atom_weights=expert_atom_weights, importance=importance, mask_idx=mask_idx)
    _L1_ffn_all = _L1_ffn_setup()
    _L1_ffn_in = {k: v for k, v in _L1_ffn_all.items() if k in ('gate_w', 'W', 'atoms', 'expert_atom_weights', 'importance', 'mask_idx')}
    del _L1_ffn_all
    return {'x': x, 'ctx_1024': ctx_1024, 'L0_attn_Wq': _L0_attn_in['Wq'], 'L0_attn_Wk': _L0_attn_in['Wk'], 'L0_attn_Wv': _L0_attn_in['Wv'], 'L0_attn_Wo': _L0_attn_in['Wo'], 'L0_xattn_Wq': _L0_xattn_in['Wq'], 'L0_xattn_bq': _L0_xattn_in['bq'], 'L0_xattn_Wk': _L0_xattn_in['Wk'], 'L0_xattn_bk': _L0_xattn_in['bk'], 'L0_xattn_Wv': _L0_xattn_in['Wv'], 'L0_xattn_bv': _L0_xattn_in['bv'], 'L0_xattn_Wkv_dca': _L0_xattn_in['Wkv_dca'], 'L0_xattn_bkv_dca': _L0_xattn_in['bkv_dca'], 'L0_xattn_qn_w': _L0_xattn_in['qn_w'], 'L0_xattn_qn_b': _L0_xattn_in['qn_b'], 'L0_xattn_kn_w': _L0_xattn_in['kn_w'], 'L0_xattn_kn_b': _L0_xattn_in['kn_b'], 'L0_xattn_kn_dca_w': _L0_xattn_in['kn_dca_w'], 'L0_xattn_kn_dca_b': _L0_xattn_in['kn_dca_b'], 'L0_xattn_Wo': _L0_xattn_in['Wo'], 'L0_xattn_bo': _L0_xattn_in['bo'], 'L0_ffn_gate_w': _L0_ffn_in['gate_w'], 'L0_ffn_w1': _L0_ffn_in['w1'], 'L0_ffn_w2': _L0_ffn_in['w2'], 'L0_ffn_w3': _L0_ffn_in['w3'], 'L0_ffn_sw1': _L0_ffn_in['sw1'], 'L0_ffn_sw2': _L0_ffn_in['sw2'], 'L0_ffn_sw3': _L0_ffn_in['sw3'], 'L1_attn_w_gate': _L1_attn_in['w_gate'], 'L1_attn_g_gate': _L1_attn_in['g_gate'], 'L1_attn_w_down': _L1_attn_in['w_down'], 'L1_attn_g_down': _L1_attn_in['g_down'], 'L1_xattn_Wq': _L1_xattn_in['Wq'], 'L1_xattn_Wk': _L1_xattn_in['Wk'], 'L1_xattn_Wv': _L1_xattn_in['Wv'], 'L1_xattn_Wo': _L1_xattn_in['Wo'], 'L1_xattn_gq': _L1_xattn_in['gq'], 'L1_xattn_gk': _L1_xattn_in['gk'], 'L1_ffn_gate_w': _L1_ffn_in['gate_w'], 'L1_ffn_W': _L1_ffn_in['W'], 'L1_ffn_atoms': _L1_ffn_in['atoms'], 'L1_ffn_expert_atom_weights': _L1_ffn_in['expert_atom_weights'], 'L1_ffn_importance': _L1_ffn_in['importance'], 'L1_ffn_mask_idx': _L1_ffn_in['mask_idx']}

def reference(x, ctx_1024, L0_attn_Wq, L0_attn_Wk, L0_attn_Wv, L0_attn_Wo, L0_xattn_Wq, L0_xattn_bq, L0_xattn_Wk, L0_xattn_bk, L0_xattn_Wv, L0_xattn_bv, L0_xattn_Wkv_dca, L0_xattn_bkv_dca, L0_xattn_qn_w, L0_xattn_qn_b, L0_xattn_kn_w, L0_xattn_kn_b, L0_xattn_kn_dca_w, L0_xattn_kn_dca_b, L0_xattn_Wo, L0_xattn_bo, L0_ffn_gate_w, L0_ffn_w1, L0_ffn_w2, L0_ffn_w3, L0_ffn_sw1, L0_ffn_sw2, L0_ffn_sw3, L1_attn_w_gate, L1_attn_g_gate, L1_attn_w_down, L1_attn_g_down, L1_xattn_Wq, L1_xattn_Wk, L1_xattn_Wv, L1_xattn_Wo, L1_xattn_gq, L1_xattn_gk, L1_ffn_gate_w, L1_ffn_W, L1_ffn_atoms, L1_ffn_expert_atom_weights, L1_ffn_importance, L1_ffn_mask_idx):
    import jax
    import jax.numpy as jnp

    def _L0_attn_ref(x, Wq, Wk, Wv, Wo):
        import jax, jax.numpy as jnp
        import numpy as np
        EMBED_DIM = 256
        NUM_HEADS = 16
        NUM_KV_HEADS = 4
        HEAD_DIM = EMBED_DIM // NUM_HEADS
        KV_DIM = NUM_KV_HEADS * HEAD_DIM
        B, N = (2, 256)
        RMS_EPS = float(jnp.finfo(jnp.float32).eps)
        L2_EPS = 1e-12

        def _rms_norm(t):
            ms = jnp.mean(t * t, axis=-1, keepdims=True)
            return t * jax.lax.rsqrt(ms + RMS_EPS)
        Bb, Nn, C = x.shape
        scale = HEAD_DIM ** (-0.5)
        rep = NUM_HEADS // NUM_KV_HEADS
        q = jnp.einsum('bnc,oc->bno', x, Wq).reshape(Bb, Nn, NUM_HEADS, HEAD_DIM).transpose(0, 2, 1, 3)
        k = jnp.einsum('bnc,oc->bno', x, Wk).reshape(Bb, Nn, NUM_KV_HEADS, HEAD_DIM).transpose(0, 2, 1, 3)
        v = jnp.einsum('bnc,oc->bno', x, Wv).reshape(Bb, Nn, NUM_KV_HEADS, HEAD_DIM).transpose(0, 2, 1, 3)
        q = _rms_norm(q)
        k = _rms_norm(k)
        k = jnp.repeat(k, rep, axis=1)
        v = jnp.repeat(v, rep, axis=1)
        attn = jnp.einsum('bhqd,bhkd->bhqk', q, k) * scale
        attn = jax.nn.softmax(attn, axis=-1)
        y = jnp.einsum('bhqk,bhkd->bhqd', attn, v)
        vn = v / jnp.maximum(jnp.linalg.norm(v, axis=-1, keepdims=True), L2_EPS)
        y = y - jnp.sum(y * vn, axis=-1, keepdims=True) * vn
        y = y.transpose(0, 2, 1, 3).reshape(Bb, Nn, C)
        return jnp.einsum('bnc,oc->bno', y, Wo)

    def _L0_xattn_ref(x, y, Wq, bq, Wk, bk, Wv, bv, Wkv_dca, bkv_dca, qn_w, qn_b, kn_w, kn_b, kn_dca_w, kn_dca_b, Wo, bo):
        import jax, jax.numpy as jnp
        import numpy as np
        B, S1, S2, DCA = (2, 256, 128, 16)
        QDIM, KDIM, H = (256, 128, 16)
        HD = QDIM // H
        SCALE = HD ** (-0.5)
        EPS = 1e-06
        DCA_WEIGHT = 1.0

        def _ln(t, w, b):
            m = jnp.mean(t, axis=-1, keepdims=True)
            v = jnp.var(t, axis=-1, keepdims=True)
            return (t - m) * jax.lax.rsqrt(v + EPS) * w + b

        def _attn(q, k, v):
            s = jnp.einsum('bhqd,bhkd->bhqk', q, k) * SCALE
            p = jax.nn.softmax(s, axis=-1)
            return jnp.einsum('bhqk,bhkd->bhqd', p, v)
        b, s1, _ = x.shape
        y_dca = y[:, -DCA:, :]
        y_main = y[:, :-DCA, :]
        kv_dca = (y_dca @ Wkv_dca + bkv_dca).reshape(b, DCA, 2, H, HD)
        k_dca = _ln(kv_dca[:, :, 0], kn_dca_w, kn_dca_b)
        v_dca = kv_dca[:, :, 1]
        s2 = y_main.shape[1]
        q = _ln((x @ Wq + bq).reshape(b, s1, H, HD), qn_w, qn_b)
        kv = jnp.concatenate([y_main @ Wk + bk, y_main @ Wv + bv], axis=-1)
        kv = kv.reshape(b, s2, H, 2 * HD)
        k = _ln(kv[..., :HD], kn_w, kn_b)
        v = kv[..., HD:]
        qT = q.transpose(0, 2, 1, 3)
        ctx = _attn(qT, k.transpose(0, 2, 1, 3), v.transpose(0, 2, 1, 3))
        ctx = ctx.transpose(0, 2, 1, 3).reshape(b, s1, QDIM)
        ctx_dca = _attn(qT, k_dca.transpose(0, 2, 1, 3), v_dca.transpose(0, 2, 1, 3))
        ctx_dca = ctx_dca.transpose(0, 2, 1, 3).reshape(b, s1, QDIM)
        ctx = ctx + DCA_WEIGHT * ctx_dca
        return ctx @ Wo + bo

    def _L0_ffn_ref(x, gate_w, w1, w2, w3, sw1, sw2, sw3):
        import jax, jax.numpy as jnp
        import numpy as np
        B, T = (1, 64)
        DIM = 256
        MOE_INTER = 176
        N_EXPERTS = 64
        TOPK = 6
        N_SHARED = 2
        SHARED_INTER = N_SHARED * MOE_INTER
        CAPACITY = 128
        ROUTE_SCALE = 1.0
        Bb, Tt, D = x.shape
        xf = x.reshape(-1, D)
        N = xf.shape[0]
        logits = xf @ gate_w.T
        scores = jax.nn.softmax(logits, axis=-1)
        gate_vals, idx = jax.lax.top_k(scores, TOPK)
        gate_vals = gate_vals * ROUTE_SCALE
        E = gate_w.shape[0]
        fe = idx.reshape(-1)
        ft = jnp.repeat(jnp.arange(N), TOPK)
        onehot = (fe[:, None] == jnp.arange(E)[None, :]).astype(jnp.int32)
        pos = jnp.take_along_axis(jnp.cumsum(onehot, axis=0) - 1, fe[:, None], axis=1)[:, 0]
        keep = pos < CAPACITY
        buf = jnp.full((E, CAPACITY), N, dtype=jnp.int32)
        buf = buf.at[fe, pos].set(ft.astype(jnp.int32), mode='drop')
        xpad = jnp.concatenate([xf, jnp.zeros((1, D), xf.dtype)], axis=0)
        xe = xpad[buf]
        h = jax.nn.silu(jnp.einsum('ecd,eid->eci', xe, w1)) * jnp.einsum('ecd,eid->eci', xe, w3)
        ye = jnp.einsum('eci,edi->ecd', h, w2)
        pc = jnp.minimum(pos, CAPACITY - 1)
        op = ye[fe, pc] * keep[:, None].astype(ye.dtype)
        routed = (op * gate_vals.reshape(-1)[:, None]).reshape(N, TOPK, D).sum(axis=1)
        z = jax.nn.silu(xf @ sw1.T) * (xf @ sw3.T) @ sw2.T
        return (routed + z).reshape(Bb, Tt, D)

    def _L1_attn_ref(x, w_gate, g_gate, w_down, g_down):
        import jax, jax.numpy as jnp
        import numpy as np
        EPS_NORM = 1e-06
        EPS_Q = 1e-05

        def rmsnorm(x, g):
            var = jnp.mean(jnp.square(x), axis=-1, keepdims=True)
            return x * jax.lax.rsqrt(var + EPS_NORM) * g

        def act_quant(x):
            scale = 127.0 / jnp.clip(jnp.max(jnp.abs(x), axis=-1, keepdims=True), EPS_Q, None)
            return jnp.clip(jnp.round(x * scale), -128.0, 127.0) / scale

        def weight_quant(w):
            scale = 1.0 / jnp.clip(jnp.mean(jnp.abs(w)), EPS_Q, None)
            return jnp.clip(jnp.round(w * scale), -1.0, 1.0) / scale

        def ste(x, fn):
            return x + jax.lax.stop_gradient(fn(x) - x)

        def bitlinear(x, w, g):
            xn = rmsnorm(x, g)
            xq = ste(xn, act_quant)
            wq = ste(w, weight_quant)
            return jnp.einsum('bsd,od->bso', xq, wq)
        y = bitlinear(x, w_gate, g_gate)
        gate, v = jnp.split(y, 2, axis=-1)
        swiglu_out = gate * jax.nn.sigmoid(gate) * v
        z = bitlinear(swiglu_out, w_down, g_down)
        return z

    def _L1_xattn_ref(hidden_states, encoder_hidden_states, Wq, Wk, Wv, Wo, gq, gk):
        import jax, jax.numpy as jnp
        import numpy as np
        EPS = 1e-05

        def rmsnorm(x, g, eps=EPS):
            var = jnp.mean(jnp.square(x), axis=-1, keepdims=True)
            return x * jax.lax.rsqrt(var + eps) * g
        B, Sq, _ = hidden_states.shape
        Skv = encoder_hidden_states.shape[1]
        D = gq.shape[0]
        H = Wq.shape[1] // D
        scale = 1.0 / np.sqrt(D)
        q = (hidden_states @ Wq).reshape(B, Sq, H, D)
        k = (encoder_hidden_states @ Wk).reshape(B, Skv, H, D)
        v = (encoder_hidden_states @ Wv).reshape(B, Skv, H, D)
        q = rmsnorm(q, gq)
        k = rmsnorm(k, gk)
        scores = jnp.einsum('bqhd,bkhd->bhqk', q, k) * scale
        attn = jax.nn.softmax(scores, axis=-1)
        out = jnp.einsum('bhqk,bkhd->bqhd', attn, v)
        out = out.reshape(B, Sq, H * D)
        return out @ Wo

    def _L1_ffn_ref(x, gate_w, W, atoms, expert_atom_weights, importance, mask_idx):
        import jax, jax.numpy as jnp
        import numpy as np
        TOP_K = 2
        B, S, H = x.shape
        xt = x.reshape(-1, H)
        logits = jnp.clip(xt @ gate_w.T, -50.0, 50.0)
        top_w, top_idx = jax.lax.top_k(logits, TOP_K)
        rw = jax.nn.softmax(top_w, axis=-1)
        deltas = jax.nn.softmax(expert_atom_weights, axis=-1) @ atoms
        weighted = deltas * jax.nn.sigmoid(importance)
        rows = mask_idx // H
        cols = mask_idx % H
        vals = jnp.einsum('tk,tks->ts', rw, weighted[top_idx])
        xg = xt[:, cols]
        contrib = jax.ops.segment_sum((xg * vals).T, rows, num_segments=H)
        out = xt @ W.T + contrib.T
        return out.reshape(B, S, H)
    x = x + _L0_attn_ref(_layernorm(x, axis=-1), L0_attn_Wq, L0_attn_Wk, L0_attn_Wv, L0_attn_Wo)
    x = x + _L0_xattn_ref(_layernorm(x, axis=-1), ctx_1024, L0_xattn_Wq, L0_xattn_bq, L0_xattn_Wk, L0_xattn_bk, L0_xattn_Wv, L0_xattn_bv, L0_xattn_Wkv_dca, L0_xattn_bkv_dca, L0_xattn_qn_w, L0_xattn_qn_b, L0_xattn_kn_w, L0_xattn_kn_b, L0_xattn_kn_dca_w, L0_xattn_kn_dca_b, L0_xattn_Wo, L0_xattn_bo)
    x = x + _L0_ffn_ref(_layernorm(x, axis=-1), L0_ffn_gate_w, L0_ffn_w1, L0_ffn_w2, L0_ffn_w3, L0_ffn_sw1, L0_ffn_sw2, L0_ffn_sw3)
    x = x + _L1_attn_ref(_layernorm(x, axis=-1), L1_attn_w_gate, L1_attn_g_gate, L1_attn_w_down, L1_attn_g_down)
    x = x + _L1_xattn_ref(_layernorm(x, axis=-1), ctx_1024, L1_xattn_Wq, L1_xattn_Wk, L1_xattn_Wv, L1_xattn_Wo, L1_xattn_gq, L1_xattn_gk)
    x = x + _L1_ffn_ref(_layernorm(x, axis=-1), L1_ffn_gate_w, L1_ffn_W, L1_ffn_atoms, L1_ffn_expert_atom_weights, L1_ffn_importance, L1_ffn_mask_idx)
    return x

_drawn_inputs = setup_inputs


def setup_inputs(seed=0):
    import zlib

    import numpy as np

    out = dict(_drawn_inputs(seed))
    spreads = {'L0_xattn_bq': (0.0, 0.435),
     'L0_xattn_bk': (0.0, 0.1),
     'L0_xattn_bv': (0.0, 0.1),
     'L0_xattn_bkv_dca': (0.0, 0.1),
     'L0_xattn_qn_w': (1.0, 0.6),
     'L0_xattn_qn_b': (0.0, 0.637),
     'L0_xattn_kn_w': (1.0, 0.6),
     'L0_xattn_kn_b': (0.0, 2.0),
     'L0_xattn_kn_dca_w': (1.0, 0.6),
     'L0_xattn_kn_dca_b': (0.0, 2.0),
     'L0_xattn_bo': (0.0, 0.1),
     'L1_attn_g_gate': (1.0, 0.2),
     'L1_attn_g_down': (1.0, 0.2),
     'L1_xattn_gq': (1.0, 0.6),
     'L1_xattn_gk': (1.0, 0.6)}
    factors = {'L1_ffn_gate_w': 31.783,
     'L1_ffn_atoms': 8.0,
     'L1_ffn_expert_atom_weights': 29.498,
     'L1_ffn_importance': 63.871}
    for name, (base, spread) in spreads.items():
        noise = np.random.default_rng([zlib.crc32(name.encode()), seed]).standard_normal(out[name].shape)
        drawn = base * np.exp(spread * noise) if base else spread * noise
        out[name] = jnp.asarray(drawn.astype(out[name].dtype))
    for name, factor in factors.items():
        out[name] = (out[name] * factor).astype(out[name].dtype)
    return out
```

```python
from contextlib import ExitStack

import numpy as np

import concourse.bass as bass
from concourse import mybir

F32 = mybir.dt.float32
BF16 = mybir.dt.bfloat16
I32 = mybir.dt.int32
U32 = mybir.dt.uint32
ALU = mybir.AluOpType
ACT = mybir.ActivationFunctionType
AX = mybir.AxisListType
ds = bass.ds

P = 128
B = 8
S = 256
D = 256
DC = D // P
TB = S // P
NT = B * TB
LN_EPS = 1e-5


class Scope:

    def __init__(self, nc, stage):
        self.nc, self.stage, self.stack, self.sems = nc, stage, ExitStack(), []

    def __enter__(self):
        self.stack.__enter__()
        return self

    def __exit__(self, *e):
        if self.sems and e[0] is None:
            with self.nc.Block() as block:

                @block.gpsimd
                def _(pool):
                    for sem in self.sems:
                        pool.sem_clear(sem)

        return self.stack.__exit__(*e)

    def sb(self, name, shape, dt=F32):
        return self.stack.enter_context(self.nc.sbuf_tensor(f"{self.stage}_{name}", shape, dt))

    def ps(self, name, shape, dt=F32):
        return self.stack.enter_context(self.nc.psum_tensor(f"{self.stage}_{name}", shape, dt))

    def sem(self, *names):
        got = [self.stack.enter_context(self.nc.semaphore(f"{self.stage}_{n}")) for n in names]
        self.sems += got
        return got if len(got) > 1 else got[0]


class Chain:

    def __init__(self, eng, sem):
        self.eng, self.sem, self.count = eng, sem, 0

    def restart(self):
        self.eng.sem_clear(self.sem)
        self.count = 0

    def link(self, ins):
        self.count += 1
        ins.then_inc(self.sem, 1)
        self.eng.wait_ge(self.sem, self.count)


def bcast(ap, n):
    return ap.unsqueeze(len(ap.shape)).to_broadcast(list(ap.shape) + [n])


def rsqrt(nc, chain, y, v, t):
    yi = y.bitcast(I32)
    chain.link(nc.vector.tensor_scalar(yi, v.bitcast(I32), 1, None, ALU.logical_shift_right))
    chain.link(nc.vector.tensor_scalar(yi, yi, -1.0, float(0x5F3759DF), ALU.mult, ALU.add))
    for _ in range(3):
        chain.link(nc.vector.scalar_tensor_tensor(t, y, -0.5, y, ALU.mult, ALU.mult))
        chain.link(nc.vector.tensor_tensor(t, t, v, ALU.mult))
        last = nc.vector.scalar_tensor_tensor(y, t, 1.5, y, ALU.add, ALU.mult)
        chain.link(last)


def constants(nc, k):
    with Scope(nc, "const") as s:
        zeroed, done, half = s.sem("zeroed", "done", "half")
        with nc.Block() as block:

            @block.gpsimd
            def _(pool):
                nc.gpsimd.memset(k.ident[:, :], 0.0).then_inc(zeroed, 1)
                pool.wait_ge(zeroed, 1)
                nc.gpsimd.affine_select(out=k.ident[:, :], in_=k.ident[:, :], compare_op=ALU.not_equal, fill=1.0,
                                        base=0, pattern=[[-1, P]], channel_multiplier=1).then_inc(done, 1)
                nc.gpsimd.memset(k.ones[:, :], 1.0).then_inc(half, 1)
                nc.gpsimd.memset(k.x[:, NT:NT + TB, :], 0.0).then_inc(half, 1)
                nc.gpsimd.memset(k.minus_half[:, :], -0.5).then_inc(half, 1)

            @block.vector
            def _(dve):
                dve.wait_ge(done, 1)
                nc.vector.tensor_copy(k.ident_bf[:, :], k.ident[:, :]).then_inc(half, 1)
                dve.wait_ge(half, 4)


def load_x(nc, k, x):
    with Scope(nc, "in") as s:
        landed = s.sem("landed")
        with nc.Block() as block:

            @block.sync
            def _(sp):
                for b in range(0, B, 2):
                    sp.dma_start(k.x[:, b * TB:(b + 2) * TB, :],
                                 x[b:b + 2].rearrange("b (t p) d -> p (b t) d", p=P)).then_inc(landed, 16)
                sp.wait_ge(landed, 16 * B // 2)


def store_x(nc, k, out):
    with Scope(nc, "out") as s:
        landed = s.sem("landed")
        with nc.Block() as block:

            @block.sync
            def _(sp):
                for b in range(0, B, 2):
                    sp.dma_start(out[b:b + 2].rearrange("b (t p) d -> p (b t) d", p=P),
                                 k.x[:, b * TB:(b + 2) * TB, :]).then_inc(landed, 16)
                sp.wait_ge(landed, 16 * B // 2)


def self_attention(nc, k, wqkvT, woT):
    H, KV, HD = 16, 4, 16
    R = H // KV
    PAD = 32
    NQKV = (H + 2 * KV) * HD
    NG = H + 2 * KV
    RMS_EPS = 1.1920928955078125e-07
    UNITS = H

    with Scope(nc, "sa") as s:
        wqkv, wo = s.sb("wqkv", [P, DC, NQKV]), s.sb("wo", [P, DC, D])
        stats, mv, ve, rstd = s.sb("stats", [P, TB, 6]), s.sb("mv", [P, TB, 2]), s.sb("ve", [P, TB]), s.sb("rstd", [P, TB])
        xn, xnT = s.sb("xn", [P, TB, D]), s.sb("xnT", [P, DC, S])
        qkv, sq = s.sb("qkv", [P, TB, NQKV]), s.sb("sq", [P, TB, NQKV])
        ms, rs, room = s.sb("ms", [P, TB * NG]), s.sb("rs", [P, TB * NG]), s.sb("room", [P, TB * NG])
        q_pad, k_pad = s.sb("q_pad", [P, TB, H, PAD]), s.sb("k_pad", [P, TB, KV, PAD])
        v_aug, vn = s.sb("v_aug", [P, TB, KV, PAD]), s.sb("vn", [P, TB, KV, HD])
        qT, kTz = s.sb("qT", [P, R, S]), s.sb("kTz", [P, KV, S])
        probs = s.sb("probs", [P, 2, TB, S])
        yT = s.sb("yT", [P, R, S])
        rden, num, y, dot = s.sb("rden", [P, TB, R, KV]), s.sb("num", [P, TB, H, HD]), s.sb("y", [P, TB, D]), s.sb("dot", [P, TB, H])
        y2T = s.sb("y2T", [P, DC, S])
        pT, pQ = s.ps("pT", [P, 512]), s.ps("pQ", [P, 1024])
        pS, pY = s.ps("pS", [P, 2, TB, S]), s.ps("pY", [P, R, S])

        (weights, prepared, ve_ready, rstd_ready, xn_ready, xnT_psum, xnT_ready, qkv_psum, 
         qk_ready, qkT_psum, qkT_ready, scores_ready, probs_ready, y_psum, yT_ready, y_tok, y_ready, y2_psum,
         y2T_ready, o_psum) = s.sem(
            "weights", "prepared", "ve_ready", "rstd_ready", "xn_ready", "xnT_psum", "xnT_ready", "qkv_psum",
             "qk_ready", "qkT_psum", "qkT_ready", "scores_ready", "probs_ready", "y_psum",
            "yT_ready", "y_tok", "y_ready", "y2_psum", "y2T_ready", "o_psum")
        dve_chain, x_done = s.sem("dve_chain", "x_done")
        with nc.Block() as block:

            @block.sync
            def _(sp):
                sp.dma_start(wqkv[:, :, :], wqkvT.rearrange("(c p) n -> p c n", p=P)).then_inc(weights, 16)
                sp.dma_start(wo[:, :, :], woT.rearrange("(c p) n -> p c n", p=P)).then_inc(weights, 16)

            @block.gpsimd
            def _(pool):
                nc.gpsimd.memset(q_pad[:, :, :, :], 0.0).then_inc(prepared, 1)
                nc.gpsimd.memset(k_pad[:, :, :, :], 0.0).then_inc(prepared, 1)
                nc.gpsimd.memset(kTz[:, :, :], 0.0).then_inc(prepared, 1)
                with pool.Fori(0, B) as b:
                    pool.wait_ge(ve_ready, b + 1)
                    nc.gpsimd.tensor_tensor(rstd[:, :], ve[:, :], k.minus_half[:, 0:TB], ALU.pow).then_inc(rstd_ready, 1)

            @block.vector
            def _(dve):
                chain = Chain(dve, dve_chain)
                chain.link(nc.vector.memset(v_aug[:, :, :, :], 0.0))
                chain.link(nc.vector.memset(v_aug[:, :, :, HD:HD + 1], 1.0))
                dve.wait_ge(prepared, 3)
                with dve.Fori(0, B) as b:
                    chain.restart()
                    for t in range(TB):
                        nc.vector.bn_stats(stats[:, t, :], k.x[:, b * TB + t, :])
                    chain.link(nc.vector.tensor_copy(sq[:, 0, 0:1], k.ones[:, 0:1]))
                    for t in range(TB):
                        chain.link(nc.vector.bn_aggr(mv[:, t, :], stats[:, t, :]))
                    nc.vector.tensor_scalar(ve[:, :], mv[:, :, 1], LN_EPS, None, ALU.add).then_inc(ve_ready, 1)
                    dve.wait_ge(rstd_ready, b + 1)
                    for t in range(TB):
                        nc.vector.tensor_scalar(xn[:, t, :], k.x[:, b * TB + t, :], mv[:, t, 0:1], rstd[:, t:t + 1],
                                                ALU.subtract, ALU.mult).then_inc(xn_ready, 1)
                    dve.wait_ge(qkv_psum, b + 1)
                    chain.link(nc.vector.tensor_copy(qkv[:, :, :], pQ[:, :].rearrange("p (t n) -> p t n", t=TB)[:, :, 0:NQKV]))
                    chain.link(nc.vector.tensor_tensor(sq[:, :, :], qkv[:, :, :], qkv[:, :, :], ALU.mult))
                    chain.link(nc.vector.tensor_reduce(ms[:, :], sq[:, :, :].rearrange("p t (g d) -> p (t g) d", d=HD), AX.X, ALU.add))
                    mst = ms[:, :].rearrange("p (t g) -> p t g", t=TB)
                    rst = rs[:, :].rearrange("p (t g) -> p t g", t=TB)
                    nqk = H + KV
                    chain.link(nc.vector.tensor_scalar(mst[:, :, 0:nqk], mst[:, :, 0:nqk], 1.0 / HD, RMS_EPS, ALU.mult, ALU.add))
                    chain.link(nc.vector.tensor_scalar(mst[:, :, nqk:NG], mst[:, :, nqk:NG], 1e-24, None, ALU.max))
                    rsqrt(nc, chain, rs[:, :], ms[:, :], room[:, :])
                    for t in range(TB):
                        q = qkv[:, t, 0:H * HD].rearrange("p (g r d) -> p r g d", g=KV, r=R)
                        nc.vector.tensor_tensor(q_pad[:, t, :, 0:HD].rearrange("p (r g) d -> p r g d", r=R), q,
                                                bcast(rst[:, t, 0:H].rearrange("p (g r) -> p r g", g=KV), HD), ALU.mult)
                        kk = qkv[:, t, H * HD:(H + KV) * HD].rearrange("p (g d) -> p g d", g=KV)
                        nc.vector.tensor_tensor(k_pad[:, t, :, 0:HD], kk, bcast(rst[:, t, H:nqk], HD), ALU.mult)
                        v = qkv[:, t, (H + KV) * HD:].rearrange("p (g d) -> p g d", g=KV)
                        nc.vector.tensor_tensor(vn[:, t, :, :], v, bcast(rst[:, t, nqk:NG], HD), ALU.mult)
                        last = nc.vector.tensor_copy(v_aug[:, t, :, 0:HD], v)
                    last.then_inc(qk_ready, 1)
                    dve.wait_ge(y_tok, b + 1)
                    pYt = pQ[:, :].rearrange("p (t r g n) -> p t r g n", t=TB, r=R, g=KV)
                    for t in range(TB):
                        chain.link(nc.vector.reciprocal(rden[:, t, :, :], pYt[:, t, :, :, HD]))
                        yt = y[:, t, :].rearrange("p (g r d) -> p r g d", g=KV, r=R)
                        chain.link(nc.vector.tensor_tensor(yt, pYt[:, t, :, :, 0:HD], bcast(rden[:, t, :, :], HD), ALU.mult))
                        yg = y[:, t, :].rearrange("p (g r d) -> p g r d", g=KV, r=R)
                        ng = num[:, t, :, :].rearrange("p (g r) d -> p g r d", g=KV)
                        vb = vn[:, t, :, :].unsqueeze(2).to_broadcast([P, KV, R, HD])
                        chain.link(nc.vector.tensor_tensor(ng, yg, vb, ALU.mult))
                        chain.link(nc.vector.tensor_reduce(dot[:, t, :], num[:, t, :, :], AX.X, ALU.add))
                        chain.link(nc.vector.tensor_tensor(ng, vb, bcast(dot[:, t, :].rearrange("p (g r) -> p g r", g=KV), HD), ALU.mult))
                        nc.vector.tensor_tensor(y[:, t, :], y[:, t, :], num[:, t, :, :].rearrange("p h d -> p (h d)"),
                                                ALU.subtract).then_inc(y_ready, 1)
                    dve.wait_ge(o_psum, b + 1)
                    xb = k.x[:, ds(b * TB, TB), :]
                    chain.link(nc.vector.tensor_tensor(xb, xb, pS[:, 0, :, :], ALU.add))

            @block.scalar
            def _(act):
                with act.Fori(0, B) as b:
                    act.wait_ge(xnT_psum, b + 1)
                    nc.scalar.activation(xnT[:, :, :], pT[:, :].rearrange("p (c n) -> p c n", c=DC), ACT.Copy).then_inc(xnT_ready, 1)
                    act.wait_ge(qkT_psum, b + 1)
                    nc.scalar.activation(qT[:, :, :], pQ[:, :].rearrange("p (r n) -> p r n", r=R), ACT.Copy)
                    for g in range(KV):
                        rows = slice(PAD * g, PAD * g + PAD)
                        last = nc.scalar.activation(kTz[rows, g, :], pT[rows, 0:S], ACT.Copy)
                    last.then_inc(qkT_ready, 1)
                    for u in range(UNITS):
                        act.wait_ge(scores_ready, b * UNITS + u + 1)
                        if u >= 2:
                            act.wait_ge(y_psum, b * UNITS + u - 1)
                        nc.scalar.activation(probs[:, u % 2, :, :], pS[:, u % 2, :, :], ACT.Exp, scale=HD ** -0.5).then_inc(probs_ready, 1)
                    act.wait_ge(y_psum, b * UNITS + UNITS)
                    nc.scalar.activation(yT[:, :, :], pY[:, :, :], ACT.Copy).then_inc(yT_ready, 1)
                    act.wait_ge(y2_psum, b + 1)
                    nc.scalar.activation(y2T[:, :, :], pT[:, :].rearrange("p (c n) -> p c n", c=DC), ACT.Copy).then_inc(y2T_ready, 1)

            @block.tensor
            def _(pe):
                pe.wait_ge(weights, 32)
                with pe.Fori(0, B) as b:
                    for t in range(TB):
                        pe.wait_ge(xn_ready, b * TB + t + 1)
                        for c in range(DC):
                            last = pe.transpose(pT[:, c * S + t * P:c * S + t * P + P], xn[:, t, c * P:c * P + P], k.ident[:, :])
                    last.then_inc(xnT_psum, 1)
                    pe.wait_ge(xnT_ready, b + 1)
                    for t in range(TB):
                        for c in range(DC):
                            last = pe.matmul(pQ[:, 512 * t:512 * t + NQKV], xnT[:, c, t * P:t * P + P], wqkv[:, c, :],
                                             start=c == 0, stop=c == DC - 1)
                    last.then_inc(qkv_psum, 1)
                    pe.wait_ge(qk_ready, b + 1)
                    for t in range(TB):
                        for r in range(R):
                            pe.transpose(pQ[:, r * S + t * P:r * S + t * P + P],
                                         q_pad[:, t, r * KV:(r + 1) * KV, :].rearrange("p g d -> p (g d)"), k.ident[:, :])
                        last = pe.transpose(pT[:, t * P:t * P + P], k_pad[:, t, :, :].rearrange("p g d -> p (g d)"), k.ident[:, :])
                    last.then_inc(qkT_psum, 1)
                    pe.wait_ge(qkT_ready, b + 1)

                    def scores(u):
                        r, g = u // KV, u % KV
                        if u >= 2:
                            pe.wait_ge(probs_ready, b * UNITS + u - 1)
                        for kt in range(TB):
                            last = pe.matmul(pS[:, u % 2, kt, :], kTz[:, g, kt * P:kt * P + P], qT[:, r, :], start=True, stop=True)
                        last.then_inc(scores_ready, 1)

                    def values(u):
                        r, g = u // KV, u % KV
                        pe.wait_ge(probs_ready, b * UNITS + u + 1)
                        for kt in range(TB):
                            last = pe.matmul(pY[PAD * g:PAD * g + PAD, r, :], v_aug[:, kt, g, :], probs[:, u % 2, kt, :],
                                             start=kt == 0, stop=kt == TB - 1, tile_position=(0, PAD * g))
                        last.then_inc(y_psum, 1)

                    scores(0)
                    for u in range(1, UNITS):
                        scores(u)
                        values(u - 1)
                    values(UNITS - 1)
                    pe.wait_ge(yT_ready, b + 1)
                    for t in range(TB):
                        for r in range(R):
                            last = pe.transpose(pQ[:, (t * R + r) * P:(t * R + r + 1) * P], yT[:, r, t * P:t * P + P], k.ident[:, :])
                    last.then_inc(y_tok, 1)
                    for t in range(TB):
                        pe.wait_ge(y_ready, b * TB + t + 1)
                        for c in range(DC):
                            last = pe.transpose(pT[:, c * S + t * P:c * S + t * P + P], y[:, t, c * P:c * P + P], k.ident[:, :])
                    last.then_inc(y2_psum, 1)
                    pe.wait_ge(y2T_ready, b + 1)
                    for t in range(TB):
                        for c in range(DC):
                            last = pe.matmul(pS[:, 0, t, :], y2T[:, c, t * P:t * P + P], wo[:, c, :], start=c == 0, stop=c == DC - 1)
                    last.then_inc(o_psum, 1)


def cross_attention_0(nc, k, ctxT, wqd, bqd, wkvd, bkvd, wdcad, bdcad, qnwd, qnbd, knwd, knbd, dwd, dbd, wod, bod):
    H, HD = 16, 16
    SK = ctxT.shape[2]
    DCA = 16
    MAIN = SK - DCA
    CH = 4
    NCH = MAIN // (CH * P)
    KT = NCH * CH + 1
    LAST = MAIN - (KT - 1) * P
    DROW = 64
    NK = KT * P
    ROWS = 6 * HD
    KR = ROWS + 2
    EPS = 1e-6
    SCALE = HD ** -0.5
    G = 4
    NGR = H // G
    PAD = 32
    UNITS = KT * 2
    HALF = 1024
    FILLS = G * TB
    assert LAST <= DROW and DROW + DCA <= P

    with Scope(nc, "xa") as s:
        wq, wo = s.sb("wq", [P, DC, D]), s.sb("wo", [P, DC, D])
        bq, bo = s.sb("bq", [P, D]), s.sb("bo", [P, D])
        wkv, wdca = s.sb("wkv", [P, 2 * D]), s.sb("wdca", [P, 2 * D])
        bkv, btail = s.sb("bkv", [P, 2 * D]), s.sb("btail", [P, 2 * D])
        qnw, qnb, knw, knb = s.sb("qnw", [P, HD]), s.sb("qnb", [P, HD]), s.sb("knw", [P, HD]), s.sb("knb", [P, HD])
        tnw, tnb = s.sb("tnw", [P, HD]), s.sb("tnb", [P, HD])
        stats, mv, ve, rstd = s.sb("stats", [P, TB, 6]), s.sb("mv", [P, TB, 2]), s.sb("ve", [P, TB]), s.sb("rstd", [P, TB])
        xn, xnT = s.sb("xn", [P, TB, D]), s.sb("xnT", [P, DC, S])
        q = s.sb("q", [P, TB, H, HD])
        q3 = s.sb("q3", [P, TB, H, 3, HD], BF16)
        qst = s.sb("qst", [P, TB, H, KR], BF16)
        qT0 = s.sb("qT0", [ROWS, H, S], BF16)
        qTs = s.sb("qTs", [KR, 2, G, S], BF16)
        eT, eTt = s.sb("eT", [P, 2, CH * P]), s.sb("eTt", [P, P])
        kk, sq = s.sb("kk", [P, CH, H, HD]), s.sb("sq", [P, CH, H, HD])
        hm, hv, hr = s.sb("hm", [P, CH * H]), s.sb("hv", [P, CH * H]), s.sb("hr", [P, CH * H])
        k1 = s.sb("k1", [P, CH, H, HD], BF16)
        kst = [s.sb("kst0", [P, CH, H, KR], BF16), s.sb("kst1", [P, CH, H, KR], BF16)]
        kst_tail = s.sb("kst_tail", [P, 1, H, KR], BF16)
        live, live_main, live_dca = s.sb("live", [P, 1]), s.sb("live_main", [P, 1]), s.sb("live_dca", [P, 1])
        kT = s.sb("kT", [KR, H, NK], BF16)
        va = s.sb("va", [P, KT + 1, H, PAD])
        mpart = s.sb("mpart", [P, 2, 2])
        probs = s.sb("probs", [P, 3, 2 * S])
        ysb, rden, y1, y2 = s.sb("ysb", [P, 2 * S]), s.sb("rden", [P, 2 * TB * G]), s.sb("y1", [P, TB, G, HD]), s.sb("y2", [P, TB, G, HD])
        y, yT = s.sb("y", [P, TB, H, HD]), s.sb("yT", [P, DC, S])
        pM, pS = s.ps("pM", [P, 4, 512]), s.ps("pS", [P, 2, 512])
        pY, pT = s.ps("pY", [P, 512]), s.ps("pT", [P, 512])

        (weights, prepared, tail_landed, ve_ready, rstd_ready, xn_ready, xnT_psum, xnT_ready, q_psum,
         qst_ready, q0_psum, q0_ready, kv_psum, 
         kk_ready, kv_taken, squared, k1_ready, k1_copied, k2_copied, centred, x_added, kst_ready, kt_psum, kt_copied, max_a, max_b, max_a_free, max_b_free, shift_ready,
         qs_psum, qs_ready, scores_ready, probs_ready, pv_done, y_copied, y_tok, y_free, y_all, yT_psum, yT_ready,
         o_psum, dve_chain, pool_chain, act_chain) = s.sem(
            "weights", "prepared", "tail_landed", "ve_ready", "rstd_ready", "xn_ready", "xnT_psum",
            "xnT_ready", "q_psum", "qst_ready", "q0_psum", "q0_ready", "kv_psum", "kk_ready", "kv_taken", "squared", "k1_ready", "k1_copied", "k2_copied", "centred", "x_added", "kst_ready", "kt_psum", "kt_copied",
            "max_a", "max_b", "max_a_free", "max_b_free", "shift_ready", "qs_psum", "qs_ready", "scores_ready",
            "probs_ready", "pv_done", "y_copied", "y_tok", "y_free", "y_all", "yT_psum", "yT_ready", "o_psum",
            "dve_chain", "pool_chain", "act_chain")
        ctx_landed = s.sem("ctx_landed0", "ctx_landed1")
        NC1 = NCH + 1
        SMALL = 15
        pTb = pT[:, :].bitcast(BF16)
        pMb = [pM[:, 2 + i, :].bitcast(BF16) for i in range(2)]
        XT_AT = 10
        pSb = [pS[:, i, :].bitcast(BF16) for i in range(2)]

        with nc.Block() as block:

            @block.sync
            def _(sp):
                def rows(dst, src, lo=0, hi=P):
                    sp.dma_start(dst[lo:hi, :], src.rearrange("(a n) -> a n", a=1).to_broadcast([hi - lo, src.shape[0]])
                                 ).then_inc(weights, 16)
                sp.dma_start(wq[:, :, :], wqd.rearrange("(c p) n -> p c n", p=P)).then_inc(weights, 16)
                sp.dma_start(wo[:, :, :], wod.rearrange("(c p) n -> p c n", p=P)).then_inc(weights, 16)
                sp.dma_start(wkv[:, :], wkvd).then_inc(weights, 16)
                sp.dma_start(wdca[:, :], wdcad).then_inc(weights, 16)
                rows(bq, bqd)
                rows(bo, bod)
                rows(bkv, bkvd)
                rows(qnw, qnwd)
                rows(qnb, qnbd)
                rows(knw, knwd)
                rows(knb, knbd)
                for dst, main, dca in ((btail, bkvd, bdcad), (tnw, knwd, dwd), (tnb, knbd, dbd)):
                    rows(dst, main, 0, DROW)
                    rows(dst, dca, DROW, P)
                sp.wait_ge(prepared, 2)
                with sp.Fori(0, B) as b:
                    for i in range(NCH):
                        before = i - 2 + NC1 if i >= 2 else NCH - 1 - (NCH - 1 - i) % 2
                        sp.wait_ge(kv_psum, b * NC1 + before + 1)
                        sp.dma_start(eT[:, i % 2, :], ctxT[b, :, i * CH * P:(i + 1) * CH * P]).then_inc(ctx_landed[i % 2], 16)
                    sp.wait_ge(kv_psum, b * NC1 + NC1)
                    sp.dma_start(eTt[:, 0:LAST], ctxT[b, :, MAIN - LAST:MAIN]).then_inc(tail_landed, 16)
                    sp.dma_start(eTt[:, DROW:DROW + DCA], ctxT[b, :, MAIN:SK]).then_inc(tail_landed, 16)

            @block.gpsimd
            def _(pool):
                chain = Chain(pool, pool_chain)
                nc.gpsimd.memset(eTt[:, :], 0.0).then_inc(prepared, 1)
                chain.link(nc.gpsimd.memset(live_main[:, :], 1.0))
                chain.link(nc.gpsimd.affine_select(out=live_main[:, :], in_=live_main[:, :], compare_op=ALU.is_gt,
                                                   fill=0.0, base=LAST, pattern=[[0, 1]], channel_multiplier=-1))
                chain.link(nc.gpsimd.memset(live_dca[:, :], 1.0))
                chain.link(nc.gpsimd.affine_select(out=live_dca[:, :], in_=live_dca[:, :], compare_op=ALU.is_ge,
                                                   fill=0.0, base=-DROW, pattern=[[0, 1]], channel_multiplier=1))
                chain.link(nc.gpsimd.affine_select(out=live_dca[:, :], in_=live_dca[:, :], compare_op=ALU.is_gt,
                                                   fill=0.0, base=DROW + DCA, pattern=[[0, 1]], channel_multiplier=-1))
                nc.gpsimd.tensor_tensor(live[:, :], live_main[:, :], live_dca[:, :], ALU.add).then_inc(prepared, 1)

                with pool.Fori(0, B + 1) as b:
                    pool.wait_ge(ve_ready, b + 1)
                    nc.gpsimd.tensor_tensor(rstd[:, :], ve[:, :], k.minus_half[:, 0:TB], ALU.pow).then_inc(rstd_ready, 1)

            @block.vector
            def _(dve):
                chain = Chain(dve, dve_chain)
                dve.wait_ge(weights, 16 * 17)
                dve.wait_ge(prepared, 2)
                chain.link(nc.vector.memset(va[:, :, :, :], 0.0))
                chain.link(nc.vector.memset(va[:, :, :, HD:HD + 1], 1.0))
                for slot, mask in ((KT - 1, live_main), (KT, live_dca)):
                    chain.link(nc.vector.tensor_scalar(va[:, slot, :, HD:HD + 1], va[:, slot, :, HD:HD + 1], mask[:, 0:1], None, ALU.mult))
                for z in kst:
                    chain.link(nc.vector.memset(z[:, :, :, :], 0.0))
                    chain.link(nc.vector.memset(z[:, :, :, ROWS:ROWS + 1], 1.0))
                for w in (wq[:, :, :].rearrange("p c (h d) -> p (c h) d", d=HD), bq[:, :].rearrange("p (h d) -> p h d", d=HD),
                          *(z[:, :].rearrange("p (h m d) -> p h m d", m=2, d=HD)[:, :, 0, :] for z in (wkv, wdca, bkv, btail))):
                    n = w.shape[1]
                    chain.link(nc.vector.tensor_reduce(hm[:, 0:n], w, AX.X, ALU.add))
                    chain.link(nc.vector.tensor_scalar(hm[:, 0:n], hm[:, 0:n], 1.0 / HD, None, ALU.mult))
                    chain.link(nc.vector.tensor_tensor(w, w, bcast(hm[:, 0:n], HD), ALU.subtract))
                dve.sem_inc(centred, 1)
                chain.link(nc.vector.memset(kst_tail[:, :, :, :], 0.0))
                chain.link(nc.vector.tensor_scalar(kst_tail[:, 0, :, ROWS:ROWS + 1], va[:, KT - 1, :, HD:HD + 1], 1.0, None, ALU.mult))
                chain.link(nc.vector.tensor_scalar(kst_tail[:, 0, :, ROWS + 1:KR], va[:, KT, :, HD:HD + 1], 1.0, None, ALU.mult))

                def head_norm(z, n, w, bias, squares):
                    zf = z.rearrange("p n h d -> p (n h) d")
                    m, v, r = hm[:, 0:n * H], hv[:, 0:n * H], hr[:, 0:n * H]
                    sqf = sq[:, 0:n, :, :].rearrange("p n h d -> p (n h) d")
                    squares(sqf, zf)
                    chain.link(nc.vector.tensor_reduce(v, sqf, AX.X, ALU.add))
                    chain.link(nc.vector.tensor_scalar(v, v, 1.0 / HD, EPS, ALU.mult, ALU.add))
                    rsqrt(nc, chain, r, v, m)
                    chain.link(nc.vector.tensor_tensor(zf, zf, bcast(r, HD), ALU.mult))
                    wb = w[:, :].unsqueeze(1).to_broadcast([P, n * H, HD])
                    bb = bias[:, :].unsqueeze(1).to_broadcast([P, n * H, HD])
                    chain.link(nc.vector.tensor_tensor(zf, zf, wb, ALU.mult))
                    chain.link(nc.vector.tensor_tensor(zf, zf, bb, ALU.add))

                def queries(b):
                    for t in range(TB):
                        chain.link(nc.vector.bn_stats(stats[:, t, :], k.x[:, b * TB + t, :]))
                    for t in range(TB):
                        chain.link(nc.vector.bn_aggr(mv[:, t, :], stats[:, t, :]))
                    nc.vector.tensor_scalar(ve[:, :], mv[:, :, 1], LN_EPS, None, ALU.add).then_inc(ve_ready, 1)
                    dve.wait_ge(rstd_ready, b + 1)
                    for t in range(TB):
                        nc.vector.tensor_scalar(xn[:, t, :], k.x[:, b * TB + t, :], mv[:, t, 0:1], rstd[:, t:t + 1],
                                                ALU.subtract, ALU.mult).then_inc(xn_ready, 1)
                    dve.wait_ge(q_psum, b + 1)
                    qf = q[:, :, :, :].rearrange("p t h d -> p t (h d)")
                    chain.link(nc.vector.tensor_tensor(qf, pM[:, 0, :].rearrange("p (t n) -> p t n", t=TB),
                                                       bq[:, :].unsqueeze(1).to_broadcast([P, TB, D]), ALU.add))
                    head_norm(q[:, :, :, :], TB, qnw, qnb, lambda o, z: chain.link(nc.vector.tensor_tensor(o, z, z, ALU.mult)))
                    rest = sq[:, 0:TB, :, :]
                    for t in range(TB):
                        chain.link(nc.vector.tensor_copy(q3[:, t, :, 0, :], q[:, t, :, :]))
                        chain.link(nc.vector.tensor_tensor(rest[:, t], q[:, t, :, :], q3[:, t, :, 0, :], ALU.subtract))
                        chain.link(nc.vector.tensor_copy(q3[:, t, :, 1, :], rest[:, t]))
                        chain.link(nc.vector.tensor_tensor(q3[:, t, :, 2, :], rest[:, t], q3[:, t, :, 1, :], ALU.subtract))
                        for at, n in ((0, 3), (3, 2), (5, 1)):
                            last = nc.vector.tensor_copy(qst[:, t, :, at * HD:(at + n) * HD],
                                                         q3[:, t, :, 0:n, :].rearrange("p h n d -> p h (n d)"))
                    last.then_inc(qst_ready, 1)

                def query_columns(b):
                    for g in range(NGR):
                        dve.wait_ge(q0_psum, b * NGR + g + 1)
                        nc.vector.tensor_copy(qT0[:, g * G:(g + 1) * G, :],
                                              pMb[g % 2][0:ROWS, :].rearrange("p (i n) -> p i n", i=G)).then_inc(q0_ready, 1)

                chain.restart()
                queries(0)
                query_columns(0)
                with dve.Fori(0, B) as b:
                    chain.restart()

                    def keys(i):
                        c = b * NC1 + i
                        n, out, bias, w, nb = (CH, kst[i % 2], bkv, knw, knb) if i < NCH else (1, kst_tail, btail, tnw, tnb)
                        slot = i * CH
                        dve.wait_ge(kv_psum, c + NC1 + 1)
                        kvb = bias[:, :].rearrange("p (h m d) -> p h m d", h=H, m=2)
                        for m, dst in ((0, kk[:, 0:n, :, :]), (1, va[:, slot:slot + n, :, 0:HD])):
                            for j in range(n):
                                kvp = pM[:, j, :].rearrange("p (h m d) -> p h m d", h=H, m=2)
                                last = nc.vector.tensor_tensor(dst[:, j], kvp[:, :, m, :], kvb[:, :, m, :], ALU.add)
                            last.then_inc((kk_ready, kv_taken)[m], 1)
                        z, rest = kk[:, 0:n, :, :], sq[:, 0:n, :, :]
                        head_norm(z, n, w, nb, lambda o, z_: dve.wait_ge(squared, c + 1))
                        if i == NCH:
                            chain.link(nc.vector.tensor_scalar(z, z, live[:, 0:1], None, ALU.mult))
                            dve.wait_ge(kv_taken, c + 1)
                            tail_v = va[:, KT - 1, :, 0:HD]
                            chain.link(nc.vector.tensor_scalar(va[:, KT, :, 0:HD], tail_v, live_dca[:, 0:1], None, ALU.mult))
                            chain.link(nc.vector.tensor_scalar(tail_v, tail_v, live_main[:, 0:1], None, ALU.mult))
                        fl = lambda a: a.rearrange("p n h d -> p (n h) d")
                        part = lambda m: out[:, 0:n, :, m * HD:(m + 1) * HD].rearrange("p n h d -> p (n h) d")
                        if i:
                            dve.wait_ge(k1_copied, 2 * c)
                        if i == 2:
                            dve.wait_ge(kt_psum, (c - 1) * (H // 2))
                        nc.vector.tensor_copy(fl(k1[:, 0:n, :, :]), fl(z)).then_inc(k1_ready, 1)
                        dve.wait_ge(k1_ready, 2 * c + 1)
                        chain.link(nc.vector.tensor_tensor(fl(rest), fl(z), fl(k1[:, 0:n, :, :]), ALU.subtract))
                        nc.vector.tensor_copy(part(3), fl(rest)).then_inc(k1_ready, 1)
                        dve.wait_ge(k1_ready, 2 * c + 2)
                        chain.link(nc.vector.tensor_tensor(part(5), fl(rest), part(3), ALU.subtract))
                        chain.link(nc.vector.tensor_copy(part(2), fl(k1[:, 0:n, :, :])))
                        dve.sem_inc(kst_ready, 1)

                    chain.restart()
                    for i in range(NC1):
                        keys(i)

                    def maxima(g):
                        for i in range(G):
                            for t in range(TB):
                                f = (b * NGR + g) * FILLS + i * TB + t
                                h = g * G + i
                                dve.wait_ge(max_a, f + 1)
                                nc.vector.tensor_reduce(mpart[:, t, 0:1], pM[:, 0:2, :].rearrange("p a n -> p (a n)"), AX.X, ALU.max).then_inc(max_a_free, 1)
                                dve.wait_ge(max_b, f + 1)
                                rest = pM[:, 2:4, :].rearrange("p a n -> p (a n)")
                                nc.vector.tensor_reduce(mpart[:, t, 1:2], rest[:, 0:MAIN - HALF], AX.X, ALU.max)
                                nc.vector.tensor_reduce(qst[:, t, h, ROWS + 1:KR], rest[:, (KT - 1) * P - HALF + DROW:(KT - 1) * P - HALF + DROW + DCA],
                                                        AX.X, ALU.max, negate=True).then_inc(max_b_free, 1)
                                dve.wait_ge(max_b_free, f + 2)
                                dve.wait_ge(max_a_free, f + 2)
                                last = nc.vector.tensor_reduce(qst[:, t, h, ROWS:ROWS + 1], mpart[:, t, :], AX.X, ALU.max, negate=True)
                        last.then_inc(shift_ready, 1)

                    def combine(g):
                        dve.wait_ge(y_tok, b * NGR + g + 1)
                        chain.link(nc.vector.reciprocal(rden[:, :], pT[:, :].rearrange("p (a n) -> p a n", n=PAD)[:, :, HD]))
                        yt = pT[:, :].rearrange("p (m t i n) -> p m t i n", m=2, t=TB, i=G)
                        rd = rden[:, :].rearrange("p (m t i) -> p m t i", m=2, t=TB)
                        chain.link(nc.vector.tensor_tensor(y1[:, :, :, :], yt[:, 0, :, :, 0:HD], bcast(rd[:, 0], HD), ALU.mult))
                        nc.vector.tensor_tensor(y2[:, :, :, :], yt[:, 1, :, :, 0:HD], bcast(rd[:, 1], HD), ALU.mult).then_inc(y_free, 1)
                        dve.wait_ge(y_free, b * NGR + g + 1)
                        chain.link(nc.vector.tensor_tensor(y[:, :, g * G:(g + 1) * G, :], y1[:, :, :, :], y2[:, :, :, :], ALU.add))

                    chain.restart()
                    maxima(0)
                    for g in range(NGR):
                        if g >= 1:
                            combine(g - 1)
                        if g + 1 < NGR:
                            maxima(g + 1)
                    queries(b + 1)
                    combine(NGR - 1)
                    nc.vector.tensor_copy(mpart[:, 0, 0:1], mpart[:, 0, 1:2]).then_inc(y_all, 1)
                    query_columns(b + 1)
                    xb = k.x[:, ds(b * TB, TB), :]
                    dve.wait_ge(o_psum, b + 1)
                    chain.link(nc.vector.tensor_tensor(xb, xb, pM[:, 0, :].rearrange("p (t n) -> p t n", t=TB), ALU.add))
                    dve.sem_inc(x_added, 1)
                    chain.link(nc.vector.tensor_tensor(xb, xb, bo[:, :].unsqueeze(1).to_broadcast([P, TB, D]), ALU.add))

            @block.scalar
            def _(act):
                act.sem_inc(kt_copied, 2)
                act.sem_inc(kv_psum, NC1)
                act.sem_inc(max_a_free, 1)
                act.sem_inc(max_b_free, 1)
                act.sem_inc(y_copied, 1)
                act.wait_ge(weights, 16 * 17)
                act.sem_inc(x_added, 1)

                def x_columns(b):
                    act.wait_ge(xnT_psum, b + 1)
                    nc.scalar.activation(xnT[:, :, :], pM[:, 1, :].rearrange("p (c n) -> p c n", c=DC), ACT.Copy).then_inc(xnT_ready, 1)

                x_columns(0)
                with act.Fori(0, B) as b:

                    def key_columns(i):
                        n = CH if i < NCH else 1
                        for hp in range(H // 2):
                            act.wait_ge(kt_psum, (b * NC1 + i) * (H // 2) + hp + 1)
                            src = pSb[hp % 2][0:KR, :].rearrange("p (i n) -> p i n", i=2)[:, :, 0:n * P]
                            nc.scalar.activation(kT[:, 2 * hp:2 * hp + 2, i * CH * P:(i * CH + n) * P], src, ACT.Copy).then_inc(kt_copied, 1)

                    for i in range(NC1):
                        c = b * NC1 + i
                        n, out = (CH, kst[i % 2]) if i < NCH else (1, kst_tail)
                        part = lambda m: out[:, 0:n, :, m * HD:(m + 1) * HD].rearrange("p n h d -> p (n h) d")
                        act.wait_ge(kk_ready, c + 1)
                        nc.scalar.activation(sq[:, 0:n, :, :], kk[:, 0:n, :, :], ACT.Square).then_inc(squared, 1)
                        if i:
                            key_columns(i - 1)
                        act.wait_ge(k1_ready, 2 * c + 1)
                        for m in range(2):
                            nc.scalar.activation(part(m), k1[:, 0:n, :, :].rearrange("p n h d -> p (n h) d"), ACT.Copy).then_inc(k1_copied, 1)
                        act.wait_ge(k1_ready, 2 * c + 2)
                        nc.scalar.activation(part(4), part(3), ACT.Copy).then_inc(k2_copied, 1)
                    key_columns(NCH)

                    def shifted_queries(g):
                        act.wait_ge(qs_psum, b * NGR + g + 1)
                        if g >= 2:
                            act.wait_ge(scores_ready, (b * NGR + g - 1) * UNITS)
                        nc.scalar.activation(qTs[:, g % 2, :, :], pTb[0:KR, :].rearrange("p (i n) -> p i n", i=G), ACT.Copy).then_inc(qs_ready, 1)

                    shifted_queries(0)
                    for g in range(NGR):
                        for u in range(UNITS):
                            n = b * (NGR * UNITS) + g * UNITS + u
                            act.wait_ge(scores_ready, n + 1)
                            if g * UNITS + u >= 3:
                                act.wait_ge(pv_done, n - 2)
                            nc.scalar.activation(probs[:, (g * UNITS + u) % 3, :], pS[:, u % 2, :], ACT.Exp, scale=SCALE).then_inc(probs_ready, 1)
                            if g == NGR - 1 and u == XT_AT:
                                x_columns(b + 1)
                        if g + 1 < NGR:
                            shifted_queries(g + 1)
                        act.wait_ge(pv_done, (b * NGR + g + 1) * UNITS)
                        nc.scalar.activation(ysb[:, :], pY[:, :], ACT.Copy).then_inc(y_copied, 1)
                    act.wait_ge(yT_psum, b + 1)
                    nc.scalar.activation(yT[:, :, :], pT[:, :].rearrange("p (c n) -> p c n", c=DC), ACT.Copy).then_inc(yT_ready, 1)

            @block.tensor
            def _(pe):
                pe.wait_ge(weights, 16 * 17)
                pe.wait_ge(centred, 1)

                def x_columns(b):
                    for t in range(TB):
                        pe.wait_ge(xn_ready, b * TB + t + 1)
                        for c in range(DC):
                            last = pe.transpose(pM[:, 1, c * S + t * P:c * S + t * P + P], xn[:, t, c * P:c * P + P], k.ident[:, :])
                    last.then_inc(xnT_psum, 1)

                def queries(b):
                    pe.wait_ge(xnT_ready, b + 1)
                    for t in range(TB):
                        for c in range(DC):
                            last = pe.matmul(pM[:, 0, t * D:(t + 1) * D], xnT[:, c, t * P:t * P + P], wq[:, c, :],
                                             start=c == 0, stop=c == DC - 1)
                    last.then_inc(q_psum, 1)

                def query_columns(b):
                    pe.wait_ge(qst_ready, b + 1)
                    for g in range(NGR):
                        if g >= 2:
                            pe.wait_ge(q0_ready, b * NGR + g - 1)
                        for i in range(G):
                            for t in range(TB):
                                last = pe.transpose(pMb[g % 2][0:ROWS, i * S + t * P:i * S + t * P + P],
                                                    qst[:, t, g * G + i, 0:ROWS], k.ident_bf[:, :])
                        last.then_inc(q0_psum, 1)

                x_columns(0)
                queries(0)
                query_columns(0)
                with pe.Fori(0, B) as b:

                    def projected(i):
                        c = b * NC1 + i
                        if i:
                            pe.wait_ge(kk_ready, c)
                            pe.wait_ge(kv_taken, c)
                        if i < NCH:
                            each = (NCH + 1) // 2 if i % 2 == 0 else NCH // 2
                            pe.wait_ge(ctx_landed[i % 2], b * (16 * each) + 16 * (i // 2 + 1))
                            for j in range(CH):
                                last = pe.matmul(pM[:, j, :], eT[:, i % 2, j * P:j * P + P], wkv[:, :], start=True, stop=True)
                        else:
                            pe.wait_ge(tail_landed, b * 32 + 32)
                            pe.matmul(pM[:, 0, :], eTt[:, :], wkv[:, :], start=True, stop=True)
                            last = pe.matmul(pM[DROW:P, 0, :], eTt[:, DROW:P], wdca[:, :], start=True, stop=True, tile_position=(0, DROW))
                        last.then_inc(kv_psum, 1)

                    def transposed(i):
                        c = b * NC1 + i
                        n, src = (CH, kst[i % 2]) if i < NCH else (1, kst_tail)
                        pe.wait_ge(kst_ready, c + 1)
                        pe.wait_ge(k1_copied, 2 * c + 2)
                        pe.wait_ge(k2_copied, c + 1)
                        for hp in range(H // 2):
                            pe.wait_ge(kt_copied, c * (H // 2) + hp + 1)
                            for m in range(2):
                                for j in range(n):
                                    last = pe.transpose(pSb[hp % 2][0:KR, m * CH * P + j * P:m * CH * P + j * P + P],
                                                        src[:, j, 2 * hp + m, :], k.ident_bf[:, :])
                            last.then_inc(kt_psum, 1)

                    pe.wait_ge(q0_ready, b * NGR + NGR)
                    pe.wait_ge(x_added, b + 1)
                    projected(0)
                    for i in range(NC1):
                        if i < NCH:
                            projected(i + 1)
                        transposed(i)
                    pe.wait_ge(kt_copied, (b + 1) * (NC1 * H // 2) + 2)

                    def fill(g, f, half):
                        h, t = g * G + f // TB, f % TB
                        n = (b * NGR + g) * FILLS + f
                        pe.wait_ge((max_a_free, max_b_free)[half], n + 1)
                        for a in range(2):
                            lo = half * HALF + a * 512
                            w = min(512, (KT - 1) * P + DROW + DCA - lo)
                            last = pe.matmul(pM[:, 2 * half + a, 0:w], qT0[:, h, t * P:t * P + P], kT[0:ROWS, h, lo:lo + w],
                                             start=True, stop=True)
                        last.then_inc((max_a, max_b)[half], 1)

                    def shifted_queries(g):
                        pe.wait_ge(shift_ready, b * NGR + g + 1)
                        for i in range(G):
                            for t in range(TB):
                                last = pe.transpose(pTb[0:KR, i * S + t * P:i * S + t * P + P], qst[:, t, g * G + i, :], k.ident_bf[:, :])
                        last.then_inc(qs_psum, 1)

                    def scores(g, u):
                        n = b * (NGR * UNITS) + g * UNITS + u
                        kt = u // 2
                        if g * UNITS + u >= 2:
                            pe.wait_ge(probs_ready, n - 1)
                        for a in range(2):
                            i = 2 * (u % 2) + a
                            last = pe.matmul(pS[:, u % 2, a * S:(a + 1) * S], kT[:, g * G + i, kt * P:kt * P + P], qTs[:, g % 2, i, :],
                                             start=True, stop=True)
                        last.then_inc(scores_ready, 1)

                    def values(g, u):
                        n = b * (NGR * UNITS) + g * UNITS + u
                        kt = u // 2
                        pe.wait_ge(probs_ready, n + 1)
                        for a in range(2):
                            i = 2 * (u % 2) + a
                            pr = probs[:, (g * UNITS + u) % 3, a * S:(a + 1) * S]
                            last = pe.matmul(pY[PAD * i:PAD * i + PAD, 0:S], va[:, kt, g * G + i, :], pr,
                                             start=kt == 0, stop=kt == KT - 1, tile_position=(0, PAD * i))
                            if kt == KT - 1:
                                last = pe.matmul(pY[PAD * i:PAD * i + PAD, S:2 * S], va[:, KT, g * G + i, :], pr,
                                                 start=True, stop=True, tile_position=(0, PAD * i))
                        last.then_inc(pv_done, 1)

                    def outputs(g):
                        pe.wait_ge(y_copied, b * NGR + g + 2)
                        if g >= 1:
                            pe.wait_ge(y_free, b * NGR + g)
                        for m in range(2 * TB):
                            last = pe.transpose(pT[:, m * P:m * P + P], ysb[:, m * P:m * P + P], k.ident[:, :])
                        last.then_inc(y_tok, 1)

                    for f in range(FILLS):
                        fill(0, f, 0)
                        fill(0, f, 1)
                    shifted_queries(0)
                    for g in range(NGR):
                        pe.wait_ge(qs_ready, b * NGR + g + 1)
                        scores(g, 0)
                        pe.wait_ge(y_copied, b * NGR + g + 1)
                        for u in range(1, UNITS):
                            scores(g, u)
                            if g + 1 < NGR and u < 3 * FILLS + 1 and u % 3:
                                fill(g + 1, u // 3, u % 3 - 1)
                            values(g, u - 1)
                            if u == 2 and g >= 1:
                                outputs(g - 1)
                            if g == NGR - 1 and u == XT_AT:
                                x_columns(b + 1)
                            if g == NGR - 1 and u == XT_AT + 4:
                                queries(b + 1)
                        values(g, UNITS - 1)
                        if g + 1 < NGR:
                            if g >= 1:
                                pe.wait_ge(y_free, b * NGR + g)
                            shifted_queries(g + 1)
                    outputs(NGR - 1)
                    query_columns(b + 1)
                    pe.wait_ge(y_all, b + 1)
                    yf = y[:, :, :, :].rearrange("p t h d -> p t (h d)")
                    for t in range(TB):
                        for c2 in range(DC):
                            last = pe.transpose(pT[:, c2 * S + t * P:c2 * S + t * P + P], yf[:, t, c2 * P:c2 * P + P], k.ident[:, :])
                    last.then_inc(yT_psum, 1)
                    pe.wait_ge(yT_ready, b + 1)
                    for t in range(TB):
                        for c2 in range(DC):
                            last = pe.matmul(pM[:, 0, t * D:(t + 1) * D], yT[:, c2, t * P:t * P + P], wo[:, c2, :],
                                             start=c2 == 0, stop=c2 == DC - 1)
                    last.then_inc(o_psum, 1)


def experts(nc, k, gateT, w13T, w2T, s13T, s2T):
    E, TOP, CAP = 64, 6, 128
    I = w2T.shape[1]
    IB = I - P
    SI = s2T.shape[0]
    SC = (SI + P - 1) // P
    ROWS = E * CAP
    SPARE = P * TB * TOP
    ZR = 16
    xe = nc.dram_tensor("expert_in", (ROWS + SPARE, D), F32).ap()
    ye = nc.dram_tensor("expert_out", (ROWS + SPARE, D), F32).ap()

    with Scope(nc, "moe") as keep:
        slots, gates = keep.sb("slots", [P, NT, TOP], U32), keep.sb("gates", [P, NT, TOP])

        with Scope(nc, "route") as s:
            gate, s13, s2 = s.sb("gate", [P, DC, E]), s.sb("s13", [P, DC, 2 * SI]), s.sb("s2", [P, SC, D])
            zeros = s.sb("zeros", [P, ZR * D])
            stats, mv, ve, rstd = s.sb("stats", [P, TB, 6]), s.sb("mv", [P, TB, 2]), s.sb("ve", [P, TB]), s.sb("rstd", [P, TB])
            xn, xnT = s.sb("xn", [P, TB, D]), s.sb("xnT", [P, DC, S])
            before = s.sb("before", [P, P])
            before_bf, ones_bf = s.sb("before_bf", [P, P], BF16), s.sb("ones_bf", [P, P], BF16)
            col_i, col = s.sb("col_i", [P, E], I32), s.sb("col", [P, E])
            spare_i, spare = s.sb("spare_i", [P, TB, TOP], I32), s.sb("spare", [P, TB, TOP])
            lg, top, topi, topf = s.sb("lg", [P, TB, E]), s.sb("top", [P, TB, 8]), s.sb("topi", [P, TB, 8], U32), s.sb("topf", [P, TB, 8])
            hot, picked = s.sb("hot", [P, TB, TOP, E]), s.sb("picked", [P, TB, TOP, E])
            chosen, chosen_bf, seen = s.sb("chosen", [P, TB, E]), s.sb("chosen_bf", [P, TB, E], BF16), s.sb("seen", [P, E], BF16)
            neg, ex, ex8, den, rden = s.sb("neg", [P, TB]), s.sb("ex", [P, TB, E]), s.sb("ex8", [P, TB, 8]), s.sb("den", [P, TB]), s.sb("rden", [P, TB])
            pos, kept, slotf = s.sb("pos", [P, TB, TOP]), s.sb("kept", [P, TB, TOP]), s.sb("slotf", [P, TB, TOP])
            slot_s = s.sb("slot_s", [P, TB, TOP], U32)
            act1, hT = s.sb("act1", [P, SC, S]), s.sb("hT", [P, SC, S])
            pT, pL, pH, pZ = s.ps("pT", [P, 512]), s.ps("pL", [P, 512]), s.ps("pH", [P, SC, 2, S]), s.ps("pZ", [P, 512])
            (weights, prepared, cleared, ve_ready, rstd_ready, xn_ready, xnT_psum, xnT_ready, l_psum, lg_ready, exp_ready,
             chosen_ready, pos_psum, slots_ready, scattered, h_psum, silu_ready, h_ready, z_psum, dve_chain, pool_chain) = s.sem(
                "weights", "prepared", "cleared", "ve_ready", "rstd_ready", "xn_ready", "xnT_psum", "xnT_ready", "l_psum",
                "lg_ready", "exp_ready", "chosen_ready", "pos_psum", "slots_ready", "scattered", "h_psum", "silu_ready",
                "h_ready", "z_psum", "dve_chain", "pool_chain")
            rows_free, issuing = s.sem("rows_free", "issuing")
            hw = [min(P, SI - j * P) for j in range(SC)]
            with nc.Block() as block:

                @block.sync
                def _(sp):
                    sp.dma_start(gate[:, :, :], gateT.rearrange("(c p) n -> p c n", p=P)).then_inc(weights, 16)
                    sp.dma_start(s13[:, :, :], s13T.rearrange("(c p) n -> p c n", p=P)).then_inc(weights, 16)
                    for j in range(SC):
                        sp.dma_start(s2[0:hw[j], j, :], s2T[j * P:j * P + hw[j], :]).then_inc(weights, 16)
                    sp.wait_ge(prepared, 1)
                    for n in range(ROWS // (P * ZR)):
                        sp.dma_start(xe[n * P * ZR:(n + 1) * P * ZR, :].rearrange("(p r) d -> p (r d)", p=P), zeros[:, :]).then_inc(cleared, 16)
                    sp.dma_start(ye[ROWS:ROWS + SPARE, :].rearrange("(p r) d -> p (r d)", p=P), zeros[:, 0:SPARE // P * D]).then_inc(cleared, 16)
                    sp.wait_ge(cleared, 16 * (ROWS // (P * ZR) + 1))

                @block.gpsimd
                def _(pool):
                    chain = Chain(pool, pool_chain)
                    nc.gpsimd.memset(zeros[:, :], 0.0).then_inc(prepared, 1)
                    chain.link(nc.gpsimd.memset(before[:, :], 1.0))
                    nc.gpsimd.affine_select(out=before[:, :], in_=before[:, :], compare_op=ALU.is_gt, fill=0.0, base=0,
                                            pattern=[[1, P]], channel_multiplier=-1).then_inc(prepared, 1)
                    nc.gpsimd.iota(col_i[:, :], pattern=[[1, E]], base=0, channel_multiplier=0).then_inc(prepared, 1)
                    nc.gpsimd.iota(spare_i[:, :, :], pattern=[[P, TB * TOP]], base=ROWS, channel_multiplier=1).then_inc(prepared, 1)
                    pool.wait_ge(cleared, 16 * (ROWS // (P * ZR) + 1))
                    pool.sem_inc(rows_free, 1)
                    with pool.Fori(0, B) as b:
                        pool.wait_ge(ve_ready, b + 1)
                        nc.gpsimd.tensor_tensor(rstd[:, :], ve[:, :], k.minus_half[:, 0:TB], ALU.pow).then_inc(rstd_ready, 1)
                        pool.wait_ge(slots_ready, b + 1)
                        pool.sem_inc(issuing, 1)
                        for t in range(TB):
                            for n in range(TOP):
                                pool.indirect_dma_start(out=xe[:, :], out_offset=bass.IndirectOffsetOnAxis(ap=slot_s[:, t, n:n + 1], axis=0),
                                                        in_=xn[:, t, :], in_offset=None).then_inc(scattered, 16)
                        pool.wait_ge(scattered, b * (16 * TB * TOP) + 16 * TB * TOP)
                        pool.sem_inc(rows_free, 1)
                    pool.wait_ge(scattered, 16 * TB * TOP * B)

                @block.vector
                def _(dve):
                    chain = Chain(dve, dve_chain)
                    dve.wait_ge(prepared, 4)
                    chain.link(nc.vector.tensor_copy(before_bf[:, :], before[:, :]))
                    chain.link(nc.vector.tensor_copy(ones_bf[:, :], k.ones[:, :]))
                    chain.link(nc.vector.tensor_copy(col[:, :], col_i[:, :]))
                    chain.link(nc.vector.tensor_copy(spare[:, :, :], spare_i[:, :, :]))
                    chain.link(nc.vector.memset(seen[:, :], 0.0))
                    nc.vector.tensor_copy(neg[:, 0:1], col[:, 0:1]).then_inc(chosen_ready, 1)
                    with dve.Fori(0, B) as b:
                        chain.restart()
                        for t in range(TB):
                            chain.link(nc.vector.bn_stats(stats[:, t, :], k.x[:, b * TB + t, :]))
                        for t in range(TB):
                            chain.link(nc.vector.bn_aggr(mv[:, t, :], stats[:, t, :]))
                        nc.vector.tensor_scalar(ve[:, :], mv[:, :, 1], LN_EPS, None, ALU.add).then_inc(ve_ready, 1)
                        dve.wait_ge(rstd_ready, b + 1)
                        dve.wait_ge(rows_free, b + 1)
                        for t in range(TB):
                            nc.vector.tensor_scalar(xn[:, t, :], k.x[:, b * TB + t, :], mv[:, t, 0:1], rstd[:, t:t + 1],
                                                    ALU.subtract, ALU.mult).then_inc(xn_ready, 1)
                        dve.wait_ge(l_psum, b + 1)
                        chain.link(nc.vector.tensor_copy(lg[:, :, :], pL[:, 0:TB * E].rearrange("p (t e) -> p t e", t=TB)))
                        for t in range(TB):
                            chain.link(nc.vector.max(top[:, t, :], lg[:, t, :]))
                        for t in range(TB):
                            chain.link(nc.vector.max_index(topi[:, t, :], top[:, t, :], lg[:, t, :]))
                        nc.vector.tensor_scalar(neg[:, :], top[:, :, 0], -1.0, None, ALU.mult).then_inc(lg_ready, 1)
                        chain.link(nc.vector.tensor_copy(topf[:, :, :], topi[:, :, :]))
                        for t in range(TB):
                            chain.link(nc.vector.tensor_tensor(hot[:, t, :, :], col[:, :].unsqueeze(1).to_broadcast([P, TOP, E]),
                                                               bcast(topf[:, t, 0:TOP], E), ALU.is_equal))
                            chain.link(nc.vector.tensor_reduce(chosen[:, t, :], hot[:, t, :, :].rearrange("p k e -> p e k"), AX.X, ALU.add))
                        nc.vector.tensor_copy(chosen_bf[:, :, :], chosen[:, :, :]).then_inc(chosen_ready, 1)
                        dve.wait_ge(pos_psum, b + 1)
                        pp = pL[:, 256:256 + TB * E].rearrange("p (t e) -> p t e", t=TB)
                        for t in range(TB):
                            chain.link(nc.vector.tensor_tensor(picked[:, t, :, :], hot[:, t, :, :],
                                                               pp[:, t, :].unsqueeze(1).to_broadcast([P, TOP, E]), ALU.mult))
                            chain.link(nc.vector.tensor_tensor(seen[:, :], seen[:, :], chosen[:, t, :], ALU.add))
                        chain.link(nc.vector.tensor_reduce(pos[:, :, :].rearrange("p t k -> p (t k)"),
                                                           picked[:, :, :, :].rearrange("p t k e -> p (t k) e"), AX.X, ALU.add))
                        chain.link(nc.vector.tensor_scalar(kept[:, :, :], pos[:, :, :], float(CAP), None, ALU.is_lt))
                        for t in range(TB):
                            chain.link(nc.vector.scalar_tensor_tensor(out=slotf[:, t, :], in0=topf[:, t, 0:TOP], scalar=float(CAP), in1=spare[:, t, :], op0=ALU.mult, op1=ALU.subtract))
                        chain.link(nc.vector.tensor_tensor(slotf[:, :, :], slotf[:, :, :], pos[:, :, :], ALU.add))
                        chain.link(nc.vector.tensor_tensor(slotf[:, :, :], slotf[:, :, :], kept[:, :, :], ALU.mult))
                        chain.link(nc.vector.tensor_tensor(slot_s[:, :, :], slotf[:, :, :], spare[:, :, :], ALU.add))
                        nc.vector.tensor_copy(slots[:, ds(b * TB, TB), :], slot_s[:, :, :]).then_inc(slots_ready, 1)
                        dve.wait_ge(exp_ready, b + 1)
                        chain.link(nc.vector.reciprocal(rden[:, :], den[:, :]))
                        chain.link(nc.vector.tensor_tensor(kept[:, :, :], kept[:, :, :], bcast(rden[:, :], TOP), ALU.mult))
                        chain.link(nc.vector.tensor_tensor(gates[:, ds(b * TB, TB), :], kept[:, :, :], ex8[:, :, 0:TOP], ALU.mult))
                        for j in range(SC):
                            dve.wait_ge(silu_ready, b * SC + j + 1)
                            nc.vector.tensor_tensor(hT[0:hw[j], j, :], act1[0:hw[j], j, :], pH[0:hw[j], j, 1, :], ALU.mult).then_inc(h_ready, 1)
                        dve.wait_ge(z_psum, b + 1)
                        xb = k.x[:, ds(b * TB, TB), :]
                        chain.link(nc.vector.tensor_tensor(xb, xb, pZ[:, :].rearrange("p (t n) -> p t n", t=TB), ALU.add))

                @block.scalar
                def _(act):
                    with act.Fori(0, B) as b:
                        act.wait_ge(xnT_psum, b + 1)
                        nc.scalar.activation(xnT[:, :, :], pT[:, :].rearrange("p (c n) -> p c n", c=DC), ACT.Copy).then_inc(xnT_ready, 1)
                        act.wait_ge(lg_ready, b + 1)
                        for t in range(TB):
                            nc.scalar.activation(ex[:, t, :], lg[:, t, :], ACT.Exp, bias=neg[:, t:t + 1], accum_out=den[:, t:t + 1])
                            last = nc.scalar.activation(ex8[:, t, :], top[:, t, :], ACT.Exp, bias=neg[:, t:t + 1])
                        last.then_inc(exp_ready, 1)
                        for j in range(SC):
                            act.wait_ge(h_psum, b * SC + j + 1)
                            nc.scalar.activation(act1[0:hw[j], j, :], pH[0:hw[j], j, 0, :], ACT.Silu).then_inc(silu_ready, 1)

                @block.tensor
                def _(pe):
                    pe.wait_ge(weights, 16 * (2 + SC))
                    with pe.Fori(0, B) as b:
                        for t in range(TB):
                            pe.wait_ge(xn_ready, b * TB + t + 1)
                            for c in range(DC):
                                last = pe.transpose(pT[:, c * S + t * P:c * S + t * P + P], xn[:, t, c * P:c * P + P], k.ident[:, :])
                        last.then_inc(xnT_psum, 1)
                        pe.wait_ge(xnT_ready, b + 1)
                        for t in range(TB):
                            for c in range(DC):
                                last = pe.matmul(pL[:, t * E:(t + 1) * E], xnT[:, c, t * P:t * P + P], gate[:, c, :],
                                                 start=c == 0, stop=c == DC - 1)
                        last.then_inc(l_psum, 1)
                        for j in range(SC):
                            for m in range(2):
                                for c in range(DC):
                                    lo = m * SI + j * P
                                    last = pe.matmul(pH[0:hw[j], j, m, :], s13[:, c, lo:lo + hw[j]], xnT[:, c, :],
                                                     start=c == 0, stop=c == DC - 1)
                            last.then_inc(h_psum, 1)
                        pe.wait_ge(chosen_ready, b + 2)
                        for t in range(TB):
                            o = pL[:, 256 + t * E:256 + (t + 1) * E]
                            pe.matmul(o, before_bf[:, :], chosen_bf[:, t, :], start=True, stop=False)
                            if t == 1:
                                pe.matmul(o, ones_bf[:, :], chosen_bf[:, 0, :], start=False, stop=False)
                            last = pe.matmul(o, ones_bf[:, :], seen[:, :], start=False, stop=True)
                        last.then_inc(pos_psum, 1)
                        for j in range(SC):
                            pe.wait_ge(h_ready, b * SC + j + 1)
                        for t in range(TB):
                            for j in range(SC):
                                last = pe.matmul(pZ[:, t * D:(t + 1) * D], hT[0:hw[j], j, t * P:t * P + P], s2[0:hw[j], j, :],
                                                 start=j == 0, stop=j == SC - 1)
                        last.then_inc(z_psum, 1)

        with Scope(nc, "exp") as s:
            wa, wb, wc = s.sb("wa", [P, 2, DC, 2 * I]), s.sb("wb", [P, 2, D]), s.sb("wc", [IB, 2, D])
            xs, xT = s.sb("xs", [P, 2, D]), s.sb("xT", [P, 2, DC, CAP])
            sa, sbb = s.sb("sa", [P, 2, CAP]), s.sb("sb", [IB, 2, CAP])
            ha, hb = s.sb("ha", [P, 2, CAP]), s.sb("hb", [IB, 2, CAP])
            yo = s.sb("yo", [P, 2, D])
            pT, pH, pO = s.ps("pT", [P, 2, 512]), s.ps("pH", [P, 2, 512]), s.ps("pO", [P, 2, 512])
            xs_landed, wa_landed = s.sem("xs_landed0", "xs_landed1"), s.sem("wa_landed0", "wa_landed1")
            wb_landed, stored = s.sem("wb_landed0", "wb_landed1"), s.sem("stored0", "stored1")
            (xT_psum, xT_ready, h_psum, silu_ready, h_ready, o_psum, yo_ready) = s.sem(
                "xT_psum", "xT_ready", "h_psum", "silu_ready", "h_ready", "o_psum", "yo_ready")
            with nc.Block() as block:

                @block.sync
                def _(sp):
                    def load_x(e, u):
                        sp.dma_start(xs[:, u, :], xe[ds(e * CAP, CAP), :]).then_inc(xs_landed[u], 16)

                    def load_up(e, u):
                        sp.dma_start(wa[:, u, :, :], w13T[e].rearrange("(c p) n -> p c n", p=P)).then_inc(wa_landed[u], 16)

                    def load_down(e, u):
                        sp.dma_start(wb[:, u, :], w2T[e, 0:P, :]).then_inc(wb_landed[u], 16)
                        sp.dma_start(wc[:, u, :], w2T[e, P:I, :]).then_inc(wb_landed[u], 16)

                    def store(e, u):
                        sp.wait_ge(yo_ready, e + 3)
                        sp.dma_start(ye[ds(e * CAP, CAP), :], yo[:, u, :]).then_inc(stored[u], 16)

                    for u in range(2):
                        load_x(u, u)
                        load_up(u, u)
                        load_down(u, u)
                    with sp.Fori(0, E // 2 - 1) as i:
                        for u in range(2):
                            e = 2 * i + u
                            sp.wait_ge(xT_psum, e + 1)
                            load_x(e + 2, u)
                            sp.wait_ge(h_psum, e + 1)
                            load_up(e + 2, u)
                            sp.wait_ge(o_psum, e + 1)
                            load_down(e + 2, u)
                            store(e, u)
                    for u in range(2):
                        store(E - 2 + u, u)
                    for u in range(2):
                        sp.wait_ge(stored[u], 16 * (E // 2))

                @block.tensor
                def _(pe):
                    def turn(i, u):
                        pe.wait_ge(xs_landed[u], i * 16 + 16)
                        for c in range(DC):
                            last = pe.transpose(pT[:, u, c * P:c * P + P], xs[:, u, c * P:c * P + P], k.ident[:, :])
                        last.then_inc(xT_psum, 1)

                    def hidden(i, u):
                        pe.wait_ge(wa_landed[u], i * 16 + 16)
                        pe.wait_ge(xT_ready, 2 * i + u + 1)
                        for m in range(2):
                            for j, w in ((0, P), (1, IB)):
                                for c in range(DC):
                                    lo = m * I + j * P
                                    last = pe.matmul(pH[0:w, u, (2 * m + j) * CAP:(2 * m + j + 1) * CAP], wa[:, u, c, lo:lo + w],
                                                     xT[:, u, c, :], start=c == 0, stop=c == DC - 1)
                        last.then_inc(h_psum, 1)

                    def down(i, u):
                        pe.wait_ge(wb_landed[u], i * 32 + 32)
                        pe.wait_ge(h_ready, 2 * i + u + 1)
                        pe.wait_ge(yo_ready, 2 * i + u + 1)
                        pe.matmul(pO[:, u, 0:D], ha[:, u, :], wb[:, u, :], start=True, stop=False)
                        pe.matmul(pO[:, u, 0:D], hb[:, u, :], wc[:, u, :], start=False, stop=True).then_inc(o_psum, 1)

                    turn(0, 0)
                    turn(0, 1)
                    hidden(0, 0)
                    with pe.Fori(0, E // 2 - 1) as i:
                        for u in range(2):
                            turn(i + 1, u)
                            hidden(i + u, 1 - u)
                            down(i, u)
                    hidden(E // 2 - 1, 1)
                    down(E // 2 - 1, 0)
                    down(E // 2 - 1, 1)

                @block.scalar
                def _(act):
                    act.sem_inc(yo_ready, 2)
                    with act.Fori(0, E // 2) as i:
                        for u in range(2):
                            e = 2 * i + u
                            act.wait_ge(xT_psum, e + 1)
                            nc.scalar.activation(xT[:, u, :, :], pT[:, u, 0:D].rearrange("p (c n) -> p c n", c=DC), ACT.Copy).then_inc(xT_ready, 1)
                            act.wait_ge(h_psum, e + 1)
                            nc.scalar.activation(sa[:, u, :], pH[:, u, 0:CAP], ACT.Silu)
                            nc.scalar.activation(sbb[:, u, :], pH[0:IB, u, CAP:2 * CAP], ACT.Silu).then_inc(silu_ready, 1)

                @block.vector
                def _(dve):
                    def product(e, u):
                        dve.wait_ge(silu_ready, e + 1)
                        nc.vector.tensor_tensor(ha[:, u, :], sa[:, u, :], pH[:, u, 2 * CAP:3 * CAP], ALU.mult)
                        nc.vector.tensor_tensor(hb[:, u, :], sbb[:, u, :], pH[0:IB, u, 3 * CAP:4 * CAP], ALU.mult).then_inc(h_ready, 1)

                    def evacuate(i, u, first=False):
                        dve.wait_ge(o_psum, 2 * i + u + 1)
                        if not first:
                            dve.wait_ge(stored[u], i * 16)
                        nc.vector.tensor_copy(yo[:, u, :], pO[:, u, 0:D]).then_inc(yo_ready, 1)

                    product(0, 0)
                    for u in range(2):
                        product(u + 1, 1 - u)
                        evacuate(0, u, first=True)
                    with dve.Fori(1, E // 2 - 1) as i:
                        for u in range(2):
                            product(2 * i + u + 1, 1 - u)
                            evacuate(i, u)
                    product(E - 1, 1)
                    for u in range(2):
                        evacuate(E // 2 - 1, u)

        with Scope(nc, "comb") as s:
            rows, sl, gt = s.sb("rows", [P, TB, TOP, D]), s.sb("sl", [P, TB, TOP], U32), s.sb("gt", [P, TB, TOP])
            sl_ready, issuing, dve_chain = s.sem("sl_ready", "issuing", "dve_chain")
            gathered = s.sem("gathered0", "gathered1")
            with nc.Block() as block:

                @block.gpsimd
                def _(pool):
                    with pool.Fori(0, B) as b:
                        for t in range(TB):
                            pool.wait_ge(sl_ready, b * TB + t + 1)
                            pool.sem_inc(issuing, 1)
                            for n in range(TOP):
                                pool.indirect_dma_start(out=rows[:, t, n, :], out_offset=None, in_=ye[:, :],
                                                        in_offset=bass.IndirectOffsetOnAxis(ap=sl[:, t, n:n + 1], axis=0)).then_inc(gathered[t], 16)

                @block.vector
                def _(dve):
                    chain = Chain(dve, dve_chain)

                    def ask(i, t):
                        chain.link(nc.vector.tensor_copy(gt[:, t, :], gates[:, i, :]))
                        nc.vector.tensor_copy(sl[:, t, :], slots[:, i, :]).then_inc(sl_ready, 1)

                    def add(b, t):
                        dve.wait_ge(gathered[t], b * (16 * TOP) + 16 * TOP)
                        i = b * TB + t
                        for n in range(TOP):
                            xt = k.x[:, i, :]
                            chain.link(nc.vector.scalar_tensor_tensor(out=xt, in0=rows[:, t, n, :], scalar=gt[:, t, n:n + 1],
                                                                      in1=xt, op0=ALU.mult, op1=ALU.add))

                    for t in range(TB):
                        ask(t, t)
                    with dve.Fori(0, B - 1) as b:
                        chain.restart()
                        for t in range(TB):
                            add(b, t)
                            ask(b * TB + TB + t, t)
                    chain.restart()
                    for t in range(TB):
                        add(B - 1, t)


def bit_mlp(nc, k, wgT, gg, wdT, gd):
    I = wdT.shape[0]
    N = 2 * I
    IC = (I + P - 1) // P
    iw = [min(P, I - j * P) for j in range(IC)]
    MAGIC = 12582912.0
    RMS_EPS, Q_EPS = 1e-6, 1e-5

    with Scope(nc, "bit") as s:
        wg, wd = s.sb("wg", [P, DC, N]), s.sb("wd", [P, IC, D])
        wgq, wdq = s.sb("wgq", [P, DC, N], BF16), s.sb("wdq", [P, IC, D], BF16)
        g1, g2 = s.sb("g1", [P, D]), s.sb("g2", [P, I])
        wsum, mean, scale = s.sb("wsum", [P, 2]), s.sb("mean", [P, 2]), s.sb("scale", [P, 2])
        stats, mv, ve, rstd = s.sb("stats", [P, TB, 6]), s.sb("mv", [P, TB, 2]), s.sb("ve", [P, TB]), s.sb("rstd", [P, TB])
        xn, xsq = s.sb("xn", [P, TB, D]), s.sb("xsq", [P, TB, D])
        ms, rs, am, inv, dq = s.sb("ms", [P, TB]), s.sb("rs", [P, TB]), s.sb("am", [P, TB]), s.sb("inv", [P, TB]), s.sb("dq", [P, TB])
        xq, xqT = s.sb("xq", [P, TB, D], BF16), s.sb("xqT", [P, DC, S], BF16)
        sg, h, hsq = s.sb("sg", [P, TB, I]), s.sb("h", [P, TB, I]), s.sb("hsq", [P, I])
        ms2, rs2, am2, inv2, dq2 = s.sb("ms2", [P, TB]), s.sb("rs2", [P, TB]), s.sb("am2", [P, TB]), s.sb("inv2", [P, TB]), s.sb("dq2", [P, TB])
        hq, hqT = s.sb("hq", [P, TB, I], BF16), s.sb("hqT", [P, IC, S], BF16)
        pY = s.ps("pY", [P, 3, 512])
        pT, pZ, pW = s.ps("pT", [P, 2, 512]), s.ps("pZ", [P, 512]), s.ps("pW", [P, 512])
        (weights, wsum_ready, wsum_psum, wq_ready, ve_ready, rstd_ready, ms_ready, rs_ready, xq_ready, xqT_psum, xqT_ready, y_psum,
         silu_ready, h_ready, hsq_ready, rs2_ready, hq_ready, hqT_psum, hqT_ready, z_psum, dve_chain) = s.sem(
            "weights", "wsum_ready", "wsum_psum", "wq_ready", "ve_ready", "rstd_ready", "ms_ready", "rs_ready", "xq_ready", "xqT_psum",
            "xqT_ready", "y_psum", "silu_ready", "h_ready", "hsq_ready", "rs2_ready", "hq_ready", "hqT_psum", "hqT_ready", "z_psum", "dve_chain")
        pYf = pY[:, :, :].rearrange("p a n -> p (a n)")
        pTb = [pT[:, i, :].bitcast(BF16) for i in range(2)]
        with nc.Block() as block:

            @block.sync
            def _(sp):
                sp.dma_start(wg[:, :, :], wgT.rearrange("(c p) n -> p c n", p=P)).then_inc(weights, 16)
                for j in range(IC):
                    sp.dma_start(wd[0:iw[j], j, :], wdT[j * P:j * P + iw[j], :]).then_inc(weights, 16)
                sp.dma_start(g1[:, :], gg.rearrange("(a n) -> a n", a=1).to_broadcast([P, D])).then_inc(weights, 16)
                sp.dma_start(g2[:, :], gd.rearrange("(a n) -> a n", a=1).to_broadcast([P, I])).then_inc(weights, 16)

            @block.gpsimd
            def _(pool):
                with pool.Fori(0, B) as b:
                    for a, (ready, src, done, dst) in enumerate(((ve_ready, ve, rstd_ready, rstd), (ms_ready, ms, rs_ready, rs))):
                        pool.wait_ge(ready, b + 1)
                        nc.gpsimd.tensor_tensor(dst[:, :], src[:, :], k.minus_half[:, 0:TB], ALU.pow).then_inc(done, 1)
                    for t in range(TB):
                        pool.wait_ge(hsq_ready, b * TB + t + 1)
                        nc.gpsimd.tensor_tensor(rs2[:, t:t + 1], ms2[:, t:t + 1], k.minus_half[:, 0:1], ALU.pow).then_inc(rs2_ready, 1)

            @block.vector
            def _(dve):
                chain = Chain(dve, dve_chain)
                dve.wait_ge(weights, 16 * (3 + IC))
                last_rows = iw[IC - 1]
                chain.link(nc.vector.memset(wd[last_rows:P, IC - 1, :], 0.0))
                for m, w in ((0, wg), (1, wd)):
                    chain.link(nc.vector.tensor_reduce(wsum[:, m:m + 1], w[:, :, :], AX.XY, ALU.add, apply_absolute_value=True))
                nc.vector.tensor_scalar(wsum[:, :], wsum[:, :], 1.0, None, ALU.mult).then_inc(wsum_ready, 1)
                dve.wait_ge(wsum_psum, 1)
                for m, n in ((0, D * N), (1, D * I)):
                    chain.link(nc.vector.tensor_scalar(mean[:, m:m + 1], pW[:, m:m + 1], 1.0 / n, Q_EPS, ALU.mult, ALU.max))
                chain.link(nc.vector.reciprocal(scale[:, :], mean[:, :]))
                for m, (w, wq) in enumerate(((wg, wgq), (wd, wdq))):
                    chain.link(nc.vector.tensor_scalar(w[:, :, :], w[:, :, :], scale[:, m:m + 1], MAGIC, ALU.mult, ALU.add))
                    chain.link(nc.vector.tensor_scalar(w[:, :, :], w[:, :, :], MAGIC, 1.0, ALU.subtract, ALU.min))
                    last = nc.vector.tensor_scalar(wq[:, :, :], w[:, :, :], -1.0, None, ALU.max)
                    chain.link(last)
                nc.vector.tensor_copy(wsum[:, 0:1], scale[:, 0:1]).then_inc(wq_ready, 1)

                def quantise(out, z, a, ainv, adq, m):
                    chain.link(nc.vector.tensor_reduce(a, z, AX.X, ALU.max, apply_absolute_value=True))
                    chain.link(nc.vector.tensor_scalar(a, a, Q_EPS, None, ALU.max))
                    chain.link(nc.vector.reciprocal(ainv, a))
                    chain.link(nc.vector.tensor_scalar(ainv, ainv, 127.0, None, ALU.mult))
                    chain.link(nc.vector.tensor_scalar(adq, a, mean[:, m:m + 1], 1.0 / 127.0, ALU.mult, ALU.mult))
                    chain.link(nc.vector.tensor_scalar(z, z, ainv, MAGIC, ALU.mult, ALU.add))
                    chain.link(nc.vector.tensor_scalar(z, z, MAGIC, 127.0, ALU.subtract, ALU.min))
                    return nc.vector.tensor_scalar(out, z, -128.0, None, ALU.max)

                with dve.Fori(0, B) as b:
                    chain.restart()
                    for t in range(TB):
                        chain.link(nc.vector.bn_stats(stats[:, t, :], k.x[:, b * TB + t, :]))
                    for t in range(TB):
                        chain.link(nc.vector.bn_aggr(mv[:, t, :], stats[:, t, :]))
                    nc.vector.tensor_scalar(ve[:, :], mv[:, :, 1], LN_EPS, None, ALU.add).then_inc(ve_ready, 1)
                    dve.wait_ge(rstd_ready, b + 1)
                    for t in range(TB):
                        chain.link(nc.vector.tensor_scalar(xn[:, t, :], k.x[:, b * TB + t, :], mv[:, t, 0:1], rstd[:, t:t + 1],
                                                           ALU.subtract, ALU.mult))
                    chain.link(nc.vector.tensor_tensor(xsq[:, :, :], xn[:, :, :], xn[:, :, :], ALU.mult))
                    chain.link(nc.vector.tensor_reduce(ms[:, :], xsq[:, :, :], AX.X, ALU.add))
                    nc.vector.tensor_scalar(ms[:, :], ms[:, :], 1.0 / D, RMS_EPS, ALU.mult, ALU.add).then_inc(ms_ready, 1)
                    dve.wait_ge(rs_ready, b + 1)
                    for t in range(TB):
                        chain.link(nc.vector.scalar_tensor_tensor(out=xn[:, t, :], in0=xn[:, t, :], scalar=rs[:, t:t + 1], in1=g1[:, :],
                                                                  op0=ALU.mult, op1=ALU.mult))
                        quantise(xq[:, t, :], xn[:, t, :], am[:, t:t + 1], inv[:, t:t + 1], dq[:, t:t + 1], 0).then_inc(xq_ready, 1)
                    for t in range(TB):
                        n = b * TB + t
                        dve.wait_ge(silu_ready, n + 1)
                        nc.vector.scalar_tensor_tensor(out=h[:, t, :], in0=pYf[:, I:N], scalar=dq[:, t:t + 1], in1=sg[:, t, :],
                                                       op0=ALU.mult, op1=ALU.mult).then_inc(h_ready, 1)
                        dve.wait_ge(h_ready, n + 1)
                        chain.link(nc.vector.tensor_tensor(hsq[:, :], h[:, t, :], h[:, t, :], ALU.mult))
                        chain.link(nc.vector.tensor_reduce(ms2[:, t:t + 1], hsq[:, :], AX.X, ALU.add))
                        nc.vector.tensor_scalar(ms2[:, t:t + 1], ms2[:, t:t + 1], 1.0 / I, RMS_EPS, ALU.mult, ALU.add).then_inc(hsq_ready, 1)
                        dve.wait_ge(rs2_ready, n + 1)
                        chain.link(nc.vector.scalar_tensor_tensor(out=h[:, t, :], in0=h[:, t, :], scalar=rs2[:, t:t + 1], in1=g2[:, :],
                                                                  op0=ALU.mult, op1=ALU.mult))
                        quantise(hq[:, t, :], h[:, t, :], am2[:, t:t + 1], inv2[:, t:t + 1], dq2[:, t:t + 1], 1).then_inc(hq_ready, 1)
                    dve.wait_ge(z_psum, b + 1)
                    for t in range(TB):
                        xt = k.x[:, b * TB + t, :]
                        chain.link(nc.vector.scalar_tensor_tensor(out=xt, in0=pZ[:, t * D:(t + 1) * D], scalar=dq2[:, t:t + 1], in1=xt,
                                                                  op0=ALU.mult, op1=ALU.add))

            @block.scalar
            def _(act):
                with act.Fori(0, B) as b:
                    for t in range(TB):
                        act.wait_ge(xqT_psum, b * TB + t + 1)
                        nc.scalar.activation(xqT[:, :, t * P:t * P + P], pTb[t][:, 0:D].rearrange("p (c n) -> p c n", c=DC), ACT.Copy).then_inc(xqT_ready, 1)
                    for t in range(TB):
                        act.wait_ge(y_psum, b * TB + t + 1)
                        nc.scalar.activation(sg[:, t, :], pYf[:, 0:I], ACT.Silu, scale=dq[:, t:t + 1]).then_inc(silu_ready, 1)
                        act.wait_ge(hqT_psum, b * TB + t + 1)
                        nc.scalar.activation(hqT[:, 0:IC - 1, t * P:t * P + P],
                                             pTb[t][:, 0:(IC - 1) * P].rearrange("p (c n) -> p c n", c=IC - 1), ACT.Copy)
                        nc.scalar.activation(hqT[0:iw[-1], IC - 1, t * P:t * P + P], pTb[t][0:iw[-1], (IC - 1) * P:IC * P], ACT.Copy).then_inc(hqT_ready, 1)

            @block.tensor
            def _(pe):
                pe.wait_ge(wsum_ready, 1)
                pe.matmul(pW[:, 0:2], k.ones[:, :], wsum[:, :], start=True, stop=True).then_inc(wsum_psum, 1)
                pe.wait_ge(wq_ready, 1)
                with pe.Fori(0, B) as b:
                    for t in range(TB):
                        pe.wait_ge(xq_ready, b * TB + t + 1)
                        for c in range(DC):
                            last = pe.transpose(pTb[t][:, c * P:c * P + P], xq[:, t, c * P:c * P + P], k.ident_bf[:, :])
                        last.then_inc(xqT_psum, 1)
                    for t in range(TB):
                        pe.wait_ge(xqT_ready, b * TB + t + 1)
                        if t:
                            pe.wait_ge(h_ready, b * TB + t)
                        for lo in range(0, N, 512):
                            w = min(512, N - lo)
                            for c in range(DC):
                                last = pe.matmul(pYf[:, lo:lo + w], xqT[:, c, t * P:t * P + P], wgq[:, c, lo:lo + w],
                                                 start=c == 0, stop=c == DC - 1)
                        last.then_inc(y_psum, 1)
                        pe.wait_ge(hq_ready, b * TB + t + 1)
                        for j in range(IC):
                            last = pe.transpose(pTb[t][0:iw[j], j * P:j * P + P], hq[:, t, j * P:j * P + iw[j]], k.ident_bf[:, :])
                        last.then_inc(hqT_psum, 1)
                    for t in range(TB):
                        pe.wait_ge(hqT_ready, b * TB + t + 1)
                        for j in range(IC):
                            last = pe.matmul(pZ[:, t * D:(t + 1) * D], hqT[0:iw[j], j, t * P:t * P + P], wdq[0:iw[j], j, :],
                                             start=j == 0, stop=j == IC - 1)
                    last.then_inc(z_psum, 1)


def cross_attention_1(nc, k, ctx_rows, ctx_tail, ctxT, wqd, wkd, wkTd, wvTd, wod, gqd, gkd):
    H, HD = 16, 128
    SK = ctxT.shape[2]
    KT = (SK + P - 1) // P
    TAIL = SK - (KT - 1) * P
    C = 512
    CG = H * HD // C
    HC = C // HD
    QU, KU = TB * CG, KT * CG
    UN = QU + KU
    SU = (KT + 1) // 2
    NB = 4
    EPS = 1e-5
    NEG = -1e30
    SPLIT = 7

    with Scope(nc, "xb") as s:
        wq, wk, wkT = s.sb("wq", [P, DC, H * HD]), s.sb("wk", [P, H * HD]), s.sb("wkT", [P, H, HD])
        wvT, wo, vo = s.sb("wvT", [P, H, P]), s.sb("wo", [P, H, D]), s.sb("vo", [P, H, D])
        gq, gk, gg, dead = s.sb("gq", [P, 1]), s.sb("gk", [P, 1]), s.sb("gg", [P, 1]), s.sb("dead", [P, 1])
        stats, mv, ve, rstd = s.sb("stats", [P, TB, 6]), s.sb("mv", [P, TB, 2]), s.sb("ve", [P, TB]), s.sb("rstd", [P, TB])
        xn, xnT = s.sb("xn", [P, TB, D]), s.sb("xnT", [P, DC, S])
        eT, eK = s.sb("eT", [P, KT * P]), s.sb("eK", [P, KT, P])
        q, sq = s.sb("q", [P, TB, H * HD]), s.sb("sq", [P, NB, C])
        qss, rq, kss, rk = s.sb("qss", [P, TB, H]), s.sb("rq", [P, TB, H]), s.sb("kss", [P, KT, H]), s.sb("rk", [P, KT, H])
        qn, wk_h = s.sb("qn", [P, 2, TB, HD]), s.sb("wk_h", [P, 2, HD])
        qT, qe = s.sb("qT", [P, S]), s.sb("qe", [P, 2, S])
        sc = s.sb("sc", [P, 2, KT + 1, S])
        mx, mcol, mdiag = s.sb("mx", [P, S]), s.sb("mcol", [P, TB]), s.sb("mdiag", [P, TB, P])
        rden, room = s.sb("rden", [P, TB]), s.sb("room", [P, KT, H])
        den, pe_n = s.sb("den", [P, S]), s.sb("pe_n", [P, S])
        pS = s.ps("pS", [P, NB, C])
        pQ, pV, pM, pO = s.ps("pQ", [P, 2, S]), s.ps("pV", [P, S]), s.ps("pM", [P, 2, S]), s.ps("pO", [P, TB, D])

        (weights, prepared, eT_landed, eK_landed, vo_psum, vo_ready, ve_ready, rstd_ready, xn_ready, xnT_psum, xnT_ready,
         unit_psum, unit_sq, unit_red, rk_ready, qn_ready, wk_ready, qT_psum, qT_ready,
         qe_psum, qe_ready, s_psum, s_copied, max_ready, maxT_psum, mdiag_ready, shift_psum, sub_ready, probs_ready,
         sum_ready, pv_done, den_psum, pe_ready, out_psum, out_added, dve_chain, pool_chain) = s.sem(
            "weights", "prepared", "eT_landed", "eK_landed", "vo_psum", "vo_ready", "ve_ready", "rstd_ready", "xn_ready",
            "xnT_psum", "xnT_ready", "unit_psum", "unit_sq", "unit_red", "rk_ready",
            "qn_ready", "wk_ready", "qT_psum", "qT_ready", "qe_psum", "qe_ready", "s_psum", "s_copied", "max_ready",
            "maxT_psum", "mdiag_ready", "shift_psum", "sub_ready", "probs_ready", "sum_ready", "pv_done", "den_psum",
            "pe_ready", "out_psum", "out_added", "dve_chain", "pool_chain")

        def heads(eng, step):
            step(0, 0)
            with eng.Fori(0, (H - 4) // 2) as j:
                step(2 * j + 1, 1)
                step(2 * j + 2, 0)
            for h in range(H - 3, H):
                step(h, h % 2)

        def last_heads(h, n):
            return isinstance(h, int) and h >= H - n

        def first(h):
            return isinstance(h, int) and h == 0

        with nc.Block() as block:

            @block.sync
            def _(sp):
                for dst, src in ((wq[:, :, :], wqd.rearrange("(c p) n -> p c n", p=P)), (wk[:, :], wkd),
                                 (wkT[:, :, :].rearrange("p h n -> p (h n)"), wkTd),
                                 (wvT[:, :, :].rearrange("p h n -> p (h n)"), wvTd),
                                 (wo[:, :, :], wod.rearrange("(h p) n -> p h n", p=P)),
                                 (gq[:, :], gqd.rearrange("(p a) -> p a", a=1)), (gk[:, :], gkd.rearrange("(p a) -> p a", a=1))):
                    sp.dma_start(dst, src).then_inc(weights, 16)
                sp.wait_ge(prepared, 3)

                def load_eT(b):
                    sp.dma_start(eT[:, 0:SK], ctxT[b, :, :]).then_inc(eT_landed, 16)

                def load_eK(b):
                    sp.dma_start(eK[:, 0:KT - 1, :].rearrange("p t c -> p (t c)"), ctx_rows[b, :, :]).then_inc(eK_landed, 16)
                    sp.dma_start(eK[0:TAIL, KT - 1, :], ctx_tail[b, :, :]).then_inc(eK_landed, 16)

                load_eT(0)
                load_eK(0)
                with sp.Fori(1, B) as b:
                    sp.wait_ge(s_psum, b * (H * SU))
                    load_eT(b)
                    sp.wait_ge(pv_done, b * H)
                    load_eK(b)

            @block.gpsimd
            def _(pool):
                chain = Chain(pool, pool_chain)
                nc.gpsimd.memset(eT[:, :], 0.0).then_inc(prepared, 1)
                nc.gpsimd.memset(eK[:, :, :], 0.0).then_inc(prepared, 1)
                chain.link(nc.gpsimd.memset(dead[:, :], 0.0))
                nc.gpsimd.affine_select(out=dead[:, :], in_=dead[:, :], compare_op=ALU.is_gt, fill=NEG,
                                        base=TAIL, pattern=[[0, 1]], channel_multiplier=-1).then_inc(prepared, 1)
                pool.wait_ge(weights, 16 * 7)
                with pool.Fori(0, B) as b:
                    pool.wait_ge(ve_ready, b + 1)
                    nc.gpsimd.tensor_tensor(rstd[:, :], ve[:, :], k.minus_half[:, 0:TB], ALU.pow).then_inc(rstd_ready, 1)

                    def head_weight(h, par):
                        nc.gpsimd.tensor_tensor(wk_h[:, par, :], wkT[:, h, :], k.ones[:, 0:HD], ALU.mult).then_inc(wk_ready, 1)

                    head_weight(0, 0)
                    head_weight(1, 1)

                    def step(h, par):
                        if not last_heads(h, 2):
                            pool.wait_ge(qe_psum, b * H + h + 1)
                            head_weight(h + 2, par)

                    heads(pool, step)

            @block.vector
            def _(dve):
                chain = Chain(dve, dve_chain)
                dve.wait_ge(weights, 16 * 7)
                chain.link(nc.vector.tensor_tensor(gg[:, :], gq[:, :], gk[:, :], ALU.mult))
                for i in range(0, H, 2):
                    dve.wait_ge(vo_psum, i // 2 + 1)
                    nc.vector.tensor_copy(vo[:, i:i + 2, :], pS[:, i // 2 % NB, :].rearrange("p (a n) -> p a n", a=2)).then_inc(vo_ready, 1)
                with dve.Fori(0, B) as b:
                    chain.restart()
                    for t in range(TB):
                        chain.link(nc.vector.bn_stats(stats[:, t, :], k.x[:, b * TB + t, :]))
                    for t in range(TB):
                        chain.link(nc.vector.bn_aggr(mv[:, t, :], stats[:, t, :]))
                    nc.vector.tensor_scalar(ve[:, :], mv[:, :, 1], LN_EPS, None, ALU.add).then_inc(ve_ready, 1)
                    dve.wait_ge(rstd_ready, b + 1)
                    for t in range(TB):
                        nc.vector.tensor_scalar(xn[:, t, :], k.x[:, b * TB + t, :], mv[:, t, 0:1], rstd[:, t:t + 1],
                                                ALU.subtract, ALU.mult).then_inc(xn_ready, 1)

                    for u in range(QU):
                        dve.wait_ge(unit_sq, b * UN + u + 1)
                        t, g = u // CG, u % CG
                        nc.vector.tensor_reduce(qss[:, t, g * HC:(g + 1) * HC], sq[:, u % NB, :].rearrange("p (h d) -> p h d", d=HD),
                                                AX.X, ALU.add).then_inc(unit_red, 1)
                    dve.wait_ge(unit_red, b * UN + QU)
                    chain.link(nc.vector.tensor_scalar(qss[:, :, :], qss[:, :, :], 1.0 / HD, EPS, ALU.mult, ALU.add))
                    rsqrt(nc, chain, rq[:, :, :], qss[:, :, :], room[:, 0:TB, :])
                    with dve.Fori(0, KT) as t:
                        for g in range(CG):
                            dve.wait_ge(unit_sq, b * UN + t * CG + (QU + g + 1))
                            nc.vector.tensor_reduce(kss[:, t, g * HC:(g + 1) * HC], sq[:, g % NB, :].rearrange("p (h d) -> p h d", d=HD),
                                                    AX.X, ALU.add).then_inc(unit_red, 1)
                    dve.wait_ge(unit_red, b * UN + UN)
                    chain.link(nc.vector.tensor_scalar(kss[:, :, :], kss[:, :, :], HD * EPS, None, ALU.add))
                    rsqrt(nc, chain, rk[:, :, :], kss[:, :, :], room[:, :, :])
                    dve.sem_inc(rk_ready, 1)

                    def query(h, par):
                        for t in range(TB):
                            last = nc.vector.tensor_scalar(qn[:, par, t, :], q[:, t, ds(h * HD, HD)], rq[:, t, ds(h, 1)], None, ALU.mult)
                        last.then_inc(qn_ready, 1)

                    def maximum_first(n, par):
                        dve.wait_ge(s_copied, n * KT + SPLIT)
                        chain.link(nc.vector.tensor_reduce(sc[:, par, KT, :], sc[:, par, 0:SPLIT, :].rearrange("p t q -> p q t"), AX.X, ALU.max))

                    def maximum(n, par):
                        dve.wait_ge(s_copied, n * KT + KT)
                        nc.vector.tensor_reduce(mx[:, :], sc[:, par, SPLIT:KT + 1, :].rearrange("p t q -> p q t"), AX.X, ALU.max).then_inc(max_ready, 1)

                    def shift(n):
                        dve.wait_ge(maxT_psum, n + 1)
                        ins = nc.vector.tensor_reduce(mcol[:, :], pM[:, 0, :].rearrange("p (t k) -> p t k", t=TB), AX.X, ALU.max)
                        chain.link(ins)
                        nc.vector.tensor_tensor(mdiag[:, :, :], k.ident[:, :].unsqueeze(1).to_broadcast([P, TB, P]), bcast(mcol[:, :], P),
                                                ALU.mult).then_inc(mdiag_ready, 1)

                    def total(h, par):
                        n = b * H + h
                        dve.wait_ge(probs_ready, 2 * n + 2)
                        if not first(h):
                            dve.wait_ge(den_psum, n)
                        nc.vector.tensor_reduce(den[:, :], sc[:, par, 0:KT, :].rearrange("p t q -> p q t"), AX.X, ALU.add).then_inc(sum_ready, 1)

                    def denominators(n):
                        dve.wait_ge(den_psum, n + 1)
                        chain.link(nc.vector.reciprocal(rden[:, :], pM[:, 0, 0:TB]))

                    def output(n):
                        dve.wait_ge(out_psum, n + 1)
                        for t in range(TB):
                            xt = k.x[:, b * TB + t, :]
                            last = nc.vector.scalar_tensor_tensor(xt, pO[:, t, :], rden[:, t:t + 1], xt, ALU.mult, ALU.add)
                            if t < TB - 1:
                                chain.link(last)
                        last.then_inc(out_added, 1)
                        dve.wait_ge(out_added, n + 1)

                    query(0, 0)
                    query(1, 1)
                    maximum_first(b * H, 0)
                    maximum(b * H, 0)

                    def step(h, par):
                        n = b * H + h
                        chain.restart()
                        shift(n)
                        if not first(h):
                            denominators(n - 1)
                        dve.wait_ge(shift_psum, n + 1)
                        for lo, hi in ((0, SPLIT), (SPLIT, KT)):
                            z = sc[:, par, lo:hi, :]
                            nc.vector.tensor_tensor(z, z, pM[:, 1, :].unsqueeze(1).to_broadcast([P, hi - lo, S]), ALU.subtract).then_inc(sub_ready, 1)
                        if not last_heads(h, 2):
                            dve.wait_ge(qT_psum, n + 1)
                            query(h + 2, par)
                        if not first(h):
                            output(n - 1)
                        if not last_heads(h, 1):
                            maximum_first(n + 1, 1 - par)
                        total(h, par)
                        if not last_heads(h, 1):
                            maximum(n + 1, 1 - par)

                    heads(dve, step)
                    chain.restart()
                    denominators(b * H + (H - 1))
                    output(b * H + (H - 1))

            @block.scalar
            def _(act):
                act.wait_ge(prepared, 3)
                with act.Fori(0, B) as b:
                    act.wait_ge(xnT_psum, b + 1)
                    nc.scalar.activation(xnT[:, :, :], pQ[:, :, :], ACT.Copy).then_inc(xnT_ready, 1)
                    for u in range(QU):
                        act.wait_ge(unit_psum, b * UN + u + 1)
                        if u >= NB:
                            act.wait_ge(unit_red, b * UN + u - NB + 1)
                        t, g = u // CG, u % CG
                        nc.scalar.activation(q[:, t, g * C:(g + 1) * C], pS[:, u % NB, :], ACT.Copy)
                        nc.scalar.activation(sq[:, u % NB, :], pS[:, u % NB, :], ACT.Square).then_inc(unit_sq, 1)
                    with act.Fori(0, KT) as t:
                        for g in range(CG):
                            act.wait_ge(unit_psum, b * UN + t * CG + (QU + g + 1))
                            act.wait_ge(unit_red, b * UN + t * CG + (QU + g - NB + 1))
                            nc.scalar.activation(sq[:, g, :], pS[:, g, :], ACT.Square).then_inc(unit_sq, 1)

                    def queries_T(n):
                        act.wait_ge(qT_psum, n + 1)
                        nc.scalar.activation(qT[:, :], pQ[:, 0, :], ACT.Copy, scale=gg[:, 0:1]).then_inc(qT_ready, 1)

                    def queries_e(n, par):
                        act.wait_ge(qe_psum, n + 1)
                        nc.scalar.activation(qe[:, par, :], pQ[:, 1, :], ACT.Copy).then_inc(qe_ready, 1)

                    def copy_scores(n, h, par, lo, hi):
                        for kt in range(lo, hi):
                            if kt % 2 == 0:
                                act.wait_ge(s_psum, n * SU + (kt // 2 + 1))
                            src = pS[:, kt // 2 % NB, (kt % 2) * S:(kt % 2) * S + S]
                            dst, r = sc[:, par, kt, :], rk[:, kt, ds(h, 1)]
                            if kt < KT - 1:
                                ins = nc.scalar.activation(dst, src, ACT.Copy, scale=r)
                            else:
                                ins = nc.scalar.activation(dst, src, ACT.Identity, scale=r, bias=dead[:, 0:1])
                            ins.then_inc(s_copied, 1)

                    def exponentials(n, par, part_):
                        lo, hi = ((0, SPLIT), (SPLIT, KT))[part_]
                        act.wait_ge(sub_ready, 2 * n + 1 + part_)
                        z = sc[:, par, lo:hi, :]
                        nc.scalar.activation(z, z, ACT.Exp).then_inc(probs_ready, 1)

                    n0 = b * H
                    queries_T(n0)
                    queries_e(n0, 0)
                    queries_T(n0 + 1)
                    queries_e(n0 + 1, 1)
                    act.wait_ge(rk_ready, b + 1)
                    copy_scores(n0, 0, 0, 0, KT)

                    def weighted(h):
                        n = b * H + h
                        act.wait_ge(pv_done, n + 1)
                        if not first(h):
                            act.wait_ge(out_psum, n)
                        nc.scalar.activation(pe_n[:, :], pV[:, :], ACT.Copy).then_inc(pe_ready, 1)

                    def step(h, par):
                        n = b * H + h
                        if not first(h):
                            weighted(h - 1)
                        if not last_heads(h, 1):
                            if not first(h):
                                act.wait_ge(sum_ready, n)
                            copy_scores(n + 1, h + 1, 1 - par, 0, 6)
                        exponentials(n, par, 0)
                        if not last_heads(h, 1):
                            copy_scores(n + 1, h + 1, 1 - par, 6, 8)
                        exponentials(n, par, 1)
                        if not last_heads(h, 1):
                            copy_scores(n + 1, h + 1, 1 - par, 8, KT)
                        if not last_heads(h, 2):
                            queries_T(n + 2)
                            queries_e(n + 2, par)

                    heads(act, step)
                    weighted(H - 1)

            @block.tensor
            def _(pe):
                pe.wait_ge(weights, 16 * 7)
                pe.wait_ge(prepared, 3)
                for h in range(H):
                    if h % 2 == 0 and h // 2 >= NB:
                        pe.wait_ge(vo_ready, h // 2 - NB + 1)
                    last = pe.matmul(pS[:, h // 2 % NB, (h % 2) * D:(h % 2 + 1) * D], wvT[:, h, :], wo[:, h, :], start=True, stop=True)
                    if h % 2:
                        last.then_inc(vo_psum, 1)
                with pe.Fori(0, B) as b:
                    for t in range(TB):
                        pe.wait_ge(xn_ready, b * TB + t + 1)
                        for c in range(DC):
                            last = pe.transpose(pQ[:, c, t * P:t * P + P], xn[:, t, c * P:c * P + P], k.ident[:, :])
                    last.then_inc(xnT_psum, 1)
                    pe.wait_ge(vo_ready, H // 2)
                    pe.wait_ge(xnT_ready, b + 1)
                    for u in range(QU):
                        if u >= NB:
                            pe.wait_ge(unit_sq, b * UN + u - NB + 1)
                        t, g = u // CG, u % CG
                        for c in range(DC):
                            last = pe.matmul(pS[:, u % NB, :], xnT[:, c, t * P:t * P + P], wq[:, c, g * C:(g + 1) * C], start=c == 0, stop=c == DC - 1)
                        last.then_inc(unit_psum, 1)
                    pe.wait_ge(eT_landed, b * 16 + 16)
                    for u in range(QU, UN):
                        pe.wait_ge(unit_sq, b * UN + u - NB + 1)
                        t, g = (u - QU) // CG, (u - QU) % CG
                        pe.matmul(pS[:, u % NB, :], eT[:, t * P:t * P + P], wk[:, g * C:(g + 1) * C], start=True, stop=True).then_inc(unit_psum, 1)

                    def queries_T(n, par):
                        pe.wait_ge(qn_ready, n + 1)
                        for t in range(TB):
                            last = pe.transpose(pQ[:, 0, t * P:t * P + P], qn[:, par, t, :], k.ident[:, :])
                        last.then_inc(qT_psum, 1)

                    def queries_e(n, par):
                        pe.wait_ge(qT_ready, n + 1)
                        pe.wait_ge(wk_ready, n + 1)
                        pe.matmul(pQ[:, 1, :], wk_h[:, par, :], qT[:, :], start=True, stop=True).then_inc(qe_psum, 1)

                    def scores(n, par, lo, hi, fresh=False):
                        for kt in range(lo, hi):
                            u = kt // 2
                            if kt % 2 == 0 and not (fresh and u < NB):
                                if u >= NB:
                                    pe.wait_ge(s_copied, n * KT + 2 * (u - NB) + 2)
                                else:
                                    pe.wait_ge(s_copied, n * KT)
                            last = pe.matmul(pS[:, u % NB, (kt % 2) * S:(kt % 2) * S + S], eT[:, kt * P:kt * P + P], qe[:, par, :],
                                             start=True, stop=True)
                            if kt % 2 or kt == KT - 1:
                                last.then_inc(s_psum, 1)

                    def max_T(n):
                        pe.wait_ge(max_ready, n + 1)
                        for t in range(TB):
                            last = pe.transpose(pM[:, 0, t * P:t * P + P], mx[:, t * P:t * P + P], k.ident[:, :])
                        last.then_inc(maxT_psum, 1)

                    def shift(n):
                        pe.wait_ge(mdiag_ready, n + 1)
                        pe.matmul(pM[:, 1, :], k.ones[:, :], mdiag[:, :, :], start=True, stop=True).then_inc(shift_psum, 1)

                    def weighted(n, par, lo, hi):
                        for kt in range(lo, hi):
                            if kt == 0 or kt == SPLIT:
                                pe.wait_ge(probs_ready, 2 * n + (1 if kt == 0 else 2))
                            last = pe.matmul(pV[:, :], eK[:, kt, :], sc[:, par, kt, :], start=kt == 0, stop=kt == KT - 1)
                        if hi == KT:
                            last.then_inc(pv_done, 1)

                    def output(h):
                        n = b * H + h
                        pe.wait_ge(pe_ready, n + 1)
                        if not first(h):
                            pe.wait_ge(out_added, n)
                        for t in range(TB):
                            last = pe.matmul(pO[:, t, :], pe_n[:, t * P:t * P + P], vo[:, h, :], start=True, stop=True)
                        last.then_inc(out_psum, 1)

                    n0 = b * H
                    pe.wait_ge(unit_sq, b * UN + UN)
                    for h in range(2):
                        queries_T(n0 + h, h)
                        queries_e(n0 + h, h)
                        pe.wait_ge(qe_ready, n0 + h + 1)
                    scores(n0, 0, 0, KT, fresh=True)
                    pe.wait_ge(eK_landed, b * 32 + 32)

                    def denominator(n):
                        pe.wait_ge(sum_ready, n + 1)
                        for t in range(TB):
                            last = pe.matmul(pM[:, 0, t:t + 1], den[:, t * P:t * P + P], k.ones[:, 0:1], start=True, stop=True)
                        last.then_inc(den_psum, 1)

                    def step(h, par):
                        n = b * H + h
                        if not last_heads(h, 1):
                            pe.wait_ge(qe_ready, n + 2)
                            scores(n + 1, 1 - par, 0, 2)
                        max_T(n)
                        if not last_heads(h, 1):
                            scores(n + 1, 1 - par, 2, 4)
                        shift(n)
                        if not first(h):
                            denominator(n - 1)
                        if not last_heads(h, 1):
                            scores(n + 1, 1 - par, 4, 10)
                        if not first(h):
                            output(h - 1)
                        if not last_heads(h, 1):
                            scores(n + 1, 1 - par, 10, KT)
                        weighted(n, par, 0, 4)
                        if not last_heads(h, 2):
                            queries_T(n + 2, par)
                        weighted(n, par, 4, KT)
                        if not last_heads(h, 2):
                            queries_e(n + 2, par)

                    heads(pe, step)
                    denominator(b * H + (H - 1))
                    output(H - 1)


def sparse_experts(nc, k, gateT, wT, atoms, eawd, impd, idxd):
    E, A = eawd.shape
    NS = atoms.shape[1]
    ST = NS // P
    CLIP = 50.0
    EG = 512 // D
    UNITS = E // EG + 1
    G = UNITS - 1

    with Scope(nc, "sp") as s:
        gate, at, eaw = s.sb("gate", [P, DC, E]), s.sb("at", [A, NS]), s.sb("eaw", [E, A])
        w9 = s.sb("w9", [P, DC, E + 1, D])
        idx, row_i, col_i, row, col = (s.sb("idx", [P, ST], I32), s.sb("row_i", [P, ST], I32), s.sb("col_i", [P, ST], I32),
                                       s.sb("row", [P, ST]), s.sb("col", [P, ST]))
        count_i, count, ecount = s.sb("count_i", [P, D], I32), s.sb("count", [P, D]), s.sb("ecount", [P, E])
        imp, wt = s.sb("imp", [P, ST, E]), s.sb("wt", [P, ST, E])
        emax, esum, erec, aw, awT = s.sb("emax", [E, 1]), s.sb("esum", [E, 1]), s.sb("erec", [E, 1]), s.sb("aw", [E, A]), s.sb("awT", [A, E])
        stats, mv = s.sb("stats", [P, NT, 6]), s.sb("mv", [P, NT, 2])
        ve, rstd, room = s.sb("ve", [P, NT]), s.sb("rstd", [P, NT]), s.sb("room", [P, NT])
        xn, xT2, xT = s.sb("xn", [P, 2, D]), s.sb("xT2", [P, 2, DC, P]), s.sb("xT", [P, NT, DC, P])
        lg, top, topi, topf = s.sb("lg", [P, NT, E]), s.sb("top", [P, NT, 8]), s.sb("topi", [P, NT, 8], U32), s.sb("topf", [P, NT, 8])
        ex, r0, r1 = s.sb("ex", [P, NT]), s.sb("r0", [P, NT]), s.sb("r1", [P, NT])
        rw, hot = s.sb("rw", [P, NT, E]), s.sb("hot", [P, NT, E])
        c1, rr = s.sb("c1", [P, 2, P]), s.sb("rr", [P, 2, E, D])
        pY = s.ps("pY", [P, UNITS, 512])
        pT, pL, pW = s.ps("pT", [P, DC, P]), s.ps("pL", [P, NT, E]), s.ps("pW", [P, ST, E])
        (weights, iotas, stats_ready, xn_ready, xT_psum, xT_ready, xT_kept, l_psum, ex_in, ex_ready, atom_in, atom_ready,
         imp_ready, aw_ready, awT_psum, awT_ready, wt_psum, rr_ready, d_used, d_psum, d_ready, x2_ready, tile_done,
         y_psum, y_used, dve_chain) = s.sem(
            "weights", "iotas", "stats_ready", "xn_ready", "xT_psum", "xT_ready", "xT_kept", "l_psum", "ex_in", "ex_ready",
            "atom_in", "atom_ready", "imp_ready", "aw_ready", "awT_psum", "awT_ready", "wt_psum", "rr_ready", "d_used",
            "d_psum", "d_ready", "x2_ready", "tile_done", "y_psum", "y_used", "dve_chain")
        LOADS = 6
        with nc.Block() as block:

            @block.sync
            def _(sp):
                for dst, src in ((gate[:, :, :], gateT.rearrange("(c p) n -> p c n", p=P)), (at[:, :], atoms), (eaw[:, :], eawd),
                                 (imp[:, :, :].rearrange("p t e -> p (t e)"), impd), (idx[:, :], idxd)):
                    sp.dma_start(dst, src).then_inc(weights, 16)
                sp.dma_start(w9[:, :, E, :], wT.rearrange("(c p) n -> p c n", p=P)).then_inc(weights, 16)

            @block.gpsimd
            def _(pool):
                nc.gpsimd.iota(count_i[:, :], pattern=[[1, D]], base=0, channel_multiplier=0).then_inc(iotas, 1)

            @block.vector
            def _(dve):
                chain = Chain(dve, dve_chain)
                for i in range(NT):
                    nc.vector.bn_stats(stats[:, i, :], k.x[:, i, :]).then_inc(stats_ready, 1)
                for i in range(NT):
                    dve.wait_ge(stats_ready, i + 1)
                    nc.vector.bn_aggr(mv[:, i, :], stats[:, i, :]).then_inc(stats_ready, 1)
                dve.wait_ge(stats_ready, 2 * NT)
                chain.link(nc.vector.tensor_scalar(ve[:, :], mv[:, :, 1], LN_EPS, None, ALU.add))
                rsqrt(nc, chain, rstd[:, :], ve[:, :], room[:, :])
                with dve.Fori(0, NT // 2) as j:
                    for a in range(2):
                        dve.wait_ge(xT_psum, j * 2 + (a + 1))
                        nc.vector.tensor_scalar(xn[:, a, :], k.x[:, j * 2 + a, :], mv[:, j * 2 + a, 0:1], rstd[:, ds(j * 2 + a, 1)],
                                                ALU.subtract, ALU.mult).then_inc(xn_ready, 1)
                dve.wait_ge(weights, 16 * LOADS)
                dve.wait_ge(iotas, 1)
                chain.link(nc.vector.tensor_copy(count[:, :], count_i[:, :]))
                chain.link(nc.vector.tensor_scalar(row_i[:, :], idx[:, :], 8, None, ALU.arith_shift_right))
                chain.link(nc.vector.tensor_scalar(col_i[:, :], idx[:, :], D - 1, None, ALU.bitwise_and))
                chain.link(nc.vector.tensor_copy(row[:, :], row_i[:, :]))
                chain.link(nc.vector.tensor_copy(col[:, :], col_i[:, :]))
                chain.link(nc.vector.tensor_reduce(emax[:, :], eaw[:, :], AX.X, ALU.max))
                nc.vector.tensor_scalar(aw[:, :], eaw[:, :], emax[:, 0:1], None, ALU.subtract).then_inc(atom_in, 1)
                dve.wait_ge(atom_ready, 1)
                chain.link(nc.vector.tensor_reduce(esum[:, :], aw[:, :], AX.X, ALU.add))
                chain.link(nc.vector.reciprocal(erec[:, :], esum[:, :]))
                nc.vector.tensor_scalar(aw[:, :], aw[:, :], erec[:, 0:1], None, ALU.mult).then_inc(aw_ready, 1)
                dve.wait_ge(imp_ready, 1)
                chain.link(nc.vector.tensor_scalar(imp[:, :, :], imp[:, :, :], 1.0, None, ALU.add))
                chain.link(nc.vector.reciprocal(imp[:, :, :], imp[:, :, :]))
                dve.wait_ge(wt_psum, 1)
                chain.link(nc.vector.tensor_tensor(wt[:, :, :], pW[:, :, :], imp[:, :, :], ALU.mult))

                for dc in range(DC):
                    with dve.Fori(0, ST // 2) as j:
                        for a in range(2):
                            dve.wait_ge(d_used, j * 2 + (dc * ST + a + 1))
                            st = j * 2 + a
                            nc.vector.tensor_scalar(c1[:, a, :], count[:, dc * P:(dc + 1) * P], col[:, ds(st, 1)], None, ALU.is_equal)
                            for e in range(E):
                                last = nc.vector.tensor_scalar(rr[:, a, e, :], count[:, :], row[:, ds(st, 1)], wt[:, st, e:e + 1],
                                                               ALU.is_equal, ALU.mult)
                            last.then_inc(rr_ready, 1)

                dve.wait_ge(l_psum, NT)
                chain.link(nc.vector.tensor_scalar(lg[:, :, :], pL[:, :, :], CLIP, -CLIP, ALU.min, ALU.max))
                for i in range(NT):
                    chain.link(nc.vector.max(top[:, i, :], lg[:, i, :]))
                    chain.link(nc.vector.max_index(topi[:, i, :], top[:, i, :], lg[:, i, :]))
                chain.link(nc.vector.tensor_copy(topf[:, :, :], topi[:, :, :]))
                nc.vector.tensor_tensor(ex[:, :], top[:, :, 1], top[:, :, 0], ALU.subtract).then_inc(ex_in, 1)
                dve.wait_ge(ex_ready, 1)
                chain.link(nc.vector.tensor_scalar(r1[:, :], ex[:, :], 1.0, None, ALU.add))
                chain.link(nc.vector.reciprocal(r0[:, :], r1[:, :]))
                chain.link(nc.vector.tensor_tensor(r1[:, :], r0[:, :], ex[:, :], ALU.mult))
                for m, r in ((0, r0), (1, r1)):
                    dst = (rw, hot)[m]
                    cb = count[:, 0:E].unsqueeze(1).to_broadcast([P, NT, E])
                    chain.link(nc.vector.tensor_tensor(dst[:, :, :], cb, bcast(topf[:, :, m], E), ALU.is_equal))
                    chain.link(nc.vector.tensor_tensor(dst[:, :, :], dst[:, :, :], bcast(r[:, :], E), ALU.mult))
                chain.link(nc.vector.tensor_tensor(rw[:, :, :], rw[:, :, :], hot[:, :, :], ALU.add))

                with dve.Fori(0, NT) as i:
                    chain.restart()
                    xt = k.x[:, i, :]
                    for u in range(UNITS):
                        dve.wait_ge(y_psum, i * UNITS + (u + 1))
                        if u < G:
                            for a in range(EG):
                                e = u * EG + a
                                last = nc.vector.scalar_tensor_tensor(xt, pY[:, u, a * D:(a + 1) * D], rw[:, i, e:e + 1], xt, ALU.mult, ALU.add)
                                if a < EG - 1:
                                    chain.link(last)
                        else:
                            last = nc.vector.tensor_tensor(xt, xt, pY[:, u, 0:D], ALU.add)
                        last.then_inc(y_used, 1)
                        dve.wait_ge(y_used, i * UNITS + (u + 1 + UNITS))

            @block.scalar
            def _(act):
                act.sem_inc(xT_psum, 2)
                act.sem_inc(xT_kept, 1)
                act.sem_inc(d_used, 2)
                act.sem_inc(tile_done, 2)
                act.sem_inc(y_used, UNITS)
                with act.Fori(0, NT // 2) as j:
                    for a in range(2):
                        act.wait_ge(xT_psum, j * 2 + (a + 3))
                        nc.scalar.activation(xT[:, j * 2 + a, :, :], pT[:, :, :], ACT.Copy)
                        nc.scalar.activation(xT2[:, a, :, :], pT[:, :, :], ACT.Copy).then_inc(xT_ready, 1)
                act.wait_ge(atom_in, 1)
                nc.scalar.activation(aw[:, :], aw[:, :], ACT.Exp).then_inc(atom_ready, 1)
                act.wait_ge(weights, 16 * LOADS)
                nc.scalar.activation(imp[:, :, :], imp[:, :, :], ACT.Exp, scale=-1.0).then_inc(imp_ready, 1)
                act.wait_ge(awT_psum, 1)
                nc.scalar.activation(awT[:, :], pW[0:A, 0, :], ACT.Copy).then_inc(awT_ready, 1)
                for dc in range(DC):
                    act.wait_ge(d_psum, dc + 1)
                    for u in range(G):
                        last = nc.scalar.activation(w9[:, dc, u * EG:(u + 1) * EG, :], pY[:, u, :].rearrange("p (a n) -> p a n", a=EG), ACT.Copy)
                    last.then_inc(d_ready, 1)
                act.wait_ge(ex_in, 1)
                nc.scalar.activation(ex[:, :], ex[:, :], ACT.Exp).then_inc(ex_ready, 1)
                with act.Fori(0, NT // 2) as j:
                    for a in range(2):
                        act.wait_ge(tile_done, j * 2 + (a + 1))
                        nc.scalar.activation(xT2[:, a, :, :], xT[:, j * 2 + a, :, :], ACT.Copy).then_inc(x2_ready, 1)

            @block.tensor
            def _(pe):
                pe.wait_ge(weights, 16 * LOADS)
                with pe.Fori(0, NT // 2) as j:
                    for a in range(2):
                        pe.wait_ge(xn_ready, j * 2 + (a + 1))
                        pe.wait_ge(xT_kept, j * 2 + (a + 1))
                        for c in range(DC):
                            last = pe.transpose(pT[:, c, :], xn[:, a, c * P:c * P + P], k.ident[:, :])
                        last.then_inc(xT_psum, 1)
                        pe.wait_ge(xT_ready, j * 2 + (a + 1))
                        pe.sem_inc(xT_kept, 1)
                        for c in range(DC):
                            last = pe.matmul(pL[:, j * 2 + a, :], xT2[:, a, c, :], gate[:, c, :], start=c == 0, stop=c == DC - 1)
                        last.then_inc(l_psum, 1)
                pe.wait_ge(aw_ready, 1)
                pe.transpose(pW[0:A, 0, :], aw[:, :], k.ident[0:E, 0:E]).then_inc(awT_psum, 1)
                pe.wait_ge(awT_ready, 1)
                for st in range(ST):
                    last = pe.matmul(pW[:, st, :], at[:, st * P:(st + 1) * P], awT[:, :], start=True, stop=True)
                last.then_inc(wt_psum, 1)
                for dc in range(DC):
                    if dc:
                        pe.wait_ge(d_ready, dc)
                    pe.wait_ge(rr_ready, dc * ST + 1)

                    def entries(a, start, stop):
                        for u in range(G):
                            last = pe.matmul(pY[:, u, :], c1[:, a, :], rr[:, a, u * EG:(u + 1) * EG, :].rearrange("p e n -> p (e n)"),
                                             start=start, stop=stop, skip_group_check=True)
                        last.then_inc(d_used, 1)
                        return last

                    entries(0, True, False)
                    pe.wait_ge(rr_ready, dc * ST + 2)
                    entries(1, False, False)
                    with pe.Fori(1, ST // 2) as j:
                        for a in range(2):
                            pe.wait_ge(rr_ready, j * 2 + (dc * ST + a + 1))
                            entries(a, False, False)
                    pe.wait_ge(d_used, (dc + 1) * ST + 2)
                    pe.sem_inc(d_psum, 1)
                pe.wait_ge(d_ready, DC)
                with pe.Fori(0, NT // 2) as j:
                    for a in range(2):
                        pe.wait_ge(x2_ready, j * 2 + (a + 1))
                        for u in range(UNITS):
                            pe.wait_ge(y_used, j * (2 * UNITS) + (a * UNITS + u + 1))
                            w = EG if u < G else 1
                            for c in range(DC):
                                last = pe.matmul(pY[:, u, 0:w * D], xT2[:, a, c, :], w9[:, c, u * EG:u * EG + w, :].rearrange("p e n -> p (e n)"),
                                                 start=c == 0, stop=c == DC - 1)
                            last.then_inc(y_psum, 1)
                        pe.wait_ge(y_psum, j * (2 * UNITS) + (a + 1) * UNITS)
                        pe.sem_inc(tile_done, 1)


class Shared:

    def __init__(self, s):
        self.x = s.sb("x", [P, NT + TB, D])
        self.ident, self.ident_bf = s.sb("ident", [P, P]), s.sb("ident_bf", [P, P], BF16)
        self.ones, self.minus_half = s.sb("ones", [P, P]), s.sb("minus_half", [P, D])


def decoder(nc, t, out):
    with Scope(nc, "keep") as s:
        k = Shared(s)
        constants(nc, k)
        load_x(nc, k, t["x"])
        self_attention(nc, k, t["sa_wqkvT"], t["sa_woT"])
        cross_attention_0(nc, k, t["ctxT"], t["xa_wq"], t["xa_bq"], t["xa_wkv"], t["xa_bkv"], t["xa_wdca"], t["xa_bdca"],
                          t["xa_qn_w"], t["xa_qn_b"], t["xa_kn_w"], t["xa_kn_b"], t["xa_kn_dca_w"], t["xa_kn_dca_b"],
                          t["xa_wo"], t["xa_bo"])
        experts(nc, k, t["moe_gateT"], t["moe_w13T"], t["moe_w2T"], t["moe_s13T"], t["moe_s2T"])
        bit_mlp(nc, k, t["bit_wgT"], t["bit_gg"], t["bit_wdT"], t["bit_gd"])
        cross_attention_1(nc, k, t["ctx_rows"], t["ctx_tail"], t["ctxT"], t["xb_wq"], t["xb_wk"], t["xb_wkT"], t["xb_wvT"],
                          t["xb_wo"], t["xb_gq"], t["xb_gk"])
        sparse_experts(nc, k, t["sp_gateT"], t["sp_wT"], t["sp_atoms"], t["sp_eaw"], t["sp_imp"], t["sp_idx"])
        store_x(nc, k, out)


def laid_out(i):
    T = lambda a: a.swapaxes(-1, -2)
    cat = np.concatenate
    i = {name: np.asarray(a) for name, a in i.items()}
    a, c, m, b, e, f = ({name[len(pre):]: v for name, v in i.items() if name.startswith(pre)} for pre in
                        ("L0_attn_", "L0_xattn_", "L0_ffn_", "L1_attn_", "L1_xattn_", "L1_ffn_"))
    ctx = i["ctx_1024"]
    whole = ctx.shape[1] // P

    def by_head(w):
        z = w.reshape(w.shape[:-1] + (2, 16, 16))
        return z.swapaxes(-3, -2).reshape(w.shape)

    def by_partition(w):
        return w.reshape(-1, P, w.shape[-1]).transpose(1, 0, 2).reshape(P, -1)

    return {
        "x": i["x"],
        "sa_wqkvT": T(cat([a["Wq"], a["Wk"], a["Wv"]], 0)), "sa_woT": T(a["Wo"]),
        "ctxT": T(ctx),
        "ctx_rows": ctx[:, :whole * P].reshape(B, whole, P, -1).transpose(0, 2, 1, 3).reshape(B, P, -1),
        "ctx_tail": ctx[:, whole * P:],
        "xa_wq": c["Wq"], "xa_bq": c["bq"], "xa_wkv": cat([c["Wk"], c["Wv"]], 1), "xa_bkv": cat([c["bk"], c["bv"]], 0),
        "xa_wdca": by_head(c["Wkv_dca"]), "xa_bdca": by_head(c["bkv_dca"]),
        "xa_qn_w": c["qn_w"], "xa_qn_b": c["qn_b"], "xa_kn_w": c["kn_w"], "xa_kn_b": c["kn_b"],
        "xa_kn_dca_w": c["kn_dca_w"], "xa_kn_dca_b": c["kn_dca_b"], "xa_wo": c["Wo"], "xa_bo": c["bo"],
        "moe_gateT": T(m["gate_w"]), "moe_w13T": cat([T(m["w1"]), T(m["w3"])], 2), "moe_w2T": T(m["w2"]),
        "moe_s13T": cat([T(m["sw1"]), T(m["sw3"])], 1), "moe_s2T": T(m["sw2"]),
        "bit_wgT": T(b["w_gate"]), "bit_gg": b["g_gate"], "bit_wdT": T(b["w_down"]), "bit_gd": b["g_down"],
        "xb_wq": e["Wq"], "xb_wk": e["Wk"], "xb_wkT": by_partition(T(e["Wk"])), "xb_wvT": by_partition(T(e["Wv"])),
        "xb_wo": e["Wo"], "xb_gq": e["gq"], "xb_gk": e["gk"],
        "sp_gateT": T(f["gate_w"]), "sp_wT": T(f["W"]), "sp_atoms": f["atoms"], "sp_eaw": f["expert_atom_weights"],
        "sp_imp": by_partition(T(f["importance"])), "sp_idx": T(f["mask_idx"].reshape(-1, P)),
    }


def kernel(**inputs):
    import concourse.bacc as bacc
    from concourse.bass_utils import run_bass_kernel_spmd

    nc = bacc.Bacc("TRN2", target_bir_lowering=False, num_devices=1)
    arrays, args = {}, {}
    for name, a in laid_out(inputs).items():
        a = np.ascontiguousarray(a)
        arrays[f"in_{name}"] = a
        args[name] = nc.dram_tensor(f"in_{name}", a.shape, mybir.dt.from_np(a.dtype), kind="ExternalInput").ap()
    out = nc.dram_tensor("out_x", (B, S, D), F32, kind="ExternalOutput").ap()
    decoder(nc, args, out)
    r = run_bass_kernel_spmd(nc, [arrays], core_ids=[0])
    return r.results[0]["out_x"]
```

```python
from contextlib import ExitStack

import numpy as np

import concourse.bass as bass
from concourse import mybir

F32 = mybir.dt.float32
BF16 = mybir.dt.bfloat16
I32 = mybir.dt.int32
U32 = mybir.dt.uint32
ALU = mybir.AluOpType
ACT = mybir.ActivationFunctionType
AX = mybir.AxisListType
ds = bass.ds

P = 128
B = 8
S = 256
D = 256
DC = D // P
TB = S // P
NT = B * TB
LN_EPS = 1e-5


class Scope:

    def __init__(self, nc, stage):
        self.nc, self.stage, self.stack, self.sems = nc, stage, ExitStack(), []

    def __enter__(self):
        self.stack.__enter__()
        return self

    def __exit__(self, *e):
        if self.sems and e[0] is None:
            with self.nc.Block() as block:

                @block.gpsimd
                def _(pool):
                    for sem in self.sems:
                        pool.sem_clear(sem)

        return self.stack.__exit__(*e)

    def sb(self, name, shape, dt=F32):
        return self.stack.enter_context(self.nc.sbuf_tensor(f"{self.stage}_{name}", shape, dt))

    def ps(self, name, shape, dt=F32):
        return self.stack.enter_context(self.nc.psum_tensor(f"{self.stage}_{name}", shape, dt))

    def sem(self, *names):
        got = [self.stack.enter_context(self.nc.semaphore(f"{self.stage}_{n}")) for n in names]
        self.sems += got
        return got if len(got) > 1 else got[0]


class Chain:

    def __init__(self, eng, sem):
        self.eng, self.sem, self.count = eng, sem, 0

    def restart(self):
        self.eng.sem_clear(self.sem)
        self.count = 0

    def link(self, ins):
        self.count += 1
        ins.then_inc(self.sem, 1)
        self.eng.wait_ge(self.sem, self.count)


def bcast(ap, n):
    return ap.unsqueeze(len(ap.shape)).to_broadcast(list(ap.shape) + [n])


def rsqrt(nc, chain, y, v, t):
    yi = y.bitcast(I32)
    chain.link(nc.vector.tensor_scalar(yi, v.bitcast(I32), 1, None, ALU.logical_shift_right))
    chain.link(nc.vector.tensor_scalar(yi, yi, -1.0, float(0x5F3759DF), ALU.mult, ALU.add))
    for _ in range(3):
        chain.link(nc.vector.scalar_tensor_tensor(t, y, -0.5, y, ALU.mult, ALU.mult))
        chain.link(nc.vector.tensor_tensor(t, t, v, ALU.mult))
        last = nc.vector.scalar_tensor_tensor(y, t, 1.5, y, ALU.add, ALU.mult)
        chain.link(last)


def constants(nc, k):
    with Scope(nc, "const") as s:
        zeroed, done, half = s.sem("zeroed", "done", "half")
        with nc.Block() as block:

            @block.gpsimd
            def _(pool):
                nc.gpsimd.memset(k.ident[:, :], 0.0).then_inc(zeroed, 1)
                pool.wait_ge(zeroed, 1)
                nc.gpsimd.affine_select(out=k.ident[:, :], in_=k.ident[:, :], compare_op=ALU.not_equal, fill=1.0,
                                        base=0, pattern=[[-1, P]], channel_multiplier=1).then_inc(done, 1)
                nc.gpsimd.memset(k.ones[:, :], 1.0).then_inc(half, 1)
                nc.gpsimd.memset(k.x[:, NT:NT + TB, :], 0.0).then_inc(half, 1)
                nc.gpsimd.memset(k.minus_half[:, :], -0.5).then_inc(half, 1)

            @block.vector
            def _(dve):
                dve.wait_ge(done, 1)
                nc.vector.tensor_copy(k.ident_bf[:, :], k.ident[:, :]).then_inc(half, 1)
                dve.wait_ge(half, 4)


def load_x(nc, k, x):
    with Scope(nc, "in") as s:
        landed = s.sem("landed")
        with nc.Block() as block:

            @block.sync
            def _(sp):
                for b in range(0, B, 2):
                    sp.dma_start(k.x[:, b * TB:(b + 2) * TB, :],
                                 x[b:b + 2].rearrange("b (t p) d -> p (b t) d", p=P)).then_inc(landed, 16)
                sp.wait_ge(landed, 16 * B // 2)


def store_x(nc, k, out):
    with Scope(nc, "out") as s:
        landed = s.sem("landed")
        with nc.Block() as block:

            @block.sync
            def _(sp):
                for b in range(0, B, 2):
                    sp.dma_start(out[b:b + 2].rearrange("b (t p) d -> p (b t) d", p=P),
                                 k.x[:, b * TB:(b + 2) * TB, :]).then_inc(landed, 16)
                sp.wait_ge(landed, 16 * B // 2)


def self_attention(nc, k, wqkvT, woT):
    H, KV, HD = 16, 4, 16
    R = H // KV
    PAD = 32
    NQKV = (H + 2 * KV) * HD
    NG = H + 2 * KV
    RMS_EPS = 1.1920928955078125e-07
    UNITS = H
    XT_AT = 5

    with Scope(nc, "sa") as s:
        wqkv, wo = s.sb("wqkv", [P, DC, NQKV]), s.sb("wo", [P, DC, D])
        stats, mv, ve, rstd = s.sb("stats", [P, TB, 6]), s.sb("mv", [P, TB, 2]), s.sb("ve", [P, TB]), s.sb("rstd", [P, TB])
        xn, xnT = s.sb("xn", [P, TB, D]), s.sb("xnT", [P, DC, S])
        qkv, sq = s.sb("qkv", [P, TB, NQKV]), s.sb("sq", [P, TB, NQKV])
        ms, rs, room = s.sb("ms", [P, TB * NG]), s.sb("rs", [P, TB * NG]), s.sb("room", [P, TB * NG])
        q_pad, k_pad = s.sb("q_pad", [P, TB, H, PAD]), s.sb("k_pad", [P, TB, KV, PAD])
        v_aug, vn = s.sb("v_aug", [P, TB, KV, PAD]), s.sb("vn", [P, TB, KV, HD])
        qT, kTz = s.sb("qT", [P, R, S]), s.sb("kTz", [P, KV, S])
        probs = s.sb("probs", [P, 2, TB, S])
        yT = s.sb("yT", [P, R, S])
        rden, num, y, dot = s.sb("rden", [P, TB, R, KV]), s.sb("num", [P, TB, H, HD]), s.sb("y", [P, TB, D]), s.sb("dot", [P, TB, H])
        y2T = s.sb("y2T", [P, DC, S])
        pT, pQ = s.ps("pT", [P, 512]), s.ps("pQ", [P, 1024])
        pS, pY = s.ps("pS", [P, 2, TB, S]), s.ps("pY", [P, R, S])

        (weights, prepared, v_ready, x_added, xn_ready, xnT_psum, xnT_ready, qkv_psum, 
         qk_ready, qkT_psum, qkT_ready, scores_ready, probs_ready, y_psum, yT_ready, y_tok, y_ready, y2_psum,
         y2T_ready, o_psum) = s.sem(
            "weights", "prepared", "v_ready", "x_added", "xn_ready", "xnT_psum", "xnT_ready", "qkv_psum",
             "qk_ready", "qkT_psum", "qkT_ready", "scores_ready", "probs_ready", "y_psum",
            "yT_ready", "y_tok", "y_ready", "y2_psum", "y2T_ready", "o_psum")
        dve_chain = s.sem("dve_chain")
        with nc.Block() as block:

            @block.sync
            def _(sp):
                sp.dma_start(wqkv[:, :, :], wqkvT.rearrange("(c p) n -> p c n", p=P)).then_inc(weights, 16)
                sp.dma_start(wo[:, :, :], woT.rearrange("(c p) n -> p c n", p=P)).then_inc(weights, 16)

            @block.gpsimd
            def _(pool):
                nc.gpsimd.memset(q_pad[:, :, :, :], 0.0).then_inc(prepared, 1)
                nc.gpsimd.memset(k_pad[:, :, :, :], 0.0).then_inc(prepared, 1)
                nc.gpsimd.memset(kTz[:, :, :], 0.0).then_inc(prepared, 1)

            @block.vector
            def _(dve):
                chain = Chain(dve, dve_chain)
                chain.link(nc.vector.memset(v_aug[:, :, :, :], 0.0))
                chain.link(nc.vector.memset(v_aug[:, :, :, HD:HD + 1], 1.0))
                dve.wait_ge(prepared, 3)
                nqk = H + KV
                rst = rs[:, :].rearrange("p (t g) -> p t g", t=TB)

                def queries_keys(b):
                    for t in range(TB):
                        chain.link(nc.vector.bn_stats(stats[:, t, :], k.x[:, b * TB + t, :]))
                    for t in range(TB):
                        chain.link(nc.vector.bn_aggr(mv[:, t, :], stats[:, t, :]))
                    chain.link(nc.vector.tensor_scalar(ve[:, :], mv[:, :, 1], LN_EPS, None, ALU.add))
                    rsqrt(nc, chain, rstd[:, :], ve[:, :], room[:, 0:TB])
                    for t in range(TB):
                        nc.vector.tensor_scalar(xn[:, t, :], k.x[:, b * TB + t, :], mv[:, t, 0:1], rstd[:, t:t + 1],
                                                ALU.subtract, ALU.mult).then_inc(xn_ready, 1)
                    dve.wait_ge(qkv_psum, b + 1)
                    chain.link(nc.vector.tensor_copy(qkv[:, :, :], pQ[:, :].rearrange("p (t n) -> p t n", t=TB)[:, :, 0:NQKV]))
                    chain.link(nc.vector.tensor_tensor(sq[:, :, :], qkv[:, :, :], qkv[:, :, :], ALU.mult))
                    chain.link(nc.vector.tensor_reduce(ms[:, :], sq[:, :, :].rearrange("p t (g d) -> p (t g) d", d=HD), AX.X, ALU.add))
                    mst = ms[:, :].rearrange("p (t g) -> p t g", t=TB)
                    chain.link(nc.vector.tensor_scalar(mst[:, :, 0:nqk], mst[:, :, 0:nqk], 1.0 / HD, RMS_EPS, ALU.mult, ALU.add))
                    chain.link(nc.vector.tensor_scalar(mst[:, :, nqk:NG], mst[:, :, nqk:NG], 1e-24, None, ALU.max))
                    rsqrt(nc, chain, rs[:, :], ms[:, :], room[:, :])
                    for t in range(TB):
                        q = qkv[:, t, 0:H * HD].rearrange("p (g r d) -> p r g d", g=KV, r=R)
                        nc.vector.tensor_tensor(q_pad[:, t, :, 0:HD].rearrange("p (r g) d -> p r g d", r=R), q,
                                                bcast(rst[:, t, 0:H].rearrange("p (g r) -> p r g", g=KV), HD), ALU.mult)
                        kk = qkv[:, t, H * HD:nqk * HD].rearrange("p (g d) -> p g d", g=KV)
                        last = nc.vector.tensor_tensor(k_pad[:, t, :, 0:HD], kk, bcast(rst[:, t, H:nqk], HD), ALU.mult)
                    last.then_inc(qk_ready, 1)

                def values():
                    for t in range(TB):
                        v = qkv[:, t, nqk * HD:].rearrange("p (g d) -> p g d", g=KV)
                        nc.vector.tensor_tensor(vn[:, t, :, :], v, bcast(rst[:, t, nqk:NG], HD), ALU.mult)
                        last = nc.vector.tensor_copy(v_aug[:, t, :, 0:HD], v)
                    last.then_inc(v_ready, 1)

                queries_keys(0)
                values()
                with dve.Fori(0, B) as b:
                    chain.restart()
                    queries_keys(b + 1)
                    dve.wait_ge(y_tok, b + 1)
                    pYt = pQ[:, :].rearrange("p (t r g n) -> p t r g n", t=TB, r=R, g=KV)
                    for t in range(TB):
                        chain.link(nc.vector.reciprocal(rden[:, t, :, :], pYt[:, t, :, :, HD]))
                        yt = y[:, t, :].rearrange("p (g r d) -> p r g d", g=KV, r=R)
                        chain.link(nc.vector.tensor_tensor(yt, pYt[:, t, :, :, 0:HD], bcast(rden[:, t, :, :], HD), ALU.mult))
                        yg = y[:, t, :].rearrange("p (g r d) -> p g r d", g=KV, r=R)
                        ng = num[:, t, :, :].rearrange("p (g r) d -> p g r d", g=KV)
                        vb = vn[:, t, :, :].unsqueeze(2).to_broadcast([P, KV, R, HD])
                        chain.link(nc.vector.tensor_tensor(ng, yg, vb, ALU.mult))
                        chain.link(nc.vector.tensor_reduce(dot[:, t, :], num[:, t, :, :], AX.X, ALU.add))
                        chain.link(nc.vector.tensor_tensor(ng, vb, bcast(dot[:, t, :].rearrange("p (g r) -> p g r", g=KV), HD), ALU.mult))
                        nc.vector.tensor_tensor(y[:, t, :], y[:, t, :], num[:, t, :, :].rearrange("p h d -> p (h d)"),
                                                ALU.subtract).then_inc(y_ready, 1)
                    values()
                    dve.wait_ge(o_psum, b + 1)
                    xb = k.x[:, ds(b * TB, TB), :]
                    nc.vector.tensor_tensor(xb, xb, pQ[:, 0:TB * D].rearrange("p (t n) -> p t n", t=TB), ALU.add).then_inc(x_added, 1)
                    dve.wait_ge(x_added, b + 2)

            @block.scalar
            def _(act):
                act.sem_inc(x_added, 1)

                def x_columns(b):
                    act.wait_ge(xnT_psum, b + 1)
                    nc.scalar.activation(xnT[:, :, :], pT[:, :].rearrange("p (c n) -> p c n", c=DC), ACT.Copy).then_inc(xnT_ready, 1)

                def qk_columns(b):
                    act.wait_ge(qkT_psum, b + 1)
                    nc.scalar.activation(qT[:, :, :], pS[:, :, :, :].rearrange("p a t n -> p (a t) n"), ACT.Copy)
                    for g in range(KV):
                        rows = slice(PAD * g, PAD * g + PAD)
                        last = nc.scalar.activation(kTz[rows, g, :], pT[rows, 0:S], ACT.Copy)
                    last.then_inc(qkT_ready, 1)

                act.wait_ge(prepared, 3)
                x_columns(0)
                qk_columns(0)
                with act.Fori(0, B) as b:
                    for u in range(UNITS):
                        act.wait_ge(scores_ready, b * UNITS + u + 1)
                        if u >= 2:
                            act.wait_ge(y_psum, b * UNITS + u - 1)
                        nc.scalar.activation(probs[:, u % 2, :, :], pS[:, u % 2, :, :], ACT.Exp, scale=HD ** -0.5).then_inc(probs_ready, 1)
                        if u == XT_AT:
                            x_columns(b + 1)
                    act.wait_ge(y_psum, b * UNITS + UNITS)
                    nc.scalar.activation(yT[:, :, :], pY[:, :, :], ACT.Copy).then_inc(yT_ready, 1)
                    qk_columns(b + 1)
                    act.wait_ge(y2_psum, b + 1)
                    nc.scalar.activation(y2T[:, :, :], pT[:, :].rearrange("p (c n) -> p c n", c=DC), ACT.Copy).then_inc(y2T_ready, 1)

            @block.tensor
            def _(pe):
                def x_columns(b):
                    for t in range(TB):
                        pe.wait_ge(xn_ready, b * TB + t + 1)
                        for c in range(DC):
                            last = pe.transpose(pT[:, c * S + t * P:c * S + t * P + P], xn[:, t, c * P:c * P + P], k.ident[:, :])
                    last.then_inc(xnT_psum, 1)

                def project(b, added):
                    pe.wait_ge(xnT_ready, b + 1)
                    pe.wait_ge(x_added, added)
                    for t in range(TB):
                        for c in range(DC):
                            last = pe.matmul(pQ[:, 512 * t:512 * t + NQKV], xnT[:, c, t * P:t * P + P], wqkv[:, c, :],
                                             start=c == 0, stop=c == DC - 1)
                    last.then_inc(qkv_psum, 1)

                def qk_columns(b):
                    pe.wait_ge(qk_ready, b + 1)
                    for t in range(TB):
                        for r in range(R):
                            pe.transpose(pS[:, r // TB, r % TB, t * P:t * P + P],
                                         q_pad[:, t, r * KV:(r + 1) * KV, :].rearrange("p g d -> p (g d)"), k.ident[:, :])
                        last = pe.transpose(pT[:, t * P:t * P + P], k_pad[:, t, :, :].rearrange("p g d -> p (g d)"), k.ident[:, :])
                    last.then_inc(qkT_psum, 1)

                pe.wait_ge(weights, 32)
                x_columns(0)
                project(0, 1)
                qk_columns(0)
                with pe.Fori(0, B) as b:
                    pe.wait_ge(qkT_ready, b + 1)
                    pe.wait_ge(v_ready, b + 1)

                    def scores(u):
                        r, g = u // KV, u % KV
                        if u >= 2:
                            pe.wait_ge(probs_ready, b * UNITS + u - 1)
                        for kt in range(TB):
                            last = pe.matmul(pS[:, u % 2, kt, :], kTz[:, g, kt * P:kt * P + P], qT[:, r, :], start=True, stop=True)
                        last.then_inc(scores_ready, 1)

                    def values(u):
                        r, g = u // KV, u % KV
                        pe.wait_ge(probs_ready, b * UNITS + u + 1)
                        for kt in range(TB):
                            last = pe.matmul(pY[PAD * g:PAD * g + PAD, r, :], v_aug[:, kt, g, :], probs[:, u % 2, kt, :],
                                             start=kt == 0, stop=kt == TB - 1, tile_position=(0, PAD * g))
                        last.then_inc(y_psum, 1)

                    scores(0)
                    for u in range(1, UNITS):
                        scores(u)
                        values(u - 1)
                        if u == XT_AT - 1:
                            x_columns(b + 1)
                        if u == XT_AT + 2:
                            project(b + 1, b + 1)
                    values(UNITS - 1)
                    pe.wait_ge(probs_ready, b * UNITS + UNITS)
                    qk_columns(b + 1)
                    pe.wait_ge(yT_ready, b + 1)
                    for t in range(TB):
                        for r in range(R):
                            last = pe.transpose(pQ[:, (t * R + r) * P:(t * R + r + 1) * P], yT[:, r, t * P:t * P + P], k.ident[:, :])
                    last.then_inc(y_tok, 1)
                    pe.wait_ge(qkT_ready, b + 2)
                    for t in range(TB):
                        pe.wait_ge(y_ready, b * TB + t + 1)
                        for c in range(DC):
                            last = pe.transpose(pT[:, c * S + t * P:c * S + t * P + P], y[:, t, c * P:c * P + P], k.ident[:, :])
                    last.then_inc(y2_psum, 1)
                    pe.wait_ge(y2T_ready, b + 1)
                    for t in range(TB):
                        for c in range(DC):
                            last = pe.matmul(pQ[:, t * D:(t + 1) * D], y2T[:, c, t * P:t * P + P], wo[:, c, :], start=c == 0, stop=c == DC - 1)
                    last.then_inc(o_psum, 1)


def cross_attention_0(nc, k, ctxT, wqd, bqd, wkvd, bkvd, wdcad, bdcad, qnwd, qnbd, knwd, knbd, dwd, dbd, wod, bod):
    H, HD = 16, 16
    SK = ctxT.shape[2]
    DCA = 16
    MAIN = SK - DCA
    CH = 4
    NCH = MAIN // (CH * P)
    KT = NCH * CH + 1
    LAST = MAIN - (KT - 1) * P
    DROW = 64
    NK = KT * P
    ROWS = 6 * HD
    KR = ROWS + 2
    EPS = 1e-6
    SCALE = HD ** -0.5
    G = 4
    NGR = H // G
    PAD = 32
    UNITS = KT * 2
    HALF = 1024
    FILLS = G * TB
    assert LAST <= DROW and DROW + DCA <= P

    with Scope(nc, "xa") as s:
        wq, wo = s.sb("wq", [P, DC, D]), s.sb("wo", [P, DC, D])
        bq, bo = s.sb("bq", [P, D]), s.sb("bo", [P, D])
        wkv, wdca = s.sb("wkv", [P, 2 * D]), s.sb("wdca", [P, 2 * D])
        bkv, btail = s.sb("bkv", [P, 2 * D]), s.sb("btail", [P, 2 * D])
        qnw, qnb, knw, knb = s.sb("qnw", [P, HD]), s.sb("qnb", [P, HD]), s.sb("knw", [P, HD]), s.sb("knb", [P, HD])
        tnw, tnb = s.sb("tnw", [P, HD]), s.sb("tnb", [P, HD])
        stats, mv, ve, rstd = s.sb("stats", [P, TB, 6]), s.sb("mv", [P, TB, 2]), s.sb("ve", [P, TB]), s.sb("rstd", [P, TB])
        xn, xnT = s.sb("xn", [P, TB, D]), s.sb("xnT", [P, DC, S])
        q = s.sb("q", [P, TB, H, HD])
        q3 = s.sb("q3", [P, TB, H, 3, HD], BF16)
        qst = s.sb("qst", [P, TB, H, KR], BF16)
        qT0 = s.sb("qT0", [ROWS, H, S], BF16)
        qTs = s.sb("qTs", [KR, 2, G, S], BF16)
        eT, eTt = s.sb("eT", [P, 2, CH * P]), s.sb("eTt", [P, P])
        kk, sq = s.sb("kk", [P, CH, H, HD]), s.sb("sq", [P, CH, H, HD])
        hm, hv, hr = s.sb("hm", [P, CH * H]), s.sb("hv", [P, CH * H]), s.sb("hr", [P, CH * H])
        k1 = s.sb("k1", [P, CH, H, HD], BF16)
        kst = [s.sb("kst0", [P, CH, H, KR], BF16), s.sb("kst1", [P, CH, H, KR], BF16)]
        kst_tail = s.sb("kst_tail", [P, 1, H, KR], BF16)
        live, live_main, live_dca = s.sb("live", [P, 1]), s.sb("live_main", [P, 1]), s.sb("live_dca", [P, 1])
        kT = s.sb("kT", [KR, H, NK], BF16)
        va = s.sb("va", [P, KT + 1, H, PAD])
        mpart = s.sb("mpart", [P, 2, 2])
        probs = s.sb("probs", [P, 3, 2 * S])
        ysb, rden, y1, y2 = s.sb("ysb", [P, 2 * S]), s.sb("rden", [P, 2 * TB * G]), s.sb("y1", [P, TB, G, HD]), s.sb("y2", [P, TB, G, HD])
        y, yT = s.sb("y", [P, TB, H, HD]), s.sb("yT", [P, DC, S])
        pM, pS = s.ps("pM", [P, 4, 512]), s.ps("pS", [P, 2, 512])
        pY, pT = s.ps("pY", [P, 512]), s.ps("pT", [P, 512])

        (weights, prepared, tail_landed, ve_ready, rstd_ready, xn_ready, xnT_psum, xnT_ready, q_psum,
         qst_ready, q0_psum, q0_ready, kv_psum, 
         kk_ready, kv_taken, squared, k1_ready, k1_copied, k2_copied, centred, x_added, kst_ready, kt_psum, kt_copied, max_a, max_b, max_a_free, max_b_free, shift_ready,
         qs_psum, qs_ready, scores_ready, probs_ready, pv_done, y_copied, y_tok, y_free, y_all, yT_psum, yT_ready,
         o_psum, dve_chain, pool_chain, act_chain) = s.sem(
            "weights", "prepared", "tail_landed", "ve_ready", "rstd_ready", "xn_ready", "xnT_psum",
            "xnT_ready", "q_psum", "qst_ready", "q0_psum", "q0_ready", "kv_psum", "kk_ready", "kv_taken", "squared", "k1_ready", "k1_copied", "k2_copied", "centred", "x_added", "kst_ready", "kt_psum", "kt_copied",
            "max_a", "max_b", "max_a_free", "max_b_free", "shift_ready", "qs_psum", "qs_ready", "scores_ready",
            "probs_ready", "pv_done", "y_copied", "y_tok", "y_free", "y_all", "yT_psum", "yT_ready", "o_psum",
            "dve_chain", "pool_chain", "act_chain")
        ctx_landed = s.sem("ctx_landed0", "ctx_landed1")
        NC1 = NCH + 1
        SMALL = 15
        pTb = pT[:, :].bitcast(BF16)
        pMb = [pM[:, 2 + i, :].bitcast(BF16) for i in range(2)]
        XT_AT = 10
        pSb = [pS[:, i, :].bitcast(BF16) for i in range(2)]

        with nc.Block() as block:

            @block.sync
            def _(sp):
                def rows(dst, src, lo=0, hi=P):
                    sp.dma_start(dst[lo:hi, :], src.rearrange("(a n) -> a n", a=1).to_broadcast([hi - lo, src.shape[0]])
                                 ).then_inc(weights, 16)
                sp.dma_start(wq[:, :, :], wqd.rearrange("(c p) n -> p c n", p=P)).then_inc(weights, 16)
                sp.dma_start(wo[:, :, :], wod.rearrange("(c p) n -> p c n", p=P)).then_inc(weights, 16)
                sp.dma_start(wkv[:, :], wkvd).then_inc(weights, 16)
                sp.dma_start(wdca[:, :], wdcad).then_inc(weights, 16)
                rows(bq, bqd)
                rows(bo, bod)
                rows(bkv, bkvd)
                rows(qnw, qnwd)
                rows(qnb, qnbd)
                rows(knw, knwd)
                rows(knb, knbd)
                for dst, main, dca in ((btail, bkvd, bdcad), (tnw, knwd, dwd), (tnb, knbd, dbd)):
                    rows(dst, main, 0, DROW)
                    rows(dst, dca, DROW, P)
                sp.wait_ge(prepared, 2)
                with sp.Fori(0, B) as b:
                    for i in range(NCH):
                        before = i - 2 + NC1 if i >= 2 else NCH - 1 - (NCH - 1 - i) % 2
                        sp.wait_ge(kv_psum, b * NC1 + before + 1)
                        sp.dma_start(eT[:, i % 2, :], ctxT[b, :, i * CH * P:(i + 1) * CH * P]).then_inc(ctx_landed[i % 2], 16)
                    sp.wait_ge(kv_psum, b * NC1 + NC1)
                    sp.dma_start(eTt[:, 0:LAST], ctxT[b, :, MAIN - LAST:MAIN]).then_inc(tail_landed, 16)
                    sp.dma_start(eTt[:, DROW:DROW + DCA], ctxT[b, :, MAIN:SK]).then_inc(tail_landed, 16)

            @block.gpsimd
            def _(pool):
                chain = Chain(pool, pool_chain)
                nc.gpsimd.memset(eTt[:, :], 0.0).then_inc(prepared, 1)
                chain.link(nc.gpsimd.memset(live_main[:, :], 1.0))
                chain.link(nc.gpsimd.affine_select(out=live_main[:, :], in_=live_main[:, :], compare_op=ALU.is_gt,
                                                   fill=0.0, base=LAST, pattern=[[0, 1]], channel_multiplier=-1))
                chain.link(nc.gpsimd.memset(live_dca[:, :], 1.0))
                chain.link(nc.gpsimd.affine_select(out=live_dca[:, :], in_=live_dca[:, :], compare_op=ALU.is_ge,
                                                   fill=0.0, base=-DROW, pattern=[[0, 1]], channel_multiplier=1))
                chain.link(nc.gpsimd.affine_select(out=live_dca[:, :], in_=live_dca[:, :], compare_op=ALU.is_gt,
                                                   fill=0.0, base=DROW + DCA, pattern=[[0, 1]], channel_multiplier=-1))
                nc.gpsimd.tensor_tensor(live[:, :], live_main[:, :], live_dca[:, :], ALU.add).then_inc(prepared, 1)

                with pool.Fori(0, B + 1) as b:
                    pool.wait_ge(ve_ready, b + 1)
                    nc.gpsimd.tensor_tensor(rstd[:, :], ve[:, :], k.minus_half[:, 0:TB], ALU.pow).then_inc(rstd_ready, 1)

            @block.vector
            def _(dve):
                chain = Chain(dve, dve_chain)
                dve.wait_ge(weights, 16 * 17)
                dve.wait_ge(prepared, 2)
                chain.link(nc.vector.memset(va[:, :, :, :], 0.0))
                chain.link(nc.vector.memset(va[:, :, :, HD:HD + 1], 1.0))
                for slot, mask in ((KT - 1, live_main), (KT, live_dca)):
                    chain.link(nc.vector.tensor_scalar(va[:, slot, :, HD:HD + 1], va[:, slot, :, HD:HD + 1], mask[:, 0:1], None, ALU.mult))
                for z in kst:
                    chain.link(nc.vector.memset(z[:, :, :, :], 0.0))
                    chain.link(nc.vector.memset(z[:, :, :, ROWS:ROWS + 1], 1.0))
                for w in (wq[:, :, :].rearrange("p c (h d) -> p (c h) d", d=HD), bq[:, :].rearrange("p (h d) -> p h d", d=HD),
                          *(z[:, :].rearrange("p (h m d) -> p h m d", m=2, d=HD)[:, :, 0, :] for z in (wkv, wdca, bkv, btail))):
                    n = w.shape[1]
                    chain.link(nc.vector.tensor_reduce(hm[:, 0:n], w, AX.X, ALU.add))
                    chain.link(nc.vector.tensor_scalar(hm[:, 0:n], hm[:, 0:n], 1.0 / HD, None, ALU.mult))
                    chain.link(nc.vector.tensor_tensor(w, w, bcast(hm[:, 0:n], HD), ALU.subtract))
                dve.sem_inc(centred, 1)
                chain.link(nc.vector.memset(kst_tail[:, :, :, :], 0.0))
                chain.link(nc.vector.tensor_scalar(kst_tail[:, 0, :, ROWS:ROWS + 1], va[:, KT - 1, :, HD:HD + 1], 1.0, None, ALU.mult))
                chain.link(nc.vector.tensor_scalar(kst_tail[:, 0, :, ROWS + 1:KR], va[:, KT, :, HD:HD + 1], 1.0, None, ALU.mult))

                def head_norm(z, n, w, bias, squares):
                    zf = z.rearrange("p n h d -> p (n h) d")
                    m, v, r = hm[:, 0:n * H], hv[:, 0:n * H], hr[:, 0:n * H]
                    sqf = sq[:, 0:n, :, :].rearrange("p n h d -> p (n h) d")
                    squares(sqf, zf)
                    chain.link(nc.vector.tensor_reduce(v, sqf, AX.X, ALU.add))
                    chain.link(nc.vector.tensor_scalar(v, v, 1.0 / HD, EPS, ALU.mult, ALU.add))
                    rsqrt(nc, chain, r, v, m)
                    chain.link(nc.vector.tensor_tensor(zf, zf, bcast(r, HD), ALU.mult))
                    wb = w[:, :].unsqueeze(1).to_broadcast([P, n * H, HD])
                    bb = bias[:, :].unsqueeze(1).to_broadcast([P, n * H, HD])
                    chain.link(nc.vector.tensor_tensor(zf, zf, wb, ALU.mult))
                    chain.link(nc.vector.tensor_tensor(zf, zf, bb, ALU.add))

                def queries(b):
                    for t in range(TB):
                        chain.link(nc.vector.bn_stats(stats[:, t, :], k.x[:, b * TB + t, :]))
                    for t in range(TB):
                        chain.link(nc.vector.bn_aggr(mv[:, t, :], stats[:, t, :]))
                    nc.vector.tensor_scalar(ve[:, :], mv[:, :, 1], LN_EPS, None, ALU.add).then_inc(ve_ready, 1)
                    dve.wait_ge(rstd_ready, b + 1)
                    for t in range(TB):
                        nc.vector.tensor_scalar(xn[:, t, :], k.x[:, b * TB + t, :], mv[:, t, 0:1], rstd[:, t:t + 1],
                                                ALU.subtract, ALU.mult).then_inc(xn_ready, 1)
                    dve.wait_ge(q_psum, b + 1)
                    qf = q[:, :, :, :].rearrange("p t h d -> p t (h d)")
                    chain.link(nc.vector.tensor_tensor(qf, pM[:, 0, :].rearrange("p (t n) -> p t n", t=TB),
                                                       bq[:, :].unsqueeze(1).to_broadcast([P, TB, D]), ALU.add))
                    head_norm(q[:, :, :, :], TB, qnw, qnb, lambda o, z: chain.link(nc.vector.tensor_tensor(o, z, z, ALU.mult)))
                    rest = sq[:, 0:TB, :, :]
                    for t in range(TB):
                        chain.link(nc.vector.tensor_copy(q3[:, t, :, 0, :], q[:, t, :, :]))
                        chain.link(nc.vector.tensor_tensor(rest[:, t], q[:, t, :, :], q3[:, t, :, 0, :], ALU.subtract))
                        chain.link(nc.vector.tensor_copy(q3[:, t, :, 1, :], rest[:, t]))
                        chain.link(nc.vector.tensor_tensor(q3[:, t, :, 2, :], rest[:, t], q3[:, t, :, 1, :], ALU.subtract))
                        for at, n in ((0, 3), (3, 2), (5, 1)):
                            last = nc.vector.tensor_copy(qst[:, t, :, at * HD:(at + n) * HD],
                                                         q3[:, t, :, 0:n, :].rearrange("p h n d -> p h (n d)"))
                    last.then_inc(qst_ready, 1)

                def query_columns(b):
                    for g in range(NGR):
                        dve.wait_ge(q0_psum, b * NGR + g + 1)
                        nc.vector.tensor_copy(qT0[:, g * G:(g + 1) * G, :],
                                              pMb[g % 2][0:ROWS, :].rearrange("p (i n) -> p i n", i=G)).then_inc(q0_ready, 1)

                chain.restart()
                queries(0)
                query_columns(0)
                with dve.Fori(0, B) as b:
                    chain.restart()

                    def keys(i):
                        c = b * NC1 + i
                        n, out, bias, w, nb = (CH, kst[i % 2], bkv, knw, knb) if i < NCH else (1, kst_tail, btail, tnw, tnb)
                        slot = i * CH
                        dve.wait_ge(kv_psum, c + NC1 + 1)
                        kvb = bias[:, :].rearrange("p (h m d) -> p h m d", h=H, m=2)
                        for m, dst in ((0, kk[:, 0:n, :, :]), (1, va[:, slot:slot + n, :, 0:HD])):
                            for j in range(n):
                                kvp = pM[:, j, :].rearrange("p (h m d) -> p h m d", h=H, m=2)
                                last = nc.vector.tensor_tensor(dst[:, j], kvp[:, :, m, :], kvb[:, :, m, :], ALU.add)
                            last.then_inc((kk_ready, kv_taken)[m], 1)
                        z, rest = kk[:, 0:n, :, :], sq[:, 0:n, :, :]
                        head_norm(z, n, w, nb, lambda o, z_: dve.wait_ge(squared, c + 1))
                        if i == NCH:
                            chain.link(nc.vector.tensor_scalar(z, z, live[:, 0:1], None, ALU.mult))
                            dve.wait_ge(kv_taken, c + 1)
                            tail_v = va[:, KT - 1, :, 0:HD]
                            chain.link(nc.vector.tensor_scalar(va[:, KT, :, 0:HD], tail_v, live_dca[:, 0:1], None, ALU.mult))
                            chain.link(nc.vector.tensor_scalar(tail_v, tail_v, live_main[:, 0:1], None, ALU.mult))
                        fl = lambda a: a.rearrange("p n h d -> p (n h) d")
                        part = lambda m: out[:, 0:n, :, m * HD:(m + 1) * HD].rearrange("p n h d -> p (n h) d")
                        if i:
                            dve.wait_ge(k1_copied, 2 * c)
                        if i == 2:
                            dve.wait_ge(kt_psum, (c - 1) * (H // 2))
                        nc.vector.tensor_copy(fl(k1[:, 0:n, :, :]), fl(z)).then_inc(k1_ready, 1)
                        dve.wait_ge(k1_ready, 2 * c + 1)
                        chain.link(nc.vector.tensor_tensor(fl(rest), fl(z), fl(k1[:, 0:n, :, :]), ALU.subtract))
                        nc.vector.tensor_copy(part(3), fl(rest)).then_inc(k1_ready, 1)
                        dve.wait_ge(k1_ready, 2 * c + 2)
                        chain.link(nc.vector.tensor_tensor(part(5), fl(rest), part(3), ALU.subtract))
                        chain.link(nc.vector.tensor_copy(part(2), fl(k1[:, 0:n, :, :])))
                        dve.sem_inc(kst_ready, 1)

                    chain.restart()
                    for i in range(NC1):
                        keys(i)

                    def maxima(g):
                        for i in range(G):
                            for t in range(TB):
                                f = (b * NGR + g) * FILLS + i * TB + t
                                h = g * G + i
                                dve.wait_ge(max_a, f + 1)
                                nc.vector.tensor_reduce(mpart[:, t, 0:1], pM[:, 0:2, :].rearrange("p a n -> p (a n)"), AX.X, ALU.max).then_inc(max_a_free, 1)
                                dve.wait_ge(max_b, f + 1)
                                rest = pM[:, 2:4, :].rearrange("p a n -> p (a n)")
                                nc.vector.tensor_reduce(mpart[:, t, 1:2], rest[:, 0:MAIN - HALF], AX.X, ALU.max)
                                nc.vector.tensor_reduce(qst[:, t, h, ROWS + 1:KR], rest[:, (KT - 1) * P - HALF + DROW:(KT - 1) * P - HALF + DROW + DCA],
                                                        AX.X, ALU.max, negate=True).then_inc(max_b_free, 1)
                                dve.wait_ge(max_b_free, f + 2)
                                dve.wait_ge(max_a_free, f + 2)
                                last = nc.vector.tensor_reduce(qst[:, t, h, ROWS:ROWS + 1], mpart[:, t, :], AX.X, ALU.max, negate=True)
                        last.then_inc(shift_ready, 1)

                    def combine(g):
                        dve.wait_ge(y_tok, b * NGR + g + 1)
                        chain.link(nc.vector.reciprocal(rden[:, :], pT[:, :].rearrange("p (a n) -> p a n", n=PAD)[:, :, HD]))
                        yt = pT[:, :].rearrange("p (m t i n) -> p m t i n", m=2, t=TB, i=G)
                        rd = rden[:, :].rearrange("p (m t i) -> p m t i", m=2, t=TB)
                        chain.link(nc.vector.tensor_tensor(y1[:, :, :, :], yt[:, 0, :, :, 0:HD], bcast(rd[:, 0], HD), ALU.mult))
                        nc.vector.tensor_tensor(y2[:, :, :, :], yt[:, 1, :, :, 0:HD], bcast(rd[:, 1], HD), ALU.mult).then_inc(y_free, 1)
                        dve.wait_ge(y_free, b * NGR + g + 1)
                        chain.link(nc.vector.tensor_tensor(y[:, :, g * G:(g + 1) * G, :], y1[:, :, :, :], y2[:, :, :, :], ALU.add))

                    chain.restart()
                    maxima(0)
                    for g in range(NGR):
                        if g >= 1:
                            combine(g - 1)
                        if g + 1 < NGR:
                            maxima(g + 1)
                    queries(b + 1)
                    combine(NGR - 1)
                    nc.vector.tensor_copy(mpart[:, 0, 0:1], mpart[:, 0, 1:2]).then_inc(y_all, 1)
                    query_columns(b + 1)
                    xb = k.x[:, ds(b * TB, TB), :]
                    dve.wait_ge(o_psum, b + 1)
                    chain.link(nc.vector.tensor_tensor(xb, xb, pM[:, 0, :].rearrange("p (t n) -> p t n", t=TB), ALU.add))
                    dve.sem_inc(x_added, 1)
                    chain.link(nc.vector.tensor_tensor(xb, xb, bo[:, :].unsqueeze(1).to_broadcast([P, TB, D]), ALU.add))

            @block.scalar
            def _(act):
                act.sem_inc(kt_copied, 2)
                act.sem_inc(kv_psum, NC1)
                act.sem_inc(max_a_free, 1)
                act.sem_inc(max_b_free, 1)
                act.sem_inc(y_copied, 1)
                act.wait_ge(weights, 16 * 17)
                act.sem_inc(x_added, 1)

                def x_columns(b):
                    act.wait_ge(xnT_psum, b + 1)
                    nc.scalar.activation(xnT[:, :, :], pM[:, 1, :].rearrange("p (c n) -> p c n", c=DC), ACT.Copy).then_inc(xnT_ready, 1)

                x_columns(0)
                with act.Fori(0, B) as b:

                    def key_columns(i):
                        n = CH if i < NCH else 1
                        for hp in range(H // 2):
                            act.wait_ge(kt_psum, (b * NC1 + i) * (H // 2) + hp + 1)
                            src = pSb[hp % 2][0:KR, :].rearrange("p (i n) -> p i n", i=2)[:, :, 0:n * P]
                            nc.scalar.activation(kT[:, 2 * hp:2 * hp + 2, i * CH * P:(i * CH + n) * P], src, ACT.Copy).then_inc(kt_copied, 1)

                    for i in range(NC1):
                        c = b * NC1 + i
                        n, out = (CH, kst[i % 2]) if i < NCH else (1, kst_tail)
                        part = lambda m: out[:, 0:n, :, m * HD:(m + 1) * HD].rearrange("p n h d -> p (n h) d")
                        act.wait_ge(kk_ready, c + 1)
                        nc.scalar.activation(sq[:, 0:n, :, :], kk[:, 0:n, :, :], ACT.Square).then_inc(squared, 1)
                        if i:
                            key_columns(i - 1)
                        act.wait_ge(k1_ready, 2 * c + 1)
                        for m in range(2):
                            nc.scalar.activation(part(m), k1[:, 0:n, :, :].rearrange("p n h d -> p (n h) d"), ACT.Copy).then_inc(k1_copied, 1)
                        act.wait_ge(k1_ready, 2 * c + 2)
                        nc.scalar.activation(part(4), part(3), ACT.Copy).then_inc(k2_copied, 1)
                    key_columns(NCH)

                    def shifted_queries(g):
                        act.wait_ge(qs_psum, b * NGR + g + 1)
                        if g >= 2:
                            act.wait_ge(scores_ready, (b * NGR + g - 1) * UNITS)
                        nc.scalar.activation(qTs[:, g % 2, :, :], pTb[0:KR, :].rearrange("p (i n) -> p i n", i=G), ACT.Copy).then_inc(qs_ready, 1)

                    shifted_queries(0)
                    for g in range(NGR):
                        for u in range(UNITS):
                            n = b * (NGR * UNITS) + g * UNITS + u
                            act.wait_ge(scores_ready, n + 1)
                            if g * UNITS + u >= 3:
                                act.wait_ge(pv_done, n - 2)
                            nc.scalar.activation(probs[:, (g * UNITS + u) % 3, :], pS[:, u % 2, :], ACT.Exp, scale=SCALE).then_inc(probs_ready, 1)
                            if g == NGR - 1 and u == XT_AT:
                                x_columns(b + 1)
                        if g + 1 < NGR:
                            shifted_queries(g + 1)
                        act.wait_ge(pv_done, (b * NGR + g + 1) * UNITS)
                        nc.scalar.activation(ysb[:, :], pY[:, :], ACT.Copy).then_inc(y_copied, 1)
                    act.wait_ge(yT_psum, b + 1)
                    nc.scalar.activation(yT[:, :, :], pT[:, :].rearrange("p (c n) -> p c n", c=DC), ACT.Copy).then_inc(yT_ready, 1)

            @block.tensor
            def _(pe):
                pe.wait_ge(weights, 16 * 17)
                pe.wait_ge(centred, 1)

                def x_columns(b):
                    for t in range(TB):
                        pe.wait_ge(xn_ready, b * TB + t + 1)
                        for c in range(DC):
                            last = pe.transpose(pM[:, 1, c * S + t * P:c * S + t * P + P], xn[:, t, c * P:c * P + P], k.ident[:, :])
                    last.then_inc(xnT_psum, 1)

                def queries(b):
                    pe.wait_ge(xnT_ready, b + 1)
                    for t in range(TB):
                        for c in range(DC):
                            last = pe.matmul(pM[:, 0, t * D:(t + 1) * D], xnT[:, c, t * P:t * P + P], wq[:, c, :],
                                             start=c == 0, stop=c == DC - 1)
                    last.then_inc(q_psum, 1)

                def query_columns(b):
                    pe.wait_ge(qst_ready, b + 1)
                    for g in range(NGR):
                        if g >= 2:
                            pe.wait_ge(q0_ready, b * NGR + g - 1)
                        for i in range(G):
                            for t in range(TB):
                                last = pe.transpose(pMb[g % 2][0:ROWS, i * S + t * P:i * S + t * P + P],
                                                    qst[:, t, g * G + i, 0:ROWS], k.ident_bf[:, :])
                        last.then_inc(q0_psum, 1)

                x_columns(0)
                queries(0)
                query_columns(0)
                with pe.Fori(0, B) as b:

                    def projected(i):
                        c = b * NC1 + i
                        if i:
                            pe.wait_ge(kk_ready, c)
                            pe.wait_ge(kv_taken, c)
                        if i < NCH:
                            each = (NCH + 1) // 2 if i % 2 == 0 else NCH // 2
                            pe.wait_ge(ctx_landed[i % 2], b * (16 * each) + 16 * (i // 2 + 1))
                            for j in range(CH):
                                last = pe.matmul(pM[:, j, :], eT[:, i % 2, j * P:j * P + P], wkv[:, :], start=True, stop=True)
                        else:
                            pe.wait_ge(tail_landed, b * 32 + 32)
                            pe.matmul(pM[:, 0, :], eTt[:, :], wkv[:, :], start=True, stop=True)
                            last = pe.matmul(pM[DROW:P, 0, :], eTt[:, DROW:P], wdca[:, :], start=True, stop=True, tile_position=(0, DROW))
                        last.then_inc(kv_psum, 1)

                    def transposed(i):
                        c = b * NC1 + i
                        n, src = (CH, kst[i % 2]) if i < NCH else (1, kst_tail)
                        pe.wait_ge(kst_ready, c + 1)
                        pe.wait_ge(k1_copied, 2 * c + 2)
                        pe.wait_ge(k2_copied, c + 1)
                        for hp in range(H // 2):
                            pe.wait_ge(kt_copied, c * (H // 2) + hp + 1)
                            for m in range(2):
                                for j in range(n):
                                    last = pe.transpose(pSb[hp % 2][0:KR, m * CH * P + j * P:m * CH * P + j * P + P],
                                                        src[:, j, 2 * hp + m, :], k.ident_bf[:, :])
                            last.then_inc(kt_psum, 1)

                    pe.wait_ge(q0_ready, b * NGR + NGR)
                    pe.wait_ge(x_added, b + 1)
                    projected(0)
                    for i in range(NC1):
                        if i < NCH:
                            projected(i + 1)
                        transposed(i)
                    pe.wait_ge(kt_copied, (b + 1) * (NC1 * H // 2) + 2)

                    def fill(g, f, half):
                        h, t = g * G + f // TB, f % TB
                        n = (b * NGR + g) * FILLS + f
                        pe.wait_ge((max_a_free, max_b_free)[half], n + 1)
                        for a in range(2):
                            lo = half * HALF + a * 512
                            w = min(512, (KT - 1) * P + DROW + DCA - lo)
                            last = pe.matmul(pM[:, 2 * half + a, 0:w], qT0[:, h, t * P:t * P + P], kT[0:ROWS, h, lo:lo + w],
                                             start=True, stop=True)
                        last.then_inc((max_a, max_b)[half], 1)

                    def shifted_queries(g):
                        pe.wait_ge(shift_ready, b * NGR + g + 1)
                        for i in range(G):
                            for t in range(TB):
                                last = pe.transpose(pTb[0:KR, i * S + t * P:i * S + t * P + P], qst[:, t, g * G + i, :], k.ident_bf[:, :])
                        last.then_inc(qs_psum, 1)

                    def scores(g, u):
                        n = b * (NGR * UNITS) + g * UNITS + u
                        kt = u // 2
                        if g * UNITS + u >= 2:
                            pe.wait_ge(probs_ready, n - 1)
                        for a in range(2):
                            i = 2 * (u % 2) + a
                            last = pe.matmul(pS[:, u % 2, a * S:(a + 1) * S], kT[:, g * G + i, kt * P:kt * P + P], qTs[:, g % 2, i, :],
                                             start=True, stop=True)
                        last.then_inc(scores_ready, 1)

                    def values(g, u):
                        n = b * (NGR * UNITS) + g * UNITS + u
                        kt = u // 2
                        pe.wait_ge(probs_ready, n + 1)
                        for a in range(2):
                            i = 2 * (u % 2) + a
                            pr = probs[:, (g * UNITS + u) % 3, a * S:(a + 1) * S]
                            last = pe.matmul(pY[PAD * i:PAD * i + PAD, 0:S], va[:, kt, g * G + i, :], pr,
                                             start=kt == 0, stop=kt == KT - 1, tile_position=(0, PAD * i))
                            if kt == KT - 1:
                                last = pe.matmul(pY[PAD * i:PAD * i + PAD, S:2 * S], va[:, KT, g * G + i, :], pr,
                                                 start=True, stop=True, tile_position=(0, PAD * i))
                        last.then_inc(pv_done, 1)

                    def outputs(g):
                        pe.wait_ge(y_copied, b * NGR + g + 2)
                        if g >= 1:
                            pe.wait_ge(y_free, b * NGR + g)
                        for m in range(2 * TB):
                            last = pe.transpose(pT[:, m * P:m * P + P], ysb[:, m * P:m * P + P], k.ident[:, :])
                        last.then_inc(y_tok, 1)

                    for f in range(FILLS):
                        fill(0, f, 0)
                        fill(0, f, 1)
                    shifted_queries(0)
                    for g in range(NGR):
                        pe.wait_ge(qs_ready, b * NGR + g + 1)
                        scores(g, 0)
                        pe.wait_ge(y_copied, b * NGR + g + 1)
                        for u in range(1, UNITS):
                            scores(g, u)
                            if g + 1 < NGR and u < 3 * FILLS + 1 and u % 3:
                                fill(g + 1, u // 3, u % 3 - 1)
                            values(g, u - 1)
                            if u == 2 and g >= 1:
                                outputs(g - 1)
                            if g == NGR - 1 and u == XT_AT:
                                x_columns(b + 1)
                            if g == NGR - 1 and u == XT_AT + 4:
                                queries(b + 1)
                        values(g, UNITS - 1)
                        if g + 1 < NGR:
                            if g >= 1:
                                pe.wait_ge(y_free, b * NGR + g)
                            shifted_queries(g + 1)
                    outputs(NGR - 1)
                    query_columns(b + 1)
                    pe.wait_ge(y_all, b + 1)
                    yf = y[:, :, :, :].rearrange("p t h d -> p t (h d)")
                    for t in range(TB):
                        for c2 in range(DC):
                            last = pe.transpose(pT[:, c2 * S + t * P:c2 * S + t * P + P], yf[:, t, c2 * P:c2 * P + P], k.ident[:, :])
                    last.then_inc(yT_psum, 1)
                    pe.wait_ge(yT_ready, b + 1)
                    for t in range(TB):
                        for c2 in range(DC):
                            last = pe.matmul(pM[:, 0, t * D:(t + 1) * D], yT[:, c2, t * P:t * P + P], wo[:, c2, :],
                                             start=c2 == 0, stop=c2 == DC - 1)
                    last.then_inc(o_psum, 1)


def experts(nc, k, gateT, w13T, w2T, s13T, s2T):
    E, TOP, CAP = 64, 6, 128
    I = w2T.shape[1]
    IB = I - P
    SI = s2T.shape[0]
    SC = (SI + P - 1) // P
    ROWS = E * CAP
    SPARE = P * TB * TOP
    ZR = 16
    xe = nc.dram_tensor("expert_in", (ROWS + SPARE, D), F32).ap()
    ye = nc.dram_tensor("expert_out", (ROWS + SPARE, D), F32).ap()

    with Scope(nc, "moe") as keep:
        slots, gates = keep.sb("slots", [P, NT, TOP], U32), keep.sb("gates", [P, NT, TOP])

        with Scope(nc, "route") as s:
            gate, s13, s2 = s.sb("gate", [P, DC, E]), s.sb("s13", [P, DC, 2 * SI]), s.sb("s2", [P, SC, D])
            zeros = s.sb("zeros", [P, ZR * D])
            stats, mv, ve, rstd = s.sb("stats", [P, TB, 6]), s.sb("mv", [P, TB, 2]), s.sb("ve", [P, TB]), s.sb("rstd", [P, TB])
            xn, xnT = s.sb("xn", [P, 2, TB, D]), s.sb("xnT", [P, DC, S])
            before = s.sb("before", [P, P])
            before_bf, ones_bf = s.sb("before_bf", [P, P], BF16), s.sb("ones_bf", [P, P], BF16)
            col_i, col = s.sb("col_i", [P, E], I32), s.sb("col", [P, E])
            spare_i, spare = s.sb("spare_i", [P, TB, TOP], I32), s.sb("spare", [P, TB, TOP])
            lg, top, topi, topf = s.sb("lg", [P, TB, E]), s.sb("top", [P, TB, 8]), s.sb("topi", [P, TB, 8], U32), s.sb("topf", [P, TB, 8])
            hot, picked = s.sb("hot", [P, TB, TOP, E]), s.sb("picked", [P, TB, TOP, E])
            chosen, chosen_bf, seen = s.sb("chosen", [P, TB, E]), s.sb("chosen_bf", [P, TB, E], BF16), s.sb("seen", [P, E], BF16)
            neg, ex, ex8, den, rden = s.sb("neg", [P, TB]), s.sb("ex", [P, TB, E]), s.sb("ex8", [P, TB, 8]), s.sb("den", [P, TB]), s.sb("rden", [P, TB])
            pos, kept, slotf = s.sb("pos", [P, TB, TOP]), s.sb("kept", [P, TB, TOP]), s.sb("slotf", [P, TB, TOP])
            slot_s = s.sb("slot_s", [P, 2, TB, TOP], U32)
            act1, hT = s.sb("act1", [P, SC, S]), s.sb("hT", [P, SC, S])
            pT, pL, pH, pZ = s.ps("pT", [P, 512]), s.ps("pL", [P, 512]), s.ps("pH", [P, SC, 2, S]), s.ps("pZ", [P, 512])
            (weights, prepared, cleared, xn_ready, xnT_psum, xnT_ready, l_psum, lg_ready, exp_ready,
             chosen_ready, pos_psum, slots_ready, scattered, h_psum, silu_ready, h_ready, z_psum, dve_chain, pool_chain) = s.sem(
                "weights", "prepared", "cleared", "xn_ready", "xnT_psum", "xnT_ready", "l_psum",
                "lg_ready", "exp_ready", "chosen_ready", "pos_psum", "slots_ready", "scattered", "h_psum", "silu_ready",
                "h_ready", "z_psum", "dve_chain", "pool_chain")
            rows_free, issuing = s.sem("rows_free", "issuing")
            hw = [min(P, SI - j * P) for j in range(SC)]
            with nc.Block() as block:

                @block.sync
                def _(sp):
                    sp.dma_start(gate[:, :, :], gateT.rearrange("(c p) n -> p c n", p=P)).then_inc(weights, 16)
                    sp.dma_start(s13[:, :, :], s13T.rearrange("(c p) n -> p c n", p=P)).then_inc(weights, 16)
                    for j in range(SC):
                        sp.dma_start(s2[0:hw[j], j, :], s2T[j * P:j * P + hw[j], :]).then_inc(weights, 16)
                    sp.wait_ge(prepared, 1)
                    for n in range(ROWS // (P * ZR)):
                        sp.dma_start(xe[n * P * ZR:(n + 1) * P * ZR, :].rearrange("(p r) d -> p (r d)", p=P), zeros[:, :]).then_inc(cleared, 16)
                    sp.dma_start(ye[ROWS:ROWS + SPARE, :].rearrange("(p r) d -> p (r d)", p=P), zeros[:, 0:SPARE // P * D]).then_inc(cleared, 16)
                    sp.wait_ge(cleared, 16 * (ROWS // (P * ZR) + 1))

                @block.gpsimd
                def _(pool):
                    chain = Chain(pool, pool_chain)
                    nc.gpsimd.memset(zeros[:, :], 0.0).then_inc(prepared, 1)
                    chain.link(nc.gpsimd.memset(before[:, :], 1.0))
                    nc.gpsimd.affine_select(out=before[:, :], in_=before[:, :], compare_op=ALU.is_gt, fill=0.0, base=0,
                                            pattern=[[1, P]], channel_multiplier=-1).then_inc(prepared, 1)
                    nc.gpsimd.iota(col_i[:, :], pattern=[[1, E]], base=0, channel_multiplier=0).then_inc(prepared, 1)
                    nc.gpsimd.iota(spare_i[:, :, :], pattern=[[P, TB * TOP]], base=ROWS, channel_multiplier=1).then_inc(prepared, 1)
                    pool.wait_ge(cleared, 16 * (ROWS // (P * ZR) + 1))
                    pool.sem_inc(rows_free, 2)
                    with pool.Fori(0, B // 2) as pair:
                        for a in range(2):
                            b = pair * 2 + a
                            pool.wait_ge(slots_ready, b + 1)
                            pool.sem_inc(issuing, 1)
                            for t in range(TB):
                                for n in range(TOP):
                                    pool.indirect_dma_start(out=xe[:, :], out_offset=bass.IndirectOffsetOnAxis(ap=slot_s[:, a, t, n:n + 1], axis=0),
                                                            in_=xn[:, a, t, :], in_offset=None).then_inc(scattered, 16)
                            pool.wait_ge(scattered, b * (16 * TB * TOP) + 16 * TB * TOP)
                            pool.sem_inc(rows_free, 1)
                    pool.wait_ge(scattered, 16 * TB * TOP * B)

                @block.vector
                def _(dve):
                    chain = Chain(dve, dve_chain)
                    dve.wait_ge(prepared, 4)
                    chain.link(nc.vector.tensor_copy(before_bf[:, :], before[:, :]))
                    chain.link(nc.vector.tensor_copy(ones_bf[:, :], k.ones[:, :]))
                    chain.link(nc.vector.tensor_copy(col[:, :], col_i[:, :]))
                    chain.link(nc.vector.tensor_copy(spare[:, :, :], spare_i[:, :, :]))
                    chain.link(nc.vector.memset(seen[:, :], 0.0))
                    nc.vector.tensor_copy(neg[:, 0:1], col[:, 0:1]).then_inc(chosen_ready, 1)
                    with dve.Fori(0, B // 2) as pair:
                        for a in range(2):
                            b = pair * 2 + a
                            chain.restart()
                            for t in range(TB):
                                chain.link(nc.vector.bn_stats(stats[:, t, :], k.x[:, b * TB + t, :]))
                            for t in range(TB):
                                chain.link(nc.vector.bn_aggr(mv[:, t, :], stats[:, t, :]))
                            chain.link(nc.vector.tensor_scalar(ve[:, :], mv[:, :, 1], LN_EPS, None, ALU.add))
                            rsqrt(nc, chain, rstd[:, :], ve[:, :], neg[:, :])
                            dve.wait_ge(rows_free, b + 1)
                            for t in range(TB):
                                nc.vector.tensor_scalar(xn[:, a, t, :], k.x[:, b * TB + t, :], mv[:, t, 0:1], rstd[:, t:t + 1],
                                                        ALU.subtract, ALU.mult).then_inc(xn_ready, 1)
                            dve.wait_ge(l_psum, b + 1)
                            chain.link(nc.vector.tensor_copy(lg[:, :, :], pL[:, 0:TB * E].rearrange("p (t e) -> p t e", t=TB)))
                            for t in range(TB):
                                chain.link(nc.vector.max(top[:, t, :], lg[:, t, :]))
                            for t in range(TB):
                                chain.link(nc.vector.max_index(topi[:, t, :], top[:, t, :], lg[:, t, :]))
                            nc.vector.tensor_scalar(neg[:, :], top[:, :, 0], -1.0, None, ALU.mult).then_inc(lg_ready, 1)
                            chain.link(nc.vector.tensor_copy(topf[:, :, :], topi[:, :, :]))
                            for t in range(TB):
                                chain.link(nc.vector.tensor_tensor(hot[:, t, :, :], col[:, :].unsqueeze(1).to_broadcast([P, TOP, E]),
                                                                   bcast(topf[:, t, 0:TOP], E), ALU.is_equal))
                                chain.link(nc.vector.tensor_reduce(chosen[:, t, :], hot[:, t, :, :].rearrange("p k e -> p e k"), AX.X, ALU.add))
                            nc.vector.tensor_copy(chosen_bf[:, :, :], chosen[:, :, :]).then_inc(chosen_ready, 1)
                            dve.wait_ge(pos_psum, b + 1)
                            pp = pL[:, 256:256 + TB * E].rearrange("p (t e) -> p t e", t=TB)
                            for t in range(TB):
                                chain.link(nc.vector.tensor_tensor(picked[:, t, :, :], hot[:, t, :, :],
                                                                   pp[:, t, :].unsqueeze(1).to_broadcast([P, TOP, E]), ALU.mult))
                                chain.link(nc.vector.tensor_tensor(seen[:, :], seen[:, :], chosen[:, t, :], ALU.add))
                            chain.link(nc.vector.tensor_reduce(pos[:, :, :].rearrange("p t k -> p (t k)"),
                                                               picked[:, :, :, :].rearrange("p t k e -> p (t k) e"), AX.X, ALU.add))
                            chain.link(nc.vector.tensor_scalar(kept[:, :, :], pos[:, :, :], float(CAP), None, ALU.is_lt))
                            for t in range(TB):
                                chain.link(nc.vector.scalar_tensor_tensor(out=slotf[:, t, :], in0=topf[:, t, 0:TOP], scalar=float(CAP), in1=spare[:, t, :], op0=ALU.mult, op1=ALU.subtract))
                            chain.link(nc.vector.tensor_tensor(slotf[:, :, :], slotf[:, :, :], pos[:, :, :], ALU.add))
                            chain.link(nc.vector.tensor_tensor(slotf[:, :, :], slotf[:, :, :], kept[:, :, :], ALU.mult))
                            chain.link(nc.vector.tensor_tensor(slot_s[:, a, :, :], slotf[:, :, :], spare[:, :, :], ALU.add))
                            nc.vector.tensor_copy(slots[:, ds(b * TB, TB), :], slot_s[:, a, :, :]).then_inc(slots_ready, 1)
                            dve.wait_ge(exp_ready, b + 1)
                            chain.link(nc.vector.reciprocal(rden[:, :], den[:, :]))
                            chain.link(nc.vector.tensor_tensor(kept[:, :, :], kept[:, :, :], bcast(rden[:, :], TOP), ALU.mult))
                            chain.link(nc.vector.tensor_tensor(gates[:, ds(b * TB, TB), :], kept[:, :, :], ex8[:, :, 0:TOP], ALU.mult))
                            for j in range(SC):
                                dve.wait_ge(silu_ready, b * SC + j + 1)
                                nc.vector.tensor_tensor(hT[0:hw[j], j, :], act1[0:hw[j], j, :], pH[0:hw[j], j, 1, :], ALU.mult).then_inc(h_ready, 1)
                            dve.wait_ge(z_psum, b + 1)
                            xb = k.x[:, ds(b * TB, TB), :]
                            chain.link(nc.vector.tensor_tensor(xb, xb, pZ[:, :].rearrange("p (t n) -> p t n", t=TB), ALU.add))

                @block.scalar
                def _(act):
                    with act.Fori(0, B // 2) as pair:
                        for a in range(2):
                            b = pair * 2 + a
                            act.wait_ge(xnT_psum, b + 1)
                            nc.scalar.activation(xnT[:, :, :], pT[:, :].rearrange("p (c n) -> p c n", c=DC), ACT.Copy).then_inc(xnT_ready, 1)
                            act.wait_ge(lg_ready, b + 1)
                            for t in range(TB):
                                nc.scalar.activation(ex[:, t, :], lg[:, t, :], ACT.Exp, bias=neg[:, t:t + 1], accum_out=den[:, t:t + 1])
                                last = nc.scalar.activation(ex8[:, t, :], top[:, t, :], ACT.Exp, bias=neg[:, t:t + 1])
                            last.then_inc(exp_ready, 1)
                            for j in range(SC):
                                act.wait_ge(h_psum, b * SC + j + 1)
                                nc.scalar.activation(act1[0:hw[j], j, :], pH[0:hw[j], j, 0, :], ACT.Silu).then_inc(silu_ready, 1)

                @block.tensor
                def _(pe):
                    pe.wait_ge(weights, 16 * (2 + SC))
                    with pe.Fori(0, B // 2) as pair:
                        for a in range(2):
                            b = pair * 2 + a
                            for t in range(TB):
                                pe.wait_ge(xn_ready, b * TB + t + 1)
                                for c in range(DC):
                                    last = pe.transpose(pT[:, c * S + t * P:c * S + t * P + P], xn[:, a, t, c * P:c * P + P], k.ident[:, :])
                            last.then_inc(xnT_psum, 1)
                            pe.wait_ge(xnT_ready, b + 1)
                            for t in range(TB):
                                for c in range(DC):
                                    last = pe.matmul(pL[:, t * E:(t + 1) * E], xnT[:, c, t * P:t * P + P], gate[:, c, :],
                                                     start=c == 0, stop=c == DC - 1)
                            last.then_inc(l_psum, 1)
                            def hidden(j):
                                for m in range(2):
                                    for c in range(DC):
                                        lo = m * SI + j * P
                                        last = pe.matmul(pH[0:hw[j], j, m, :], s13[:, c, lo:lo + hw[j]], xnT[:, c, :],
                                                         start=c == 0, stop=c == DC - 1)
                                last.then_inc(h_psum, 1)

                            hidden(0)
                            hidden(1)
                            pe.wait_ge(chosen_ready, b + 2)
                            for t in range(TB):
                                o = pL[:, 256 + t * E:256 + (t + 1) * E]
                                pe.matmul(o, before_bf[:, :], chosen_bf[:, t, :], start=True, stop=False)
                                if t == 1:
                                    pe.matmul(o, ones_bf[:, :], chosen_bf[:, 0, :], start=False, stop=False)
                                last = pe.matmul(o, ones_bf[:, :], seen[:, :], start=False, stop=True)
                            last.then_inc(pos_psum, 1)
                            for j in range(2, SC):
                                hidden(j)
                            for j in range(SC):
                                pe.wait_ge(h_ready, b * SC + j + 1)
                            for t in range(TB):
                                for j in range(SC):
                                    last = pe.matmul(pZ[:, t * D:(t + 1) * D], hT[0:hw[j], j, t * P:t * P + P], s2[0:hw[j], j, :],
                                                     start=j == 0, stop=j == SC - 1)
                            last.then_inc(z_psum, 1)

        with Scope(nc, "exp") as s:
            NB = 4
            wa, wb, wc = s.sb("wa", [P, NB, DC, 2 * I]), s.sb("wb", [P, NB, D]), s.sb("wc", [IB, NB, D])
            xs, xT = s.sb("xs", [P, NB, D]), s.sb("xT", [P, 2, DC, CAP])
            sa, sbb = s.sb("sa", [P, 2, CAP]), s.sb("sb", [IB, 2, CAP])
            ha, hb = s.sb("ha", [P, 2, CAP]), s.sb("hb", [IB, 2, CAP])
            yo = s.sb("yo", [P, NB, D])
            pT, pH, pO = s.ps("pT", [P, 2, 512]), s.ps("pH", [P, 2, 512]), s.ps("pO", [P, 2, 512])
            xs_landed, wa_landed, wb_landed, stored = (s.sem(*(f"{what}{u}" for u in range(NB))) for what in
                                                       ("xs_landed", "wa_landed", "wb_landed", "stored"))
            (xT_psum, xT_ready, h_psum, silu_ready, h_ready, o_psum, yo_ready) = s.sem(
                "xT_psum", "xT_ready", "h_psum", "silu_ready", "h_ready", "o_psum", "yo_ready")
            with nc.Block() as block:

                @block.sync
                def _(sp):
                    def load_x(e, u):
                        sp.dma_start(xs[:, u, :], xe[ds(e * CAP, CAP), :]).then_inc(xs_landed[u], 16)

                    def load_up(e, u):
                        sp.dma_start(wa[:, u, :, :], w13T[e].rearrange("(c p) n -> p c n", p=P)).then_inc(wa_landed[u], 16)

                    def load_down(e, u):
                        sp.dma_start(wb[:, u, :], w2T[e, 0:P, :]).then_inc(wb_landed[u], 16)
                        sp.dma_start(wc[:, u, :], w2T[e, P:I, :]).then_inc(wb_landed[u], 16)

                    def store(e, u):
                        sp.wait_ge(yo_ready, e + 3)
                        sp.dma_start(ye[ds(e * CAP, CAP), :], yo[:, u, :]).then_inc(stored[u], 16)

                    for u in range(NB):
                        load_x(u, u)
                        load_up(u, u)
                        load_down(u, u)
                    with sp.Fori(0, E // NB - 1) as i:
                        for u in range(NB):
                            e = NB * i + u
                            sp.wait_ge(xT_psum, e + 1)
                            load_x(e + NB, u)
                            sp.wait_ge(h_psum, e + 1)
                            load_up(e + NB, u)
                            sp.wait_ge(o_psum, e + 1)
                            load_down(e + NB, u)
                            store(e, u)
                    for u in range(NB):
                        store(E - NB + u, u)
                    for u in range(NB):
                        sp.wait_ge(stored[u], 16 * (E // NB))

                @block.tensor
                def _(pe):
                    def turn(i, v):
                        i, u, a = i + v // NB, v % NB, v % 2
                        pe.wait_ge(xs_landed[u], i * 16 + 16)
                        for c in range(DC):
                            last = pe.transpose(pT[:, a, c * P:c * P + P], xs[:, u, c * P:c * P + P], k.ident[:, :])
                        last.then_inc(xT_psum, 1)

                    def hidden(i, v):
                        i, u, a = i + v // NB, v % NB, v % 2
                        pe.wait_ge(wa_landed[u], i * 16 + 16)
                        pe.wait_ge(xT_ready, NB * i + u + 1)
                        for m in range(2):
                            for j, w in ((0, P), (1, IB)):
                                for c in range(DC):
                                    lo = m * I + j * P
                                    last = pe.matmul(pH[0:w, a, (2 * m + j) * CAP:(2 * m + j + 1) * CAP], wa[:, u, c, lo:lo + w],
                                                     xT[:, a, c, :], start=c == 0, stop=c == DC - 1)
                        last.then_inc(h_psum, 1)

                    def down(i, v):
                        i, u, a = i + v // NB, v % NB, v % 2
                        pe.wait_ge(wb_landed[u], i * 32 + 32)
                        pe.wait_ge(h_ready, NB * i + u + 1)
                        pe.wait_ge(yo_ready, NB * i + u + 1)
                        pe.matmul(pO[:, a, 0:D], ha[:, a, :], wb[:, u, :], start=True, stop=False)
                        pe.matmul(pO[:, a, 0:D], hb[:, a, :], wc[:, u, :], start=False, stop=True).then_inc(o_psum, 1)

                    turn(0, 0)
                    turn(0, 1)
                    hidden(0, 0)
                    with pe.Fori(0, E // NB - 1) as i:
                        for u in range(NB):
                            turn(i, u + 2)
                            hidden(i, u + 1)
                            down(i, u)
                    last_i = E // NB - 1
                    for u in range(NB):
                        if u + 2 < NB:
                            turn(last_i, u + 2)
                        if u + 1 < NB:
                            hidden(last_i, u + 1)
                        down(last_i, u)

                @block.scalar
                def _(act):
                    act.sem_inc(yo_ready, 2)
                    with act.Fori(0, E // 2) as i:
                        for u in range(2):
                            e = 2 * i + u
                            act.wait_ge(xT_psum, e + 1)
                            nc.scalar.activation(xT[:, u, :, :], pT[:, u, 0:D].rearrange("p (c n) -> p c n", c=DC), ACT.Copy).then_inc(xT_ready, 1)
                            act.wait_ge(h_psum, e + 1)
                            nc.scalar.activation(sa[:, u, :], pH[:, u, 0:CAP], ACT.Silu)
                            nc.scalar.activation(sbb[:, u, :], pH[0:IB, u, CAP:2 * CAP], ACT.Silu).then_inc(silu_ready, 1)

                @block.vector
                def _(dve):
                    def product(e, u):
                        dve.wait_ge(silu_ready, e + 1)
                        nc.vector.tensor_tensor(ha[:, u, :], sa[:, u, :], pH[:, u, 2 * CAP:3 * CAP], ALU.mult)
                        nc.vector.tensor_tensor(hb[:, u, :], sbb[:, u, :], pH[0:IB, u, 3 * CAP:4 * CAP], ALU.mult).then_inc(h_ready, 1)

                    def evacuate(i, u, first=False):
                        dve.wait_ge(o_psum, NB * i + u + 1)
                        if not first:
                            dve.wait_ge(stored[u], i * 16)
                        nc.vector.tensor_copy(yo[:, u, :], pO[:, u % 2, 0:D]).then_inc(yo_ready, 1)

                    product(0, 0)
                    for u in range(NB):
                        product(u + 1, (u + 1) % 2)
                        evacuate(0, u, first=True)
                    with dve.Fori(1, E // NB - 1) as i:
                        for u in range(NB):
                            product(NB * i + u + 1, (u + 1) % 2)
                            evacuate(i, u)
                    for u in range(NB):
                        if u + 1 < NB:
                            product(E - NB + u + 1, (u + 1) % 2)
                        evacuate(E // NB - 1, u)

        with Scope(nc, "comb") as s:
            rows, sl, gt = s.sb("rows", [P, TB, TOP, D]), s.sb("sl", [P, TB, TOP], U32), s.sb("gt", [P, TB, TOP])
            sl_ready, issuing, dve_chain = s.sem("sl_ready", "issuing", "dve_chain")
            gathered = s.sem("gathered0", "gathered1")
            with nc.Block() as block:

                @block.gpsimd
                def _(pool):
                    with pool.Fori(0, B) as b:
                        for t in range(TB):
                            pool.wait_ge(sl_ready, b * TB + t + 1)
                            pool.sem_inc(issuing, 1)
                            for n in range(TOP):
                                pool.indirect_dma_start(out=rows[:, t, n, :], out_offset=None, in_=ye[:, :],
                                                        in_offset=bass.IndirectOffsetOnAxis(ap=sl[:, t, n:n + 1], axis=0)).then_inc(gathered[t], 16)

                @block.vector
                def _(dve):
                    chain = Chain(dve, dve_chain)

                    def ask(i, t):
                        chain.link(nc.vector.tensor_copy(gt[:, t, :], gates[:, i, :]))
                        nc.vector.tensor_copy(sl[:, t, :], slots[:, i, :]).then_inc(sl_ready, 1)

                    def add(b, t):
                        dve.wait_ge(gathered[t], b * (16 * TOP) + 16 * TOP)
                        i = b * TB + t
                        for n in range(TOP):
                            xt = k.x[:, i, :]
                            chain.link(nc.vector.scalar_tensor_tensor(out=xt, in0=rows[:, t, n, :], scalar=gt[:, t, n:n + 1],
                                                                      in1=xt, op0=ALU.mult, op1=ALU.add))

                    for t in range(TB):
                        ask(t, t)
                    with dve.Fori(0, B - 1) as b:
                        chain.restart()
                        for t in range(TB):
                            add(b, t)
                            ask(b * TB + TB + t, t)
                    chain.restart()
                    for t in range(TB):
                        add(B - 1, t)


def bit_mlp(nc, k, wgT, gg, wdT, gd):
    I = wdT.shape[0]
    N = 2 * I
    IC = (I + P - 1) // P
    iw = [min(P, I - j * P) for j in range(IC)]
    MAGIC = 12582912.0
    RMS_EPS, Q_EPS = 1e-6, 1e-5

    with Scope(nc, "bit") as s:
        wg, wd = s.sb("wg", [P, DC, N]), s.sb("wd", [P, IC, D])
        wgq, wdq = s.sb("wgq", [P, DC, N], BF16), s.sb("wdq", [P, IC, D], BF16)
        g1, g2 = s.sb("g1", [P, D]), s.sb("g2", [P, I])
        wsum, mean, scale = s.sb("wsum", [P, 2]), s.sb("mean", [P, 2]), s.sb("scale", [P, 2])
        stats, mv = s.sb("stats", [P, NT, 6]), s.sb("mv", [P, NT, 2])
        ve, rstd, c, room = s.sb("ve", [P, NT]), s.sb("rstd", [P, NT]), s.sb("c", [P, NT]), s.sb("room", [P, NT])
        xg, am, inv, dq = s.sb("xg", [P, D]), s.sb("am", [P, 1]), s.sb("inv", [P, 1]), s.sb("dq", [P, 2])
        xq, xqT = s.sb("xq", [P, 2, D], BF16), s.sb("xqT", [P, 2, DC, P], BF16)
        sg, h, hsq, hg = s.sb("sg", [P, 2, I]), s.sb("h", [P, 2, I]), s.sb("hsq", [P, I]), s.sb("hg", [P, I])
        ss, ms2, rs2, am2, inv2, dq2 = (s.sb(n, [P, 2]) for n in ("ss", "ms2", "rs2", "am2", "inv2", "dq2"))
        hq, hqT = s.sb("hq", [P, 2, I], BF16), s.sb("hqT", [P, 2, IC, P], BF16)
        pY = s.ps("pY", [P, 3, 512])
        pX, pH, pZ = s.ps("pX", [P, 512]), s.ps("pH", [P, 512]), s.ps("pZ", [P, 2, 512])
        (weights, wsum_ready, wsum_psum, wq_ready, xq_ready, xqT_psum, xqT_ready, y_psum,
         silu_ready, h_ready, ss_ready, ms2_ready, rs2_ready, hq_ready, hqT_psum, hqT_ready, z_psum, stats_ready, dve_chain) = s.sem(
            "weights", "wsum_ready", "wsum_psum", "wq_ready", "xq_ready", "xqT_psum", "xqT_ready", "y_psum",
            "silu_ready", "h_ready", "ss_ready", "ms2_ready", "rs2_ready", "hq_ready", "hqT_psum", "hqT_ready", "z_psum", "stats_ready", "dve_chain")
        pYf = pY[:, :, :].rearrange("p a n -> p (a n)")
        pXb, pHb = pX[:, :].bitcast(BF16), pH[:, :].bitcast(BF16)

        def tiles(eng, step):
            step(0, 0)
            step(1, 1)
            with eng.Fori(1, NT // 2 - 1) as j:
                step(j * 2, 0)
                step(j * 2 + 1, 1)
            step(NT - 2, 0)
            step(NT - 1, 1)

        def first(n, m):
            return isinstance(n, int) and n < m

        def final(n, m):
            return isinstance(n, int) and n >= NT - m

        with nc.Block() as block:

            @block.sync
            def _(sp):
                sp.dma_start(wg[:, :, :], wgT.rearrange("(c p) n -> p c n", p=P)).then_inc(weights, 16)
                for j in range(IC):
                    sp.dma_start(wd[0:iw[j], j, :], wdT[j * P:j * P + iw[j], :]).then_inc(weights, 16)
                sp.dma_start(g1[:, :], gg.rearrange("(a n) -> a n", a=1).to_broadcast([P, D])).then_inc(weights, 16)
                sp.dma_start(g2[:, :], gd.rearrange("(a n) -> a n", a=1).to_broadcast([P, I])).then_inc(weights, 16)

            @block.gpsimd
            def _(pool):
                def step(n, a):
                    pool.wait_ge(ms2_ready, n + 1)
                    nc.gpsimd.tensor_tensor(rs2[:, a:a + 1], ms2[:, a:a + 1], k.minus_half[:, 0:1], ALU.pow).then_inc(rs2_ready, 1)

                tiles(pool, step)

            @block.vector
            def _(dve):
                chain = Chain(dve, dve_chain)
                dve.wait_ge(weights, 16 * (3 + IC))
                last_rows = iw[IC - 1]
                chain.link(nc.vector.memset(wd[last_rows:P, IC - 1, :], 0.0))
                for m, w in ((0, wg), (1, wd)):
                    chain.link(nc.vector.tensor_reduce(wsum[:, m:m + 1], w[:, :, :], AX.XY, ALU.add, apply_absolute_value=True))
                nc.vector.tensor_scalar(wsum[:, :], wsum[:, :], 1.0, None, ALU.mult).then_inc(wsum_ready, 1)
                dve.wait_ge(wsum_psum, 1)
                for m, n in ((0, D * N), (1, D * I)):
                    chain.link(nc.vector.tensor_scalar(mean[:, m:m + 1], pZ[:, 1, m:m + 1], 1.0 / n, Q_EPS, ALU.mult, ALU.max))
                chain.link(nc.vector.reciprocal(scale[:, :], mean[:, :]))
                for m, (w, wq) in enumerate(((wg, wgq), (wd, wdq))):
                    chain.link(nc.vector.tensor_scalar(w[:, :, :], w[:, :, :], scale[:, m:m + 1], MAGIC, ALU.mult, ALU.add))
                    chain.link(nc.vector.tensor_scalar(w[:, :, :], w[:, :, :], MAGIC, 1.0, ALU.subtract, ALU.min))
                    last = nc.vector.tensor_scalar(wq[:, :, :], w[:, :, :], -1.0, None, ALU.max)
                    chain.link(last)
                nc.vector.tensor_copy(wsum[:, 0:1], scale[:, 0:1]).then_inc(wq_ready, 1)

                for i in range(NT):
                    nc.vector.bn_stats(stats[:, i, :], k.x[:, i, :]).then_inc(stats_ready, 1)
                for i in range(NT):
                    dve.wait_ge(stats_ready, i + 1)
                    nc.vector.bn_aggr(mv[:, i, :], stats[:, i, :]).then_inc(stats_ready, 1)
                dve.wait_ge(stats_ready, 2 * NT)
                chain.link(nc.vector.tensor_scalar(ve[:, :], mv[:, :, 1], LN_EPS, None, ALU.add))
                rsqrt(nc, chain, rstd[:, :], ve[:, :], room[:, :])
                chain.link(nc.vector.tensor_tensor(ve[:, :], rstd[:, :], rstd[:, :], ALU.mult))
                chain.link(nc.vector.tensor_tensor(ve[:, :], ve[:, :], mv[:, :, 1], ALU.mult))
                chain.link(nc.vector.tensor_scalar(ve[:, :], ve[:, :], RMS_EPS, None, ALU.add))
                rsqrt(nc, chain, c[:, :], ve[:, :], room[:, :])
                chain.link(nc.vector.tensor_tensor(c[:, :], c[:, :], rstd[:, :], ALU.mult))

                def quantise(out, z, factor, a, ainv, adq, m):
                    chain.link(nc.vector.tensor_scalar(a, a, factor, Q_EPS, ALU.mult, ALU.max))
                    chain.link(nc.vector.reciprocal(ainv, a))
                    chain.link(nc.vector.tensor_scalar(ainv, ainv, factor, 127.0, ALU.mult, ALU.mult))
                    nc.vector.tensor_scalar(adq, a, mean[:, m:m + 1], 1.0 / 127.0, ALU.mult, ALU.mult)
                    chain.link(nc.vector.tensor_scalar(z, z, ainv, MAGIC, ALU.mult, ALU.add))
                    chain.link(nc.vector.tensor_scalar(z, z, MAGIC, 127.0, ALU.subtract, ALU.min))
                    return nc.vector.tensor_scalar(out, z, -128.0, None, ALU.max)

                def rows(n, a):
                    cn = c[:, n:n + 1] if isinstance(n, int) else c[:, ds(n, 1)]
                    chain.link(nc.vector.scalar_tensor_tensor(out=xg[:, :], in0=k.x[:, n, :], scalar=mv[:, n, 0:1], in1=g1[:, :],
                                                              op0=ALU.subtract, op1=ALU.mult))
                    chain.link(nc.vector.tensor_reduce(am[:, :], xg[:, :], AX.X, ALU.max, apply_absolute_value=True))
                    quantise(xq[:, a, :], xg[:, :], cn, am[:, :], inv[:, :], dq[:, a:a + 1], 0).then_inc(xq_ready, 1)
                    dve.wait_ge(xq_ready, n + 1)

                def add(n, a):
                    dve.wait_ge(z_psum, n + 1)
                    xt = k.x[:, n, :]
                    chain.link(nc.vector.scalar_tensor_tensor(out=xt, in0=pZ[:, a, 0:D], scalar=dq2[:, a:a + 1], in1=xt,
                                                              op0=ALU.mult, op1=ALU.add))

                rows(0, 0)
                rows(1, 1)

                def step(n, a):
                    dve.wait_ge(silu_ready, n + 1)
                    nc.vector.scalar_tensor_tensor(out=h[:, a, :], in0=pYf[:, I:N], scalar=dq[:, a:a + 1], in1=sg[:, a, :],
                                                   op0=ALU.mult, op1=ALU.mult).then_inc(h_ready, 1)
                    chain.restart()
                    dve.wait_ge(h_ready, n + 1)
                    chain.link(nc.vector.tensor_tensor(hg[:, :], h[:, a, :], g2[:, :], ALU.mult))
                    dve.wait_ge(ss_ready, n + 1)
                    nc.vector.tensor_scalar(ms2[:, a:a + 1], ss[:, a:a + 1], 1.0 / I, RMS_EPS, ALU.mult, ALU.add).then_inc(ms2_ready, 1)
                    chain.link(nc.vector.tensor_reduce(am2[:, a:a + 1], hg[:, :], AX.X, ALU.max, apply_absolute_value=True))
                    if not first(n, 1):
                        add(n - 1, 1 - a)
                    if not final(n, 2):
                        rows(n + 2, a)
                    dve.wait_ge(rs2_ready, n + 1)
                    quantise(hq[:, a, :], hg[:, :], rs2[:, a:a + 1], am2[:, a:a + 1], inv2[:, a:a + 1], dq2[:, a:a + 1], 1).then_inc(hq_ready, 1)
                    dve.wait_ge(hq_ready, n + 1)

                tiles(dve, step)
                add(NT - 1, 1)

            @block.scalar
            def _(act):
                def rows_T(n, a):
                    act.wait_ge(xqT_psum, n + 1)
                    nc.scalar.activation(xqT[:, a, :, :], pXb[:, 0:D].rearrange("p (c n) -> p c n", c=DC), ACT.Copy).then_inc(xqT_ready, 1)

                def silu(n, a):
                    act.wait_ge(y_psum, n + 1)
                    nc.scalar.activation(sg[:, a, :], pYf[:, 0:I], ACT.Silu, scale=dq[:, a:a + 1]).then_inc(silu_ready, 1)

                rows_T(0, 0)
                rows_T(1, 1)
                silu(0, 0)

                def step(n, a):
                    act.wait_ge(h_ready, n + 1)
                    nc.scalar.activation(hsq[:, :], h[:, a, :], ACT.Square, accum_out=ss[:, a:a + 1]).then_inc(ss_ready, 1)
                    if not final(n, 1):
                        silu(n + 1, 1 - a)
                    if not final(n, 2):
                        rows_T(n + 2, a)
                    act.wait_ge(hqT_psum, n + 1)
                    nc.scalar.activation(hqT[:, a, 0:IC - 1, :], pHb[:, 0:(IC - 1) * P].rearrange("p (c n) -> p c n", c=IC - 1), ACT.Copy)
                    nc.scalar.activation(hqT[0:iw[-1], a, IC - 1, :], pHb[0:iw[-1], (IC - 1) * P:IC * P], ACT.Copy).then_inc(hqT_ready, 1)

                tiles(act, step)

            @block.tensor
            def _(pe):
                pe.wait_ge(wsum_ready, 1)
                pe.matmul(pZ[:, 1, 0:2], k.ones[:, :], wsum[:, :], start=True, stop=True).then_inc(wsum_psum, 1)
                pe.wait_ge(wq_ready, 1)

                def rows_T(n, a):
                    pe.wait_ge(xq_ready, n + 1)
                    if not first(n, 1):
                        pe.wait_ge(xqT_ready, n)
                    for c_ in range(DC):
                        ins = pe.transpose(pXb[:, c_ * P:c_ * P + P], xq[:, a, c_ * P:c_ * P + P], k.ident_bf[:, :])
                    ins.then_inc(xqT_psum, 1)

                def up(n, a):
                    pe.wait_ge(xqT_ready, n + 1)
                    if not first(n, 1):
                        pe.wait_ge(h_ready, n)
                    for lo in range(0, N, 512):
                        w = min(512, N - lo)
                        for c_ in range(DC):
                            ins = pe.matmul(pYf[:, lo:lo + w], xqT[:, a, c_, :], wgq[:, c_, lo:lo + w], start=c_ == 0, stop=c_ == DC - 1)
                    ins.then_inc(y_psum, 1)

                rows_T(0, 0)
                rows_T(1, 1)
                up(0, 0)

                def step(n, a):
                    if not final(n, 1):
                        up(n + 1, 1 - a)
                    if not final(n, 2):
                        rows_T(n + 2, a)
                    pe.wait_ge(hq_ready, n + 1)
                    for j in range(IC):
                        ins = pe.transpose(pHb[0:iw[j], j * P:j * P + P], hq[:, a, j * P:j * P + iw[j]], k.ident_bf[:, :])
                    ins.then_inc(hqT_psum, 1)
                    pe.wait_ge(hqT_ready, n + 1)
                    for j in range(IC):
                        ins = pe.matmul(pZ[:, a, 0:D], hqT[0:iw[j], a, j, :], wdq[0:iw[j], j, :], start=j == 0, stop=j == IC - 1)
                    ins.then_inc(z_psum, 1)

                tiles(pe, step)


def cross_attention_1(nc, k, ctx_rows, ctx_tail, ctxT, wqd, wkd, wkTd, wvTd, wod, gqd, gkd):
    H, HD = 16, 128
    SK = ctxT.shape[2]
    KT = (SK + P - 1) // P
    TAIL = SK - (KT - 1) * P
    C = 512
    CG = H * HD // C
    HC = C // HD
    QU, KU = TB * CG, KT * CG
    UN = QU + KU
    SU = (KT + 1) // 2
    NB = 4
    EPS = 1e-5
    NEG = -1e30
    SPLIT = 7

    with Scope(nc, "xb") as s:
        wq, wk, wkT = s.sb("wq", [P, DC, H * HD]), s.sb("wk", [P, H * HD]), s.sb("wkT", [P, H, HD])
        wvT, wo, vo = s.sb("wvT", [P, H, P]), s.sb("wo", [P, H, D]), s.sb("vo", [P, H, D])
        gq, gk, gg, dead = s.sb("gq", [P, 1]), s.sb("gk", [P, 1]), s.sb("gg", [P, 1]), s.sb("dead", [P, 1])
        stats, mv, ve, rstd = s.sb("stats", [P, TB, 6]), s.sb("mv", [P, TB, 2]), s.sb("ve", [P, TB]), s.sb("rstd", [P, TB])
        xn, xnT = s.sb("xn", [P, TB, D]), s.sb("xnT", [P, DC, S])
        eT, eK = s.sb("eT", [P, KT * P]), s.sb("eK", [P, KT, P])
        q, sq = s.sb("q", [P, TB, H * HD]), s.sb("sq", [P, NB, C])
        qss, rq, kss, rk = s.sb("qss", [P, TB, H]), s.sb("rq", [P, TB, H]), s.sb("kss", [P, KT, H]), s.sb("rk", [P, KT, H])
        qn, wk_h = s.sb("qn", [P, 2, TB, HD]), s.sb("wk_h", [P, 2, HD])
        qT, qe = s.sb("qT", [P, S]), s.sb("qe", [P, 2, S])
        sc = s.sb("sc", [P, 2, KT + 1, S])
        mx, mcol, mdiag = s.sb("mx", [P, S]), s.sb("mcol", [P, TB]), s.sb("mdiag", [P, TB, P])
        rden, room = s.sb("rden", [P, TB]), s.sb("room", [P, KT, H])
        den, pe_n = s.sb("den", [P, S]), s.sb("pe_n", [P, S])
        pS = s.ps("pS", [P, NB, C])
        pQ, pV, pM, pO = s.ps("pQ", [P, 2, S]), s.ps("pV", [P, S]), s.ps("pM", [P, 2, S]), s.ps("pO", [P, TB, D])

        (weights, prepared, eT_landed, eK_landed, vo_psum, vo_ready, ve_ready, rstd_ready, xn_ready, xnT_psum, xnT_ready,
         unit_psum, unit_sq, unit_red, rk_ready, qn_ready, wk_ready, qT_psum, qT_ready,
         qe_psum, qe_ready, s_psum, s_copied, max_ready, maxT_psum, mdiag_ready, shift_psum, sub_ready, probs_ready,
         sum_ready, pv_done, den_psum, pe_ready, out_psum, out_added, dve_chain, pool_chain) = s.sem(
            "weights", "prepared", "eT_landed", "eK_landed", "vo_psum", "vo_ready", "ve_ready", "rstd_ready", "xn_ready",
            "xnT_psum", "xnT_ready", "unit_psum", "unit_sq", "unit_red", "rk_ready",
            "qn_ready", "wk_ready", "qT_psum", "qT_ready", "qe_psum", "qe_ready", "s_psum", "s_copied", "max_ready",
            "maxT_psum", "mdiag_ready", "shift_psum", "sub_ready", "probs_ready", "sum_ready", "pv_done", "den_psum",
            "pe_ready", "out_psum", "out_added", "dve_chain", "pool_chain")

        def heads(eng, step):
            step(0, 0)
            with eng.Fori(0, (H - 4) // 2) as j:
                step(2 * j + 1, 1)
                step(2 * j + 2, 0)
            for h in range(H - 3, H):
                step(h, h % 2)

        def last_heads(h, n):
            return isinstance(h, int) and h >= H - n

        def first(h):
            return isinstance(h, int) and h == 0

        with nc.Block() as block:

            @block.sync
            def _(sp):
                for dst, src in ((wq[:, :, :], wqd.rearrange("(c p) n -> p c n", p=P)), (wk[:, :], wkd),
                                 (wkT[:, :, :].rearrange("p h n -> p (h n)"), wkTd),
                                 (wvT[:, :, :].rearrange("p h n -> p (h n)"), wvTd),
                                 (wo[:, :, :], wod.rearrange("(h p) n -> p h n", p=P)),
                                 (gq[:, :], gqd.rearrange("(p a) -> p a", a=1)), (gk[:, :], gkd.rearrange("(p a) -> p a", a=1))):
                    sp.dma_start(dst, src).then_inc(weights, 16)
                sp.wait_ge(prepared, 3)

                def load_eT(b):
                    sp.dma_start(eT[:, 0:SK], ctxT[b, :, :]).then_inc(eT_landed, 16)

                def load_eK(b):
                    sp.dma_start(eK[:, 0:KT - 1, :].rearrange("p t c -> p (t c)"), ctx_rows[b, :, :]).then_inc(eK_landed, 16)
                    sp.dma_start(eK[0:TAIL, KT - 1, :], ctx_tail[b, :, :]).then_inc(eK_landed, 16)

                load_eT(0)
                load_eK(0)
                with sp.Fori(1, B) as b:
                    sp.wait_ge(s_psum, b * (H * SU))
                    load_eT(b)
                    sp.wait_ge(pv_done, b * H)
                    load_eK(b)

            @block.gpsimd
            def _(pool):
                chain = Chain(pool, pool_chain)
                nc.gpsimd.memset(eT[:, :], 0.0).then_inc(prepared, 1)
                nc.gpsimd.memset(eK[:, :, :], 0.0).then_inc(prepared, 1)
                chain.link(nc.gpsimd.memset(dead[:, :], 0.0))
                nc.gpsimd.affine_select(out=dead[:, :], in_=dead[:, :], compare_op=ALU.is_gt, fill=NEG,
                                        base=TAIL, pattern=[[0, 1]], channel_multiplier=-1).then_inc(prepared, 1)
                pool.wait_ge(weights, 16 * 7)
                with pool.Fori(0, B) as b:
                    pool.wait_ge(ve_ready, b + 1)
                    nc.gpsimd.tensor_tensor(rstd[:, :], ve[:, :], k.minus_half[:, 0:TB], ALU.pow).then_inc(rstd_ready, 1)

                    def head_weight(h, par):
                        nc.gpsimd.tensor_tensor(wk_h[:, par, :], wkT[:, h, :], k.ones[:, 0:HD], ALU.mult).then_inc(wk_ready, 1)

                    head_weight(0, 0)
                    head_weight(1, 1)

                    def step(h, par):
                        if not last_heads(h, 2):
                            pool.wait_ge(qe_psum, b * H + h + 1)
                            head_weight(h + 2, par)

                    heads(pool, step)

            @block.vector
            def _(dve):
                chain = Chain(dve, dve_chain)
                dve.wait_ge(weights, 16 * 7)
                chain.link(nc.vector.tensor_tensor(gg[:, :], gq[:, :], gk[:, :], ALU.mult))
                for i in range(0, H, 2):
                    dve.wait_ge(vo_psum, i // 2 + 1)
                    nc.vector.tensor_copy(vo[:, i:i + 2, :], pS[:, i // 2 % NB, :].rearrange("p (a n) -> p a n", a=2)).then_inc(vo_ready, 1)
                with dve.Fori(0, B) as b:
                    chain.restart()
                    for t in range(TB):
                        chain.link(nc.vector.bn_stats(stats[:, t, :], k.x[:, b * TB + t, :]))
                    for t in range(TB):
                        chain.link(nc.vector.bn_aggr(mv[:, t, :], stats[:, t, :]))
                    nc.vector.tensor_scalar(ve[:, :], mv[:, :, 1], LN_EPS, None, ALU.add).then_inc(ve_ready, 1)
                    dve.wait_ge(rstd_ready, b + 1)
                    for t in range(TB):
                        nc.vector.tensor_scalar(xn[:, t, :], k.x[:, b * TB + t, :], mv[:, t, 0:1], rstd[:, t:t + 1],
                                                ALU.subtract, ALU.mult).then_inc(xn_ready, 1)

                    for u in range(QU):
                        dve.wait_ge(unit_sq, b * UN + u + 1)
                        t, g = u // CG, u % CG
                        nc.vector.tensor_reduce(qss[:, t, g * HC:(g + 1) * HC], sq[:, u % NB, :].rearrange("p (h d) -> p h d", d=HD),
                                                AX.X, ALU.add).then_inc(unit_red, 1)
                    dve.wait_ge(unit_red, b * UN + QU)
                    chain.link(nc.vector.tensor_scalar(qss[:, :, :], qss[:, :, :], 1.0 / HD, EPS, ALU.mult, ALU.add))
                    rsqrt(nc, chain, rq[:, :, :], qss[:, :, :], room[:, 0:TB, :])
                    with dve.Fori(0, KT) as t:
                        for g in range(CG):
                            dve.wait_ge(unit_sq, b * UN + t * CG + (QU + g + 1))
                            nc.vector.tensor_reduce(kss[:, t, g * HC:(g + 1) * HC], sq[:, g % NB, :].rearrange("p (h d) -> p h d", d=HD),
                                                    AX.X, ALU.add).then_inc(unit_red, 1)
                    dve.wait_ge(unit_red, b * UN + UN)
                    chain.link(nc.vector.tensor_scalar(kss[:, :, :], kss[:, :, :], HD * EPS, None, ALU.add))
                    rsqrt(nc, chain, rk[:, :, :], kss[:, :, :], room[:, :, :])
                    dve.sem_inc(rk_ready, 1)

                    def query(h, par):
                        for t in range(TB):
                            last = nc.vector.tensor_scalar(qn[:, par, t, :], q[:, t, ds(h * HD, HD)], rq[:, t, ds(h, 1)], None, ALU.mult)
                        last.then_inc(qn_ready, 1)

                    def maximum_first(n, par):
                        dve.wait_ge(s_copied, n * KT + SPLIT)
                        chain.link(nc.vector.tensor_reduce(sc[:, par, KT, :], sc[:, par, 0:SPLIT, :].rearrange("p t q -> p q t"), AX.X, ALU.max))

                    def maximum(n, par):
                        dve.wait_ge(s_copied, n * KT + KT)
                        nc.vector.tensor_reduce(mx[:, :], sc[:, par, SPLIT:KT + 1, :].rearrange("p t q -> p q t"), AX.X, ALU.max).then_inc(max_ready, 1)

                    def shift(n):
                        dve.wait_ge(maxT_psum, n + 1)
                        ins = nc.vector.tensor_reduce(mcol[:, :], pM[:, 0, :].rearrange("p (t k) -> p t k", t=TB), AX.X, ALU.max)
                        chain.link(ins)
                        nc.vector.tensor_tensor(mdiag[:, :, :], k.ident[:, :].unsqueeze(1).to_broadcast([P, TB, P]), bcast(mcol[:, :], P),
                                                ALU.mult).then_inc(mdiag_ready, 1)

                    def total(h, par):
                        n = b * H + h
                        dve.wait_ge(probs_ready, 2 * n + 2)
                        if not first(h):
                            dve.wait_ge(den_psum, n)
                        nc.vector.tensor_reduce(den[:, :], sc[:, par, 0:KT, :].rearrange("p t q -> p q t"), AX.X, ALU.add).then_inc(sum_ready, 1)

                    def denominators(n):
                        dve.wait_ge(den_psum, n + 1)
                        chain.link(nc.vector.reciprocal(rden[:, :], pM[:, 0, 0:TB]))

                    def output(n):
                        dve.wait_ge(out_psum, n + 1)
                        for t in range(TB):
                            xt = k.x[:, b * TB + t, :]
                            last = nc.vector.scalar_tensor_tensor(xt, pO[:, t, :], rden[:, t:t + 1], xt, ALU.mult, ALU.add)
                            if t < TB - 1:
                                chain.link(last)
                        last.then_inc(out_added, 1)
                        dve.wait_ge(out_added, n + 1)

                    query(0, 0)
                    query(1, 1)
                    maximum_first(b * H, 0)
                    maximum(b * H, 0)

                    def step(h, par):
                        n = b * H + h
                        chain.restart()
                        shift(n)
                        if not first(h):
                            denominators(n - 1)
                        dve.wait_ge(shift_psum, n + 1)
                        for lo, hi in ((0, SPLIT), (SPLIT, KT)):
                            z = sc[:, par, lo:hi, :]
                            nc.vector.tensor_tensor(z, z, pM[:, 1, :].unsqueeze(1).to_broadcast([P, hi - lo, S]), ALU.subtract).then_inc(sub_ready, 1)
                        if not last_heads(h, 2):
                            dve.wait_ge(qT_psum, n + 1)
                            query(h + 2, par)
                        if not first(h):
                            output(n - 1)
                        if not last_heads(h, 1):
                            maximum_first(n + 1, 1 - par)
                        total(h, par)
                        if not last_heads(h, 1):
                            maximum(n + 1, 1 - par)

                    heads(dve, step)
                    chain.restart()
                    denominators(b * H + (H - 1))
                    output(b * H + (H - 1))

            @block.scalar
            def _(act):
                act.wait_ge(prepared, 3)
                with act.Fori(0, B) as b:
                    act.wait_ge(xnT_psum, b + 1)
                    nc.scalar.activation(xnT[:, :, :], pQ[:, :, :], ACT.Copy).then_inc(xnT_ready, 1)
                    for u in range(QU):
                        act.wait_ge(unit_psum, b * UN + u + 1)
                        if u >= NB:
                            act.wait_ge(unit_red, b * UN + u - NB + 1)
                        t, g = u // CG, u % CG
                        nc.scalar.activation(q[:, t, g * C:(g + 1) * C], pS[:, u % NB, :], ACT.Copy)
                        nc.scalar.activation(sq[:, u % NB, :], pS[:, u % NB, :], ACT.Square).then_inc(unit_sq, 1)
                    with act.Fori(0, KT) as t:
                        for g in range(CG):
                            act.wait_ge(unit_psum, b * UN + t * CG + (QU + g + 1))
                            act.wait_ge(unit_red, b * UN + t * CG + (QU + g - NB + 1))
                            nc.scalar.activation(sq[:, g, :], pS[:, g, :], ACT.Square).then_inc(unit_sq, 1)

                    def queries_T(n):
                        act.wait_ge(qT_psum, n + 1)
                        nc.scalar.activation(qT[:, :], pQ[:, 0, :], ACT.Copy, scale=gg[:, 0:1]).then_inc(qT_ready, 1)

                    def queries_e(n, par):
                        act.wait_ge(qe_psum, n + 1)
                        nc.scalar.activation(qe[:, par, :], pQ[:, 1, :], ACT.Copy).then_inc(qe_ready, 1)

                    def copy_scores(n, h, par, lo, hi):
                        for kt in range(lo, hi):
                            if kt % 2 == 0:
                                act.wait_ge(s_psum, n * SU + (kt // 2 + 1))
                            src = pS[:, kt // 2 % NB, (kt % 2) * S:(kt % 2) * S + S]
                            dst, r = sc[:, par, kt, :], rk[:, kt, ds(h, 1)]
                            if kt < KT - 1:
                                ins = nc.scalar.activation(dst, src, ACT.Copy, scale=r)
                            else:
                                ins = nc.scalar.activation(dst, src, ACT.Identity, scale=r, bias=dead[:, 0:1])
                            ins.then_inc(s_copied, 1)

                    def exponentials(n, par, part_):
                        lo, hi = ((0, SPLIT), (SPLIT, KT))[part_]
                        act.wait_ge(sub_ready, 2 * n + 1 + part_)
                        z = sc[:, par, lo:hi, :]
                        nc.scalar.activation(z, z, ACT.Exp).then_inc(probs_ready, 1)

                    n0 = b * H
                    queries_T(n0)
                    queries_e(n0, 0)
                    queries_T(n0 + 1)
                    queries_e(n0 + 1, 1)
                    act.wait_ge(rk_ready, b + 1)
                    copy_scores(n0, 0, 0, 0, KT)

                    def weighted(h):
                        n = b * H + h
                        act.wait_ge(pv_done, n + 1)
                        if not first(h):
                            act.wait_ge(out_psum, n)
                        nc.scalar.activation(pe_n[:, :], pV[:, :], ACT.Copy).then_inc(pe_ready, 1)

                    def step(h, par):
                        n = b * H + h
                        if not first(h):
                            weighted(h - 1)
                        if not last_heads(h, 1):
                            if not first(h):
                                act.wait_ge(sum_ready, n)
                            copy_scores(n + 1, h + 1, 1 - par, 0, 6)
                        exponentials(n, par, 0)
                        if not last_heads(h, 1):
                            copy_scores(n + 1, h + 1, 1 - par, 6, 8)
                        exponentials(n, par, 1)
                        if not last_heads(h, 1):
                            copy_scores(n + 1, h + 1, 1 - par, 8, KT)
                        if not last_heads(h, 2):
                            queries_T(n + 2)
                            queries_e(n + 2, par)

                    heads(act, step)
                    weighted(H - 1)

            @block.tensor
            def _(pe):
                pe.wait_ge(weights, 16 * 7)
                pe.wait_ge(prepared, 3)
                for h in range(H):
                    if h % 2 == 0 and h // 2 >= NB:
                        pe.wait_ge(vo_ready, h // 2 - NB + 1)
                    last = pe.matmul(pS[:, h // 2 % NB, (h % 2) * D:(h % 2 + 1) * D], wvT[:, h, :], wo[:, h, :], start=True, stop=True)
                    if h % 2:
                        last.then_inc(vo_psum, 1)
                with pe.Fori(0, B) as b:
                    for t in range(TB):
                        pe.wait_ge(xn_ready, b * TB + t + 1)
                        for c in range(DC):
                            last = pe.transpose(pQ[:, c, t * P:t * P + P], xn[:, t, c * P:c * P + P], k.ident[:, :])
                    last.then_inc(xnT_psum, 1)
                    pe.wait_ge(vo_ready, H // 2)
                    pe.wait_ge(xnT_ready, b + 1)
                    for u in range(QU):
                        if u >= NB:
                            pe.wait_ge(unit_sq, b * UN + u - NB + 1)
                        t, g = u // CG, u % CG
                        for c in range(DC):
                            last = pe.matmul(pS[:, u % NB, :], xnT[:, c, t * P:t * P + P], wq[:, c, g * C:(g + 1) * C], start=c == 0, stop=c == DC - 1)
                        last.then_inc(unit_psum, 1)
                    pe.wait_ge(eT_landed, b * 16 + 16)
                    for u in range(QU, UN):
                        pe.wait_ge(unit_sq, b * UN + u - NB + 1)
                        t, g = (u - QU) // CG, (u - QU) % CG
                        pe.matmul(pS[:, u % NB, :], eT[:, t * P:t * P + P], wk[:, g * C:(g + 1) * C], start=True, stop=True).then_inc(unit_psum, 1)

                    def queries_T(n, par):
                        pe.wait_ge(qn_ready, n + 1)
                        for t in range(TB):
                            last = pe.transpose(pQ[:, 0, t * P:t * P + P], qn[:, par, t, :], k.ident[:, :])
                        last.then_inc(qT_psum, 1)

                    def queries_e(n, par):
                        pe.wait_ge(qT_ready, n + 1)
                        pe.wait_ge(wk_ready, n + 1)
                        pe.matmul(pQ[:, 1, :], wk_h[:, par, :], qT[:, :], start=True, stop=True).then_inc(qe_psum, 1)

                    def scores(n, par, lo, hi, fresh=False):
                        for kt in range(lo, hi):
                            u = kt // 2
                            if kt % 2 == 0 and not (fresh and u < NB):
                                if u >= NB:
                                    pe.wait_ge(s_copied, n * KT + 2 * (u - NB) + 2)
                                else:
                                    pe.wait_ge(s_copied, n * KT)
                            last = pe.matmul(pS[:, u % NB, (kt % 2) * S:(kt % 2) * S + S], eT[:, kt * P:kt * P + P], qe[:, par, :],
                                             start=True, stop=True)
                            if kt % 2 or kt == KT - 1:
                                last.then_inc(s_psum, 1)

                    def max_T(n):
                        pe.wait_ge(max_ready, n + 1)
                        for t in range(TB):
                            last = pe.transpose(pM[:, 0, t * P:t * P + P], mx[:, t * P:t * P + P], k.ident[:, :])
                        last.then_inc(maxT_psum, 1)

                    def shift(n):
                        pe.wait_ge(mdiag_ready, n + 1)
                        pe.matmul(pM[:, 1, :], k.ones[:, :], mdiag[:, :, :], start=True, stop=True).then_inc(shift_psum, 1)

                    def weighted(n, par, lo, hi):
                        for kt in range(lo, hi):
                            if kt == 0 or kt == SPLIT:
                                pe.wait_ge(probs_ready, 2 * n + (1 if kt == 0 else 2))
                            last = pe.matmul(pV[:, :], eK[:, kt, :], sc[:, par, kt, :], start=kt == 0, stop=kt == KT - 1)
                        if hi == KT:
                            last.then_inc(pv_done, 1)

                    def output(h):
                        n = b * H + h
                        pe.wait_ge(pe_ready, n + 1)
                        if not first(h):
                            pe.wait_ge(out_added, n)
                        for t in range(TB):
                            last = pe.matmul(pO[:, t, :], pe_n[:, t * P:t * P + P], vo[:, h, :], start=True, stop=True)
                        last.then_inc(out_psum, 1)

                    n0 = b * H
                    pe.wait_ge(unit_sq, b * UN + UN)
                    for h in range(2):
                        queries_T(n0 + h, h)
                        queries_e(n0 + h, h)
                        pe.wait_ge(qe_ready, n0 + h + 1)
                    scores(n0, 0, 0, KT, fresh=True)
                    pe.wait_ge(eK_landed, b * 32 + 32)

                    def denominator(n):
                        pe.wait_ge(sum_ready, n + 1)
                        for t in range(TB):
                            last = pe.matmul(pM[:, 0, t:t + 1], den[:, t * P:t * P + P], k.ones[:, 0:1], start=True, stop=True)
                        last.then_inc(den_psum, 1)

                    def step(h, par):
                        n = b * H + h
                        if not last_heads(h, 1):
                            pe.wait_ge(qe_ready, n + 2)
                            scores(n + 1, 1 - par, 0, 2)
                        max_T(n)
                        if not last_heads(h, 1):
                            scores(n + 1, 1 - par, 2, 4)
                        shift(n)
                        if not first(h):
                            denominator(n - 1)
                        if not last_heads(h, 1):
                            scores(n + 1, 1 - par, 4, 10)
                        if not first(h):
                            output(h - 1)
                        if not last_heads(h, 1):
                            scores(n + 1, 1 - par, 10, KT)
                        weighted(n, par, 0, 4)
                        if not last_heads(h, 2):
                            queries_T(n + 2, par)
                        weighted(n, par, 4, KT)
                        if not last_heads(h, 2):
                            queries_e(n + 2, par)

                    heads(pe, step)
                    denominator(b * H + (H - 1))
                    output(H - 1)


def sparse_experts(nc, k, gateT, wT, atoms, eawd, impd, idxd):
    E, A = eawd.shape
    NS = atoms.shape[1]
    ST = NS // P
    CLIP = 50.0
    EG = 512 // D
    UNITS = E // EG + 1
    G = UNITS - 1

    with Scope(nc, "sp") as s:
        gate, at, eaw = s.sb("gate", [P, DC, E]), s.sb("at", [A, NS]), s.sb("eaw", [E, A])
        w9 = s.sb("w9", [P, DC, E + 1, D])
        idx, row_i, col_i, row, col = (s.sb("idx", [P, ST], I32), s.sb("row_i", [P, ST], I32), s.sb("col_i", [P, ST], I32),
                                       s.sb("row", [P, ST]), s.sb("col", [P, ST]))
        count_i, count, ecount = s.sb("count_i", [P, D], I32), s.sb("count", [P, D]), s.sb("ecount", [P, E])
        imp, wt = s.sb("imp", [P, ST, E]), s.sb("wt", [P, ST, E])
        emax, esum, erec, aw, awT = s.sb("emax", [E, 1]), s.sb("esum", [E, 1]), s.sb("erec", [E, 1]), s.sb("aw", [E, A]), s.sb("awT", [A, E])
        stats, mv = s.sb("stats", [P, NT, 6]), s.sb("mv", [P, NT, 2])
        ve, rstd, room = s.sb("ve", [P, NT]), s.sb("rstd", [P, NT]), s.sb("room", [P, NT])
        xn, xT2, xT = s.sb("xn", [P, 2, D]), s.sb("xT2", [P, 2, DC, P]), s.sb("xT", [P, NT, DC, P])
        lg, top, topi, topf = s.sb("lg", [P, NT, E]), s.sb("top", [P, NT, 8]), s.sb("topi", [P, NT, 8], U32), s.sb("topf", [P, NT, 8])
        ex, r0, r1 = s.sb("ex", [P, NT]), s.sb("r0", [P, NT]), s.sb("r1", [P, NT])
        rw, hot = s.sb("rw", [P, NT, E]), s.sb("hot", [P, NT, E])
        c1, rr = s.sb("c1", [P, 2, P]), s.sb("rr", [P, 2, E, D])
        pY = s.ps("pY", [P, UNITS, 512])
        pT, pL, pW = s.ps("pT", [P, DC, P]), s.ps("pL", [P, NT, E]), s.ps("pW", [P, ST, E])
        (weights, iotas, stats_ready, xn_ready, xT_psum, xT_ready, xT_kept, l_psum, ex_in, ex_ready, atom_in, atom_ready,
         imp_ready, aw_ready, awT_psum, awT_ready, wt_psum, rr_ready, d_used, d_psum, d_ready, x2_ready, tile_done,
         y_psum, y_used, dve_chain) = s.sem(
            "weights", "iotas", "stats_ready", "xn_ready", "xT_psum", "xT_ready", "xT_kept", "l_psum", "ex_in", "ex_ready",
            "atom_in", "atom_ready", "imp_ready", "aw_ready", "awT_psum", "awT_ready", "wt_psum", "rr_ready", "d_used",
            "d_psum", "d_ready", "x2_ready", "tile_done", "y_psum", "y_used", "dve_chain")
        LOADS = 6
        with nc.Block() as block:

            @block.sync
            def _(sp):
                for dst, src in ((gate[:, :, :], gateT.rearrange("(c p) n -> p c n", p=P)), (at[:, :], atoms), (eaw[:, :], eawd),
                                 (imp[:, :, :].rearrange("p t e -> p (t e)"), impd), (idx[:, :], idxd)):
                    sp.dma_start(dst, src).then_inc(weights, 16)
                sp.dma_start(w9[:, :, E, :], wT.rearrange("(c p) n -> p c n", p=P)).then_inc(weights, 16)

            @block.gpsimd
            def _(pool):
                nc.gpsimd.iota(count_i[:, :], pattern=[[1, D]], base=0, channel_multiplier=0).then_inc(iotas, 1)

            @block.vector
            def _(dve):
                chain = Chain(dve, dve_chain)
                for i in range(NT):
                    nc.vector.bn_stats(stats[:, i, :], k.x[:, i, :]).then_inc(stats_ready, 1)
                for i in range(NT):
                    dve.wait_ge(stats_ready, i + 1)
                    nc.vector.bn_aggr(mv[:, i, :], stats[:, i, :]).then_inc(stats_ready, 1)
                dve.wait_ge(stats_ready, 2 * NT)
                chain.link(nc.vector.tensor_scalar(ve[:, :], mv[:, :, 1], LN_EPS, None, ALU.add))
                rsqrt(nc, chain, rstd[:, :], ve[:, :], room[:, :])
                with dve.Fori(0, NT // 2) as j:
                    for a in range(2):
                        dve.wait_ge(xT_psum, j * 2 + (a + 1))
                        nc.vector.tensor_scalar(xn[:, a, :], k.x[:, j * 2 + a, :], mv[:, j * 2 + a, 0:1], rstd[:, ds(j * 2 + a, 1)],
                                                ALU.subtract, ALU.mult).then_inc(xn_ready, 1)
                dve.wait_ge(weights, 16 * LOADS)
                dve.wait_ge(iotas, 1)
                chain.link(nc.vector.tensor_copy(count[:, :], count_i[:, :]))
                chain.link(nc.vector.tensor_scalar(row_i[:, :], idx[:, :], 8, None, ALU.arith_shift_right))
                chain.link(nc.vector.tensor_scalar(col_i[:, :], idx[:, :], D - 1, None, ALU.bitwise_and))
                chain.link(nc.vector.tensor_copy(row[:, :], row_i[:, :]))
                chain.link(nc.vector.tensor_copy(col[:, :], col_i[:, :]))
                chain.link(nc.vector.tensor_reduce(emax[:, :], eaw[:, :], AX.X, ALU.max))
                nc.vector.tensor_scalar(aw[:, :], eaw[:, :], emax[:, 0:1], None, ALU.subtract).then_inc(atom_in, 1)
                dve.wait_ge(atom_ready, 1)
                chain.link(nc.vector.tensor_reduce(esum[:, :], aw[:, :], AX.X, ALU.add))
                chain.link(nc.vector.reciprocal(erec[:, :], esum[:, :]))
                nc.vector.tensor_scalar(aw[:, :], aw[:, :], erec[:, 0:1], None, ALU.mult).then_inc(aw_ready, 1)
                dve.wait_ge(imp_ready, 1)
                chain.link(nc.vector.tensor_scalar(imp[:, :, :], imp[:, :, :], 1.0, None, ALU.add))
                chain.link(nc.vector.reciprocal(imp[:, :, :], imp[:, :, :]))
                dve.wait_ge(wt_psum, 1)
                chain.link(nc.vector.tensor_tensor(wt[:, :, :], pW[:, :, :], imp[:, :, :], ALU.mult))

                for dc in range(DC):
                    with dve.Fori(0, ST // 2) as j:
                        for a in range(2):
                            dve.wait_ge(d_used, j * 2 + (dc * ST + a + 1))
                            st = j * 2 + a
                            nc.vector.tensor_scalar(c1[:, a, :], count[:, dc * P:(dc + 1) * P], col[:, ds(st, 1)], None, ALU.is_equal)
                            for e in range(E):
                                last = nc.vector.tensor_scalar(rr[:, a, e, :], count[:, :], row[:, ds(st, 1)], wt[:, st, e:e + 1],
                                                               ALU.is_equal, ALU.mult)
                            last.then_inc(rr_ready, 1)

                dve.wait_ge(l_psum, NT)
                chain.link(nc.vector.tensor_scalar(lg[:, :, :], pL[:, :, :], CLIP, -CLIP, ALU.min, ALU.max))
                for i in range(NT):
                    chain.link(nc.vector.max(top[:, i, :], lg[:, i, :]))
                    chain.link(nc.vector.max_index(topi[:, i, :], top[:, i, :], lg[:, i, :]))
                chain.link(nc.vector.tensor_copy(topf[:, :, :], topi[:, :, :]))
                nc.vector.tensor_tensor(ex[:, :], top[:, :, 1], top[:, :, 0], ALU.subtract).then_inc(ex_in, 1)
                dve.wait_ge(ex_ready, 1)
                chain.link(nc.vector.tensor_scalar(r1[:, :], ex[:, :], 1.0, None, ALU.add))
                chain.link(nc.vector.reciprocal(r0[:, :], r1[:, :]))
                chain.link(nc.vector.tensor_tensor(r1[:, :], r0[:, :], ex[:, :], ALU.mult))
                for m, r in ((0, r0), (1, r1)):
                    dst = (rw, hot)[m]
                    cb = count[:, 0:E].unsqueeze(1).to_broadcast([P, NT, E])
                    chain.link(nc.vector.tensor_tensor(dst[:, :, :], cb, bcast(topf[:, :, m], E), ALU.is_equal))
                    chain.link(nc.vector.tensor_tensor(dst[:, :, :], dst[:, :, :], bcast(r[:, :], E), ALU.mult))
                chain.link(nc.vector.tensor_tensor(rw[:, :, :], rw[:, :, :], hot[:, :, :], ALU.add))

                with dve.Fori(0, NT) as i:
                    chain.restart()
                    xt = k.x[:, i, :]
                    for u in range(UNITS):
                        dve.wait_ge(y_psum, i * UNITS + (u + 1))
                        if u < G:
                            for a in range(EG):
                                e = u * EG + a
                                last = nc.vector.scalar_tensor_tensor(xt, pY[:, u, a * D:(a + 1) * D], rw[:, i, e:e + 1], xt, ALU.mult, ALU.add)
                                if a < EG - 1:
                                    chain.link(last)
                        else:
                            last = nc.vector.tensor_tensor(xt, xt, pY[:, u, 0:D], ALU.add)
                        last.then_inc(y_used, 1)
                        dve.wait_ge(y_used, i * UNITS + (u + 1 + UNITS))

            @block.scalar
            def _(act):
                act.sem_inc(xT_psum, 2)
                act.sem_inc(xT_kept, 1)
                act.sem_inc(d_used, 2)
                act.sem_inc(tile_done, 2)
                act.sem_inc(y_used, UNITS)
                with act.Fori(0, NT // 2) as j:
                    for a in range(2):
                        act.wait_ge(xT_psum, j * 2 + (a + 3))
                        nc.scalar.activation(xT[:, j * 2 + a, :, :], pT[:, :, :], ACT.Copy)
                        nc.scalar.activation(xT2[:, a, :, :], pT[:, :, :], ACT.Copy).then_inc(xT_ready, 1)
                act.wait_ge(atom_in, 1)
                nc.scalar.activation(aw[:, :], aw[:, :], ACT.Exp).then_inc(atom_ready, 1)
                act.wait_ge(weights, 16 * LOADS)
                nc.scalar.activation(imp[:, :, :], imp[:, :, :], ACT.Exp, scale=-1.0).then_inc(imp_ready, 1)
                act.wait_ge(awT_psum, 1)
                nc.scalar.activation(awT[:, :], pW[0:A, 0, :], ACT.Copy).then_inc(awT_ready, 1)
                for dc in range(DC):
                    act.wait_ge(d_psum, dc + 1)
                    for u in range(G):
                        last = nc.scalar.activation(w9[:, dc, u * EG:(u + 1) * EG, :], pY[:, u, :].rearrange("p (a n) -> p a n", a=EG), ACT.Copy)
                    last.then_inc(d_ready, 1)
                act.wait_ge(ex_in, 1)
                nc.scalar.activation(ex[:, :], ex[:, :], ACT.Exp).then_inc(ex_ready, 1)
                with act.Fori(0, NT // 2) as j:
                    for a in range(2):
                        act.wait_ge(tile_done, j * 2 + (a + 1))
                        nc.scalar.activation(xT2[:, a, :, :], xT[:, j * 2 + a, :, :], ACT.Copy).then_inc(x2_ready, 1)

            @block.tensor
            def _(pe):
                pe.wait_ge(weights, 16 * LOADS)
                with pe.Fori(0, NT // 2) as j:
                    for a in range(2):
                        pe.wait_ge(xn_ready, j * 2 + (a + 1))
                        pe.wait_ge(xT_kept, j * 2 + (a + 1))
                        for c in range(DC):
                            last = pe.transpose(pT[:, c, :], xn[:, a, c * P:c * P + P], k.ident[:, :])
                        last.then_inc(xT_psum, 1)
                        pe.wait_ge(xT_ready, j * 2 + (a + 1))
                        pe.sem_inc(xT_kept, 1)
                        for c in range(DC):
                            last = pe.matmul(pL[:, j * 2 + a, :], xT2[:, a, c, :], gate[:, c, :], start=c == 0, stop=c == DC - 1)
                        last.then_inc(l_psum, 1)
                pe.wait_ge(aw_ready, 1)
                pe.transpose(pW[0:A, 0, :], aw[:, :], k.ident[0:E, 0:E]).then_inc(awT_psum, 1)
                pe.wait_ge(awT_ready, 1)
                for st in range(ST):
                    last = pe.matmul(pW[:, st, :], at[:, st * P:(st + 1) * P], awT[:, :], start=True, stop=True)
                last.then_inc(wt_psum, 1)
                for dc in range(DC):
                    if dc:
                        pe.wait_ge(d_ready, dc)
                    pe.wait_ge(rr_ready, dc * ST + 1)

                    def entries(a, start, stop):
                        for u in range(G):
                            last = pe.matmul(pY[:, u, :], c1[:, a, :], rr[:, a, u * EG:(u + 1) * EG, :].rearrange("p e n -> p (e n)"),
                                             start=start, stop=stop, skip_group_check=True)
                        last.then_inc(d_used, 1)
                        return last

                    entries(0, True, False)
                    pe.wait_ge(rr_ready, dc * ST + 2)
                    entries(1, False, False)
                    with pe.Fori(1, ST // 2) as j:
                        for a in range(2):
                            pe.wait_ge(rr_ready, j * 2 + (dc * ST + a + 1))
                            entries(a, False, False)
                    pe.wait_ge(d_used, (dc + 1) * ST + 2)
                    pe.sem_inc(d_psum, 1)
                pe.wait_ge(d_ready, DC)
                with pe.Fori(0, NT // 2) as j:
                    for a in range(2):
                        pe.wait_ge(x2_ready, j * 2 + (a + 1))
                        for u in range(UNITS):
                            pe.wait_ge(y_used, j * (2 * UNITS) + (a * UNITS + u + 1))
                            w = EG if u < G else 1
                            for c in range(DC):
                                last = pe.matmul(pY[:, u, 0:w * D], xT2[:, a, c, :], w9[:, c, u * EG:u * EG + w, :].rearrange("p e n -> p (e n)"),
                                                 start=c == 0, stop=c == DC - 1)
                            last.then_inc(y_psum, 1)
                        pe.wait_ge(y_psum, j * (2 * UNITS) + (a + 1) * UNITS)
                        pe.sem_inc(tile_done, 1)


class Shared:

    def __init__(self, s):
        self.x = s.sb("x", [P, NT + TB, D])
        self.ident, self.ident_bf = s.sb("ident", [P, P]), s.sb("ident_bf", [P, P], BF16)
        self.ones, self.minus_half = s.sb("ones", [P, P]), s.sb("minus_half", [P, D])


def decoder(nc, t, out):
    with Scope(nc, "keep") as s:
        k = Shared(s)
        constants(nc, k)
        load_x(nc, k, t["x"])
        self_attention(nc, k, t["sa_wqkvT"], t["sa_woT"])
        cross_attention_0(nc, k, t["ctxT"], t["xa_wq"], t["xa_bq"], t["xa_wkv"], t["xa_bkv"], t["xa_wdca"], t["xa_bdca"],
                          t["xa_qn_w"], t["xa_qn_b"], t["xa_kn_w"], t["xa_kn_b"], t["xa_kn_dca_w"], t["xa_kn_dca_b"],
                          t["xa_wo"], t["xa_bo"])
        experts(nc, k, t["moe_gateT"], t["moe_w13T"], t["moe_w2T"], t["moe_s13T"], t["moe_s2T"])
        bit_mlp(nc, k, t["bit_wgT"], t["bit_gg"], t["bit_wdT"], t["bit_gd"])
        cross_attention_1(nc, k, t["ctx_rows"], t["ctx_tail"], t["ctxT"], t["xb_wq"], t["xb_wk"], t["xb_wkT"], t["xb_wvT"],
                          t["xb_wo"], t["xb_gq"], t["xb_gk"])
        sparse_experts(nc, k, t["sp_gateT"], t["sp_wT"], t["sp_atoms"], t["sp_eaw"], t["sp_imp"], t["sp_idx"])
        store_x(nc, k, out)


def laid_out(i):
    T = lambda a: a.swapaxes(-1, -2)
    cat = np.concatenate
    i = {name: np.asarray(a) for name, a in i.items()}
    a, c, m, b, e, f = ({name[len(pre):]: v for name, v in i.items() if name.startswith(pre)} for pre in
                        ("L0_attn_", "L0_xattn_", "L0_ffn_", "L1_attn_", "L1_xattn_", "L1_ffn_"))
    ctx = i["ctx_1024"]
    whole = ctx.shape[1] // P

    def by_head(w):
        z = w.reshape(w.shape[:-1] + (2, 16, 16))
        return z.swapaxes(-3, -2).reshape(w.shape)

    def by_partition(w):
        return w.reshape(-1, P, w.shape[-1]).transpose(1, 0, 2).reshape(P, -1)

    return {
        "x": i["x"],
        "sa_wqkvT": T(cat([a["Wq"], a["Wk"], a["Wv"]], 0)), "sa_woT": T(a["Wo"]),
        "ctxT": T(ctx),
        "ctx_rows": ctx[:, :whole * P].reshape(B, whole, P, -1).transpose(0, 2, 1, 3).reshape(B, P, -1),
        "ctx_tail": ctx[:, whole * P:],
        "xa_wq": c["Wq"], "xa_bq": c["bq"], "xa_wkv": cat([c["Wk"], c["Wv"]], 1), "xa_bkv": cat([c["bk"], c["bv"]], 0),
        "xa_wdca": by_head(c["Wkv_dca"]), "xa_bdca": by_head(c["bkv_dca"]),
        "xa_qn_w": c["qn_w"], "xa_qn_b": c["qn_b"], "xa_kn_w": c["kn_w"], "xa_kn_b": c["kn_b"],
        "xa_kn_dca_w": c["kn_dca_w"], "xa_kn_dca_b": c["kn_dca_b"], "xa_wo": c["Wo"], "xa_bo": c["bo"],
        "moe_gateT": T(m["gate_w"]), "moe_w13T": cat([T(m["w1"]), T(m["w3"])], 2), "moe_w2T": T(m["w2"]),
        "moe_s13T": cat([T(m["sw1"]), T(m["sw3"])], 1), "moe_s2T": T(m["sw2"]),
        "bit_wgT": T(b["w_gate"]), "bit_gg": b["g_gate"], "bit_wdT": T(b["w_down"]), "bit_gd": b["g_down"],
        "xb_wq": e["Wq"], "xb_wk": e["Wk"], "xb_wkT": by_partition(T(e["Wk"])), "xb_wvT": by_partition(T(e["Wv"])),
        "xb_wo": e["Wo"], "xb_gq": e["gq"], "xb_gk": e["gk"],
        "sp_gateT": T(f["gate_w"]), "sp_wT": T(f["W"]), "sp_atoms": f["atoms"], "sp_eaw": f["expert_atom_weights"],
        "sp_imp": by_partition(T(f["importance"])), "sp_idx": T(f["mask_idx"].reshape(-1, P)),
    }


def kernel(**inputs):
    import concourse.bacc as bacc
    from concourse.bass_utils import run_bass_kernel_spmd

    nc = bacc.Bacc("TRN2", target_bir_lowering=False, num_devices=1)
    arrays, args = {}, {}
    for name, a in laid_out(inputs).items():
        a = np.ascontiguousarray(a)
        arrays[f"in_{name}"] = a
        args[name] = nc.dram_tensor(f"in_{name}", a.shape, mybir.dt.from_np(a.dtype), kind="ExternalInput").ap()
    out = nc.dram_tensor("out_x", (B, S, D), F32, kind="ExternalOutput").ap()
    decoder(nc, args, out)
    r = run_bass_kernel_spmd(nc, [arrays], core_ids=[0])
    return r.results[0]["out_x"]
```
